# Optimizing a Trainium2 kernel written in Bass

```python
import numpy as np
import jax
import jax.numpy as jnp

def _softmax(x, axis=-1):
    return jax.nn.softmax(x, axis=axis)

def _gelu(x):
    return jax.nn.gelu(x, approximate=True)

def _silu(x):
    return jax.nn.silu(x)

def _sigmoid(x):
    return jax.nn.sigmoid(x)

def _layernorm(x, axis=-1, eps=1e-05):
    m = jnp.mean(x, axis=axis, keepdims=True)
    v = jnp.var(x, axis=axis, keepdims=True)
    return (x - m) / jnp.sqrt(v + eps)

def _scatter_add(tgt, idx, src, axis=0):
    return tgt.at[idx].add(src)

def _segment_sum(src, seg, n):
    return jax.ops.segment_sum(src, seg, n)
kernel_name = 'mk_decoder_postln_d1_seqx_r8_873c4c'

def setup_inputs(seed: int=0):
    np.random.seed(seed)
    _w = jnp.asarray

    def _rec_inputs():
        import jax
        import jax.numpy as jnp
        _rk = jax.random.key(seed)
        x = -0.000125 + 0.9999 * jax.random.normal(jax.random.fold_in(_rk, 1), (16, 64, 256), jnp.float32)
        _lenS = 64 - jax.random.randint(jax.random.fold_in(_rk, 7), (16,), 0, max(1, 64 // 4) + 1, jnp.int32)
        _lenS2 = 64 - jax.random.randint(jax.random.fold_in(_rk, 8), (16,), 0, max(1, 64 // 4) + 1, jnp.int32)
        _ctx_2048P = jax.random.normal(jax.random.fold_in(_rk, 11), (16, 16, 256), jnp.float32)
        _ctx_2048c = jax.random.dirichlet(jax.random.fold_in(_rk, 511), 0.3 * jnp.ones((16,), jnp.float32), (16, 64))
        _ctx_2048t = jnp.einsum('bsk,bkd->bsd', _ctx_2048c, _ctx_2048P)
        _ctx_2048t = _ctx_2048t * jax.lax.rsqrt(jnp.mean(jnp.square(_ctx_2048t)) + 1e-12) * 0.953939
        ctx_2048 = -1.52775e-05 + 0.999936 * (_ctx_2048t + 0.3 * jax.random.normal(jax.random.fold_in(_rk, 611), (16, 64, 256), jnp.float32))
        return (x, ctx_2048)
    x, ctx_2048 = _rec_inputs()

    def _L0_attn_setup():
        import jax, jax.numpy as jnp
        import numpy as np
        HID = 256
        QCD = 128
        H = 16
        D = 128
        RD = 64
        THETA = 10000.0
        SW = 64
        M = 32
        TOPK = 32
        G = 4
        DG = 64
        NIH = 4
        CI = 64
        EPS = 1e-06

        def _rms(x, w):
            return x * jax.lax.rsqrt(jnp.mean(x * x, axis=-1, keepdims=True) + EPS) * w

        def _rope_cache(t):
            inv = 1.0 / THETA ** (jnp.arange(0, RD, 2, dtype=jnp.float32) / RD)
            ang = jnp.arange(t, dtype=jnp.float32)[:, None] * inv
            return (jnp.cos(ang), jnp.sin(ang))

        def _rope(x, cos, sin):
            xr, xp = (x[..., :RD], x[..., RD:])
            x1, x2 = (xr[..., :RD // 2], xr[..., RD // 2:])
            return jnp.concatenate([x1 * cos - x2 * sin, x2 * cos + x1 * sin, xp], axis=-1)

        def _compress(h, w_kv, w_z, bias):
            b, t, _ = h.shape
            ut = t // M * M
            nb = ut // M
            hu = h[:, :ut]
            c_b = (hu @ w_kv).reshape(b, nb, M, -1)
            z_b = (hu @ w_z).reshape(b, nb, M, -1) + bias
            w = jax.nn.softmax(z_b, axis=-2)
            return (w * c_b).sum(axis=-2)
        key = jax.random.key(seed)
        ks = jax.random.split(key, 16)

        def p(k, shape, scale=0.02):
            return jax.random.normal(k, shape, jnp.float32) * scale
        B, T = (1, 256)
        return {'h': jax.random.normal(ks[0], (B, T, HID), jnp.float32), 'w_qc': p(ks[1], (HID, QCD)), 'w_qup': p(ks[2], (QCD, H * D)), 'w_kv_b': p(ks[3], (HID, D)), 'w_z_b': p(ks[4], (HID, D)), 'bias_b': jnp.zeros((M, D), jnp.float32), 'w_k': p(ks[5], (HID, D)), 'w_v': p(ks[6], (HID, D)), 'wi_kv': p(ks[7], (HID, CI)), 'wi_z': p(ks[8], (HID, CI)), 'bias_i': jnp.zeros((M, CI), jnp.float32), 'w_dq': p(ks[9], (HID, CI)), 'w_iuq': p(ks[10], (CI, NIH * CI)), 'w_w': p(ks[11], (HID, NIH)), 'q_norm_w': jnp.ones((D,), jnp.float32), 'k_norm_w': jnp.ones((D,), jnp.float32), 'sink_logit': jnp.zeros((H,), jnp.float32), 'group_w': p(ks[12], (G, H // G * D, DG)), 'final_w': p(ks[13], (G * DG, HID))}
    _L0_attn_all = _L0_attn_setup()
    _L0_attn_in = {k: v for k, v in _L0_attn_all.items() if k in ('w_qc', 'w_qup', 'w_kv_b', 'w_z_b', 'bias_b', 'w_k', 'w_v', 'wi_kv', 'wi_z', 'bias_i', 'w_dq', 'w_iuq', 'w_w', 'q_norm_w', 'k_norm_w', 'sink_logit', 'group_w', 'final_w')}
    del _L0_attn_all

    def _L0_xattn_setup():
        import jax, jax.numpy as jnp
        import numpy as np
        NUM_HEADS = 16
        key = jax.random.key(seed)
        k1, k2, k3 = jax.random.split(key, 3)
        B, S, D = (4, 512, 256)
        q = jax.random.normal(k1, (B, S, D), dtype=jnp.float32)
        k = jax.random.normal(k2, (B, S, D), dtype=jnp.float32)
        v = jax.random.normal(k3, (B, S, D), dtype=jnp.float32)
        decay = jnp.full((1, NUM_HEADS, 1), 0.9, dtype=jnp.float32)
        return {'q': q, 'k': k, 'v': v, 'decay': decay}
    _L0_xattn_all = _L0_xattn_setup()
    _L0_xattn_in = {k: v for k, v in _L0_xattn_all.items() if k in ('decay',)}
    del _L0_xattn_all

    def _L0_ffn_setup():
        import jax, jax.numpy as jnp
        import numpy as np
        H = 256
        E = 8
        TOP_K = 2
        I_MOE = 176
        I_SH = 704
        BS, NT = (2, 64)
        key = jax.random.key(seed)
        ks = jax.random.split(key, 7)
        s = lambda d: (1.0 / np.sqrt(d)).astype(np.float32)
        return {'hidden_states': jax.random.normal(ks[0], (BS, NT, H), jnp.float32), 'gate_w': jax.random.normal(ks[1], (E, H), jnp.float32) * s(H), 'w1': jax.random.normal(ks[2], (E, 2 * I_MOE, H), jnp.float32) * s(H), 'w2': jax.random.normal(ks[3], (E, H, I_MOE), jnp.float32) * s(I_MOE), 'shared_gate_up_w': jax.random.normal(ks[4], (2 * I_SH, H), jnp.float32) * s(H), 'shared_down_w': jax.random.normal(ks[5], (H, I_SH), jnp.float32) * s(I_SH), 'shared_gate_w': jax.random.normal(ks[6], (1, H), jnp.float32) * s(H)}
    _L0_ffn_all = _L0_ffn_setup()
    _L0_ffn_in = {k: v for k, v in _L0_ffn_all.items() if k in ('gate_w', 'w1', 'w2', 'shared_gate_up_w', 'shared_down_w', 'shared_gate_w')}
    del _L0_ffn_all
    return {'x': x, 'ctx_2048': ctx_2048, 'L0_attn_w_qc': _L0_attn_in['w_qc'], 'L0_attn_w_qup': _L0_attn_in['w_qup'], 'L0_attn_w_kv_b': _L0_attn_in['w_kv_b'], 'L0_attn_w_z_b': _L0_attn_in['w_z_b'], 'L0_attn_bias_b': _L0_attn_in['bias_b'], 'L0_attn_w_k': _L0_attn_in['w_k'], 'L0_attn_w_v': _L0_attn_in['w_v'], 'L0_attn_wi_kv': _L0_attn_in['wi_kv'], 'L0_attn_wi_z': _L0_attn_in['wi_z'], 'L0_attn_bias_i': _L0_attn_in['bias_i'], 'L0_attn_w_dq': _L0_attn_in['w_dq'], 'L0_attn_w_iuq': _L0_attn_in['w_iuq'], 'L0_attn_w_w': _L0_attn_in['w_w'], 'L0_attn_q_norm_w': _L0_attn_in['q_norm_w'], 'L0_attn_k_norm_w': _L0_attn_in['k_norm_w'], 'L0_attn_sink_logit': _L0_attn_in['sink_logit'], 'L0_attn_group_w': _L0_attn_in['group_w'], 'L0_attn_final_w': _L0_attn_in['final_w'], 'L0_xattn_decay': _L0_xattn_in['decay'], 'L0_ffn_gate_w': _L0_ffn_in['gate_w'], 'L0_ffn_w1': _L0_ffn_in['w1'], 'L0_ffn_w2': _L0_ffn_in['w2'], 'L0_ffn_shared_gate_up_w': _L0_ffn_in['shared_gate_up_w'], 'L0_ffn_shared_down_w': _L0_ffn_in['shared_down_w'], 'L0_ffn_shared_gate_w': _L0_ffn_in['shared_gate_w']}

def reference(x, ctx_2048, L0_attn_w_qc, L0_attn_w_qup, L0_attn_w_kv_b, L0_attn_w_z_b, L0_attn_bias_b, L0_attn_w_k, L0_attn_w_v, L0_attn_wi_kv, L0_attn_wi_z, L0_attn_bias_i, L0_attn_w_dq, L0_attn_w_iuq, L0_attn_w_w, L0_attn_q_norm_w, L0_attn_k_norm_w, L0_attn_sink_logit, L0_attn_group_w, L0_attn_final_w, L0_xattn_decay, L0_ffn_gate_w, L0_ffn_w1, L0_ffn_w2, L0_ffn_shared_gate_up_w, L0_ffn_shared_down_w, L0_ffn_shared_gate_w):
    import jax
    import jax.numpy as jnp

    def _L0_attn_ref(h, w_qc, w_qup, w_kv_b, w_z_b, bias_b, w_k, w_v, wi_kv, wi_z, bias_i, w_dq, w_iuq, w_w, q_norm_w, k_norm_w, sink_logit, group_w, final_w):
        import jax, jax.numpy as jnp
        import numpy as np
        HID = 256
        QCD = 128
        H = 16
        D = 128
        RD = 64
        THETA = 10000.0
        SW = 64
        M = 32
        TOPK = 32
        G = 4
        DG = 64
        NIH = 4
        CI = 64
        EPS = 1e-06

        def _rms(x, w):
            return x * jax.lax.rsqrt(jnp.mean(x * x, axis=-1, keepdims=True) + EPS) * w

        def _rope_cache(t):
            inv = 1.0 / THETA ** (jnp.arange(0, RD, 2, dtype=jnp.float32) / RD)
            ang = jnp.arange(t, dtype=jnp.float32)[:, None] * inv
            return (jnp.cos(ang), jnp.sin(ang))

        def _rope(x, cos, sin):
            xr, xp = (x[..., :RD], x[..., RD:])
            x1, x2 = (xr[..., :RD // 2], xr[..., RD // 2:])
            return jnp.concatenate([x1 * cos - x2 * sin, x2 * cos + x1 * sin, xp], axis=-1)

        def _compress(h, w_kv, w_z, bias):
            b, t, _ = h.shape
            ut = t // M * M
            nb = ut // M
            hu = h[:, :ut]
            c_b = (hu @ w_kv).reshape(b, nb, M, -1)
            z_b = (hu @ w_z).reshape(b, nb, M, -1) + bias
            w = jax.nn.softmax(z_b, axis=-2)
            return (w * c_b).sum(axis=-2)
        b, t, _ = h.shape
        cos, sin = _rope_cache(t)
        q = (h @ w_qc @ w_qup).reshape(b, t, H, D).transpose(0, 2, 1, 3)
        q = _rms(_rope(q, cos, sin), q_norm_w)
        k_comp_i = _compress(h, wi_kv, wi_z, bias_i)
        nb = k_comp_i.shape[1]
        qi = (h @ w_dq @ w_iuq).reshape(b, t, NIH, CI)
        wgt = h @ w_w
        head_scores = jnp.maximum(jnp.einsum('bthc,bnc->bthn', qi, k_comp_i), 0.0)
        isc = jnp.einsum('bth,bthn->btn', wgt, head_scores)
        block_end = jnp.arange(nb) * M + (M - 1)
        valid = block_end[None, :] < jnp.arange(t)[:, None]
        isc = jnp.where(valid[None], isc, -jnp.inf)
        k = min(TOPK, nb)
        top_s, top_idx = jax.lax.top_k(isc, k)
        top_idx = jnp.where(jnp.isfinite(top_s), top_idx, -1)
        comp_kv = _compress(h, w_kv_b, w_z_b, bias_b)
        valid_pick = top_idx >= 0
        idx = jnp.maximum(top_idx, 0)
        sparse_kv = comp_kv[jnp.arange(b)[:, None, None], idx]
        sparse_kv = _rms(sparse_kv, k_norm_w)
        sc = jnp.einsum('bhtd,btkd->bthk', q, sparse_kv) / np.sqrt(D).astype(np.float32)
        sc = jnp.where(valid_pick[:, :, None, :], sc, -jnp.inf)
        has_pick = valid_pick.any(axis=-1)[:, :, None, None]
        sc = jnp.where(has_pick, sc, 0.0)
        probs = jax.nn.softmax(sc, axis=-1)
        mixed = jnp.einsum('bthk,btkd->bthd', probs, sparse_kv)
        mixed = jnp.where(has_pick, mixed, 0.0)
        sparse_out = mixed.transpose(0, 2, 1, 3)
        sw_k = _rope(_rms(h @ w_k, k_norm_w), cos, sin)
        sw_v = h @ w_v
        i = jnp.arange(t)
        mask = (i[None, :] <= i[:, None]) & (i[:, None] - i[None, :] < SW)
        sws = jnp.einsum('bhtd,bsd->bhts', q, sw_k) / np.sqrt(D).astype(np.float32)
        sws = jnp.where(mask, sws, -jnp.inf)
        sink = jnp.broadcast_to(sink_logit[None, :, None, None], (b, H, t, 1))
        p_full = jax.nn.softmax(jnp.concatenate([sws, sink], axis=-1), axis=-1)
        sw_out = jnp.einsum('bhts,bsd->bhtd', p_full[..., :t], sw_v)
        attn = sparse_out + sw_out
        o = attn.transpose(0, 2, 1, 3).reshape(b, t, G, H // G * D)
        o = jnp.einsum('btgi,gio->btgo', o, group_w).reshape(b, t, G * DG)
        return o @ final_w

    def _L0_xattn_ref(q, k, v, decay):
        import jax, jax.numpy as jnp
        import numpy as np
        NUM_HEADS = 16
        B, S, D = q.shape
        H = NUM_HEADS
        hd = D // H
        qh = q.reshape(B, S, H, hd)
        kh = k.reshape(B, S, H, hd)
        vh = v.reshape(B, S, H, hd)
        kv = kh * vh
        kv_t = jnp.moveaxis(kv, 1, 0)
        d = decay

        def step(r, inc):
            r = d * r + inc
            return (r, r)
        r0 = jnp.zeros((B, H, hd), dtype=q.dtype)
        _, rs = jax.lax.scan(step, r0, kv_t)
        out = qh * jnp.moveaxis(rs, 0, 1)
        return out.reshape(B, S, D)

    def _L0_ffn_ref(hidden_states, gate_w, w1, w2, shared_gate_up_w, shared_down_w, shared_gate_w):
        import jax, jax.numpy as jnp
        import numpy as np
        H = 256
        E = 8
        TOP_K = 2
        I_MOE = 176
        I_SH = 704
        BS, NT = (2, 64)
        bs, nt, h = hidden_states.shape
        x = hidden_states.reshape(-1, h)
        T = x.shape[0]
        gu = x @ shared_gate_up_w.T
        g, u = jnp.split(gu, 2, axis=-1)
        shared = jax.nn.silu(g) * u @ shared_down_w.T
        shared = jax.nn.sigmoid(x @ shared_gate_w.T) * shared
        logits = x @ gate_w.T
        probs = jax.nn.softmax(logits.astype(jnp.float32), axis=-1)
        top_w, top_i = jax.lax.top_k(probs, TOP_K)
        top_w = top_w / jnp.sum(top_w, axis=-1, keepdims=True)
        combine = jnp.zeros((T, E), top_w.dtype).at[jnp.arange(T)[:, None], top_i].set(top_w)
        gu_e = jnp.einsum('th,eih->tei', x, w1)
        ge, ue = jnp.split(gu_e, 2, axis=-1)
        he = jax.nn.silu(ge) * ue
        ye = jnp.einsum('tei,ehi->teh', he, w2)
        out = jnp.einsum('teh,te->th', ye, combine.astype(x.dtype)) + shared
        return out.reshape(bs, nt, h)
    x = _layernorm(x + _L0_attn_ref(x, L0_attn_w_qc, L0_attn_w_qup, L0_attn_w_kv_b, L0_attn_w_z_b, L0_attn_bias_b, L0_attn_w_k, L0_attn_w_v, L0_attn_wi_kv, L0_attn_wi_z, L0_attn_bias_i, L0_attn_w_dq, L0_attn_w_iuq, L0_attn_w_w, L0_attn_q_norm_w, L0_attn_k_norm_w, L0_attn_sink_logit, L0_attn_group_w, L0_attn_final_w), axis=-1)
    x = _layernorm(x + _L0_xattn_ref(x, ctx_2048, ctx_2048, L0_xattn_decay), axis=-1)
    x = _layernorm(x + _L0_ffn_ref(x, L0_ffn_gate_w, L0_ffn_w1, L0_ffn_w2, L0_ffn_shared_gate_up_w, L0_ffn_shared_down_w, L0_ffn_shared_gate_w), axis=-1)
    return x

_drawn_inputs = setup_inputs


def setup_inputs(seed=0):
    import zlib

    import numpy as np

    out = dict(_drawn_inputs(seed))
    spreads = {'L0_attn_bias_b': (0.0, 0.286),
     'L0_attn_bias_i': (0.0, 0.1),
     'L0_attn_q_norm_w': (1.0, 0.6),
     'L0_attn_k_norm_w': (1.0, 0.2),
     'L0_attn_sink_logit': (0.0, 0.8),
     'L0_xattn_decay': (0.8999999761581421, 0.2)}
    factors = {}
    for name, (base, spread) in spreads.items():
        noise = np.random.default_rng([zlib.crc32(name.encode()), seed]).standard_normal(out[name].shape)
        drawn = base * np.exp(spread * noise) if base else spread * noise
        out[name] = jnp.asarray(drawn.astype(out[name].dtype))
    for name, factor in factors.items():
        out[name] = (out[name] * factor).astype(out[name].dtype)
    return out
```

```python
from contextlib import ExitStack

import concourse.bass as bass
from concourse import mybir

F32 = mybir.dt.float32
F32R = mybir.dt.float32r
BF16 = mybir.dt.bfloat16
U32 = mybir.dt.uint32
ALU = mybir.AluOpType
ACT = mybir.ActivationFunctionType
AX_X = mybir.AxisListType.X

P = 128
BATCH, SEQ, HID = 16, 64, 256
TOK = BATCH * SEQ
TILES = TOK // P
KH = HID // P
HEADS, D, ROT = 16, 128, 64
HALF = HEADS // 2
UNITS = 2 * TILES
GROUPS, GDIM = 4, 64
BLK = 32
EXPERTS, I_MOE, I_SH = 8, 176, 704
MOE_ROWS = EXPERTS * I_MOE
FT = -(-(MOE_ROWS + I_SH) // P)
GATES = EXPERTS + 1
CHUNK = 512
TPC = CHUNK // P
WB = 3
RMS_EPS = 1e-6
LN_EPS = 1e-5
SCALE = float(D) ** -0.5


def build(nc, x, xT, ctxT, w_qc, w_qup, w_kv, w_z, biasT, w_k, w_v, knw, qnw, sink, gw, fw, decay,
          gates, wffn, cosT, sinT, mask, ident, first, late, sel, iota, out):
    with ExitStack() as ctx:
        def sb(name, shape, dt=F32):
            return ctx.enter_context(nc.sbuf_tensor(name, shape, dt))

        def psum(name, shape, dt=F32):
            return ctx.enter_context(nc.psum_tensor(name, shape, dt))

        def sem(name):
            return ctx.enter_context(nc.semaphore(name))

        ps_q = psum("ps_q", [P, 1024])
        ps_t = psum("ps_t", [P, 1024])
        ps_s = psum("ps_s", [P, 1024])
        ps_p = psum("ps_p", [P, 512])
        ps_o = psum("ps_o", [P, 512])

        x_sb = sb("x_sb", [P, TILES, HID])
        xT_sb = sb("xT_sb", [P, KH, TOK])
        ctx_sb = sb("ctx_sb", [P, KH, TOK])
        wqc_sb = sb("wqc_sb", [P, KH, P])
        wk_sb = sb("wk_sb", [P, KH, D])
        wv_sb = sb("wv_sb", [P, KH, D])
        wkv_sb = sb("wkv_sb", [P, KH, D])
        wz_sb = sb("wz_sb", [P, KH, D])
        w_raws = sb("w_raws", [P, WB * 3 * HID])
        wqup_sb = w_raws[:, 0:HEADS * D]
        vg_tok = sb("vg_tok", [P, 2, 2, HALF, GDIM])
        gw_sb = vg_tok[:, 0]
        fw_sb = sb("fw_sb", [P, KH, HID])
        bias_sb = sb("bias_sb", [P, BLK])
        knw_sb = sb("knw_sb", [P, D])
        qnw_sb = sb("qnw_sb", [P, D])
        sink_sb = sb("sink_sb", [P, HEADS])
        decay_sb = sb("decay_sb", [P, KH])
        gates_sb = sb("gates_sb", [P, KH, GATES])
        cos_sb = sb("cos_sb", [P, ROT])
        sin_sb = sb("sin_sb", [P, ROT])
        mask_sb = sb("mask_sb", [P, SEQ])
        id_sb = sb("id_sb", [P, P])
        idb_sb = sb("idb_sb", [P, P], BF16)
        first_sb = sb("first_sb", [P, TOK])
        late_sb = sb("late_sb", [BATCH, TOK])
        sel_sb = sb("sel_sb", [3 * GATES, FT * P], BF16)
        iota_sb = sb("iota_sb", [P, EXPERTS])
        nhalf = sb("nhalf", [P, 16])

        whi_buf = sb("whi_buf", [P, WB * 3 * HID], F32R)
        wlo_buf = sb("wlo_buf", [P, WB * 3 * HID], F32R)
        wqup_hi, wqup_lo = whi_buf[:, 0:HEADS * D], wlo_buf[:, 0:HEADS * D]
        gw_hi = sb("gw_hi", [P, 2, HALF, GDIM], F32R)
        gw_lo = sb("gw_lo", [P, 2, HALF, GDIM], F32R)
        qc_hi = sb("qc_hi", [P, TOK], F32R)
        qc_lo = sb("qc_lo", [P, TOK], F32R)
        v_hi = sb("v_hi", [P, TOK], F32R)
        v_lo = sb("v_lo", [P, TOK], F32R)

        q_sq = sb("q_sq", [P, 2, HALF, D])
        qs = sb("qs", [P, 2, HALF, D])
        s_sb = sb("s_sb", [P, 2, HALF, SEQ])
        k_sq = q_sq[:, 0]
        k_ss = sb("k_ss", [P, TILES])
        k_r = sb("k_r", [P, TILES])
        k_n = s_sb[:].rearrange("p u h j -> p (u h j)").rearrange("p (t d) -> p t d", d=D)
        k_a = q_sq[:, 1].rearrange("p h d -> p (h d)")[:, 0:TILES * ROT].rearrange("p (t d) -> p t d", d=ROT)
        k_b = q_sq[:, 1].rearrange("p h d -> p (h d)")[:, TILES * ROT:].rearrange("p (t d) -> p t d", d=ROT)
        kT = sb("kT", [P, TOK])

        z_sb = sb("z_sb", [P, BATCH, BLK])
        z_max = sb("z_max", [P, BATCH])
        z_sum = sb("z_sum", [P, BATCH])
        c_num = sb("c_num", [P, BATCH])
        c_sb = sb("c_sb", [P, BATCH])
        skv_t = sb("skv_t", [BATCH, D])
        skv_sq = sb("skv_sq", [BATCH, D])
        skv_ss = sb("skv_ss", [BATCH, 1])
        skv_r = sb("skv_r", [BATCH, 1])
        skvT = sb("skvT", [P, BATCH])
        sg_sb = sb("sg_sb", [BATCH, HID])
        sgT = sb("sgT", [P, KH, BATCH])
        sgf = sb("sgf", [BATCH, HID])

        kvx = ctx_sb
        dk = qs[:].rearrange("p u h d -> p u (h d)")
        rT = q_sq[:].rearrange("p u h d -> p u (h d)")
        r1 = sb("r1", [P, TILES, HID])

        q_a = sb("q_a", [P, 2, HALF, ROT])
        q_b = sb("q_b", [P, 2, HALF, ROT])
        q_ss = sb("q_ss", [P, 2, HALF])
        q_r = sb("q_r", [P, 2, HALF])
        qT = xT_sb
        m_sb = sb("m_sb", [P, 2, HALF])
        sk_sb = sb("sk_sb", [P, 2, HALF])
        l_sb = sb("l_sb", [P, 2, HALF])
        pT = first_sb[:].rearrange("p (u n) -> p u n", u=2)
        vg = sb("vg", [P, 2, HALF, 2, GDIM])
        oT = sb("oT", [P, 2, KH, P])

        x1p = sb("x1p", [P, 2, HID])
        x1 = sb("x1", [P, 2, HID])
        x2p = sb("x2p", [P, 2, HID])
        x2 = sb("x2", [P, 2, HID])
        st1 = sb("st1", [P, 2, 6])
        mv1 = sb("mv1", [P, 2, 2])
        st2 = sb("st2", [P, 2, 6])
        mv2 = sb("mv2", [P, 2, 2])
        rs1 = sb("rs1", [P, 2])
        rs2 = sb("rs2", [P, 2])
        x2T = ctx_sb
        x2T_hi = sb("x2T_hi", [P, KH, TOK], F32R)
        x2T_lo = sb("x2T_lo", [P, KH, TOK], F32R)

        lgT = sb("lgT", [GATES, CHUNK])
        lg = sb("lg", [P, TPC, GATES])
        lmax = sb("lmax", [P, TPC])
        ex = sb("ex", [P, TPC, GATES])
        top = sb("top", [P, TPC, 8])
        topi = sb("topi", [P, TPC, 8], U32)
        topf = sb("topf", [P, TPC, 2])
        pick = sb("pick", [P, 2, TPC, EXPERTS])
        den = sb("den", [P, TPC])
        cw = sb("cw", [P, TPC, GATES])
        cres = sb("cres", [P, 2, TPC, GATES])
        cparts = sb("cparts", [P, TPC, 3, GATES], BF16)
        cT = sb("cT", [3 * GATES, 2, CHUNK], BF16)

        w_raw = w_raws[:].rearrange("p (b n) -> p b n", b=WB)
        w_hi = whi_buf[:].rearrange("p (b n) -> p b n", b=WB)
        w_lo = wlo_buf[:].rearrange("p (b n) -> p b n", b=WB)
        act_g = q_a[:].rearrange("p u h d -> p u (h d)")
        act_c = q_b[:].rearrange("p u h d -> p u (h d)")
        h_sb = s_sb[:].rearrange("p u h j -> p u (h j)")
        h_hi = qc_hi[:].rearrange("p (u n) -> p u n", u=2)
        h_lo = qc_lo[:].rearrange("p (u n) -> p u n", u=2)
        yT = xT_sb[:, :, 0:CHUNK]
        y_sb = sb("y_sb", [P, 2, HID])
        st3 = sb("st3", [P, 2, 6])
        mv3 = sb("mv3", [P, 2, 2])
        rs3 = sb("rs3", [P, 2])
        y_out = qs[:].rearrange("p u h d -> p (u h d)").rearrange("p (t n) -> p t n", n=HID)

        ld = {n: sem("ld_" + n) for n in ("xT", "wqc", "wqup", "wk", "wv", "wc", "gw", "fw", "x", "norm", "rope",
                                           "mask", "id", "ctx", "decay", "late", "gates", "route", "bias")}
        ld_w = [sem(f"ld_w{i}") for i in range(WB)]
        s_const = sem("s_const")
        s_qc_mm, s_v_mm, s_k_mm, s_c_mm = sem("s_qc_mm"), sem("s_v_mm"), sem("s_k_mm"), sem("s_c_mm")
        s_qc_hi, s_qc_lo, s_v_hi, s_v_lo = sem("s_qc_hi"), sem("s_qc_lo"), sem("s_v_hi"), sem("s_v_lo")
        s_wqup_hi, s_wqup_lo, s_gw_hi, s_gw_lo = sem("s_wqup_hi"), sem("s_wqup_lo"), sem("s_gw_hi"), sem("s_gw_lo")
        s_k_sq, s_k_ss, s_k_r, s_k_dve, s_k_t, s_kT = (sem("s_k_sq"), sem("s_k_ss"), sem("s_k_r"), sem("s_k_dve"),
                                                      sem("s_k_t"), sem("s_kT"))
        s_z, s_z_exp, s_c_act, s_skv_r, s_skv_mm = (sem("s_z"), sem("s_z_exp"), sem("s_c_act"),
                                                   sem("s_skv_r"), sem("s_skv_mm"))
        s_skv = sem("s_skv")
        s_kvx, s_scan, s_r_t, s_r1 = sem("s_kvx"), sem("s_scan"), sem("s_r_t"), sem("s_r1")
        s_q_mm, s_qs, s_q_sq, s_rope, s_q_ss, s_q_r = (sem("s_q_mm"), sem("s_qs"), sem("s_q_sq"), sem("s_rope"),
                                                      sem("s_q_ss"), sem("s_q_r"))
        s_rot, s_qT_t, s_qT, s_s_mm, s_s1, s_mask, s_max, s_sub = (sem("s_rot"), sem("s_qT_t"), sem("s_qT"),
                                                                  sem("s_s_mm"), sem("s_s1"), sem("s_mask"),
                                                                  sem("s_max"), sem("s_sub"))
        s_exp, s_l, s_norm, s_pT_t, s_pT, s_pv = (sem("s_exp"), sem("s_l"), sem("s_norm"), sem("s_pT_t"),
                                                 sem("s_pT"), sem("s_pv"))
        s_vg_mm, s_vg_tok = sem("s_vg_mm"), sem("s_vg_tok")
        s_vg = [sem("s_vg0"), sem("s_vg1")]
        s_oT, s_fin = sem("s_oT"), sem("s_fin")
        s_x1p, s_ln1, s_rs1, s_ln2, s_rs2, s_x2, s_x2_t, s_x2T, s_x2hi, s_x2lo = (
            sem("s_x1p"), sem("s_ln1"), sem("s_rs1"), sem("s_ln2"), sem("s_rs2"), sem("s_x2"), sem("s_x2_t"),
            sem("s_x2T"), sem("s_x2hi"), sem("s_x2lo"))
        s_lnc = sem("s_lnc")
        s_pool, s_scan_in, s_skv_ss, s_mx, s_l0 = (sem("s_pool"), sem("s_scan_in"), sem("s_skv_ss"), sem("s_mx"),
                                                  sem("s_l0"))
        s_lg_mm, s_lgT, s_lg_t, s_lg, s_lsub, s_lexp, s_rt, s_cw, s_c_t, s_cT = (
            sem("s_lg_mm"), sem("s_lgT"), sem("s_lg_t"), sem("s_lg"), sem("s_lsub"), sem("s_lexp"), sem("s_rt"),
            sem("s_cw"), sem("s_c_t"), sem("s_cT"))
        s_whi, s_wlo, s_g_mm, s_u_mm, s_cb, s_silu, s_gc, s_h, s_hhi, s_hlo, s_dn = (
            sem("s_whi"), sem("s_wlo"), sem("s_g_mm"), sem("s_u_mm"), sem("s_cb"), sem("s_silu"), sem("s_gc"),
            sem("s_h"), sem("s_hhi"), sem("s_hlo"), sem("s_dn"))
        s_y3 = sem("s_y3")
        s_yT, s_y_t, s_y, s_ln3, s_rs3, s_yo, s_st = (sem("s_yT"), sem("s_y_t"), sem("s_y"), sem("s_ln3"),
                                                     sem("s_rs3"), sem("s_yo"), sem("s_st"))

        NIT = 2 * FT

        def bc(ap, shape):
            return ap.to_broadcast(shape)

        def tok(t):
            return slice(t * P, (t + 1) * P)

        block = ctx.enter_context(nc.Block())

        @block.sync
        def _(sp):
            def load(dst, src, s):
                sp.dma_start(dst, src).then_inc(s, 16)

            def store(t):
                sp.wait_ge(s_yo, t + 1)
                sp.dma_start(out[tok(t)], y_out[:, t]).then_inc(s_st, 16)

            load(xT_sb[:], xT.rearrange("(k p) n -> p k n", p=P), ld["xT"])
            load(wqc_sb[:], w_qc.rearrange("(k p) n -> p k n", p=P), ld["wqc"])
            load(wk_sb[:], w_k.rearrange("(k p) n -> p k n", p=P), ld["wk"])
            load(wqup_sb, w_qup, ld["wqup"])
            load(ctx_sb[:], ctxT.rearrange("(k p) n -> p k n", p=P), ld["ctx"])
            load(wv_sb[:], w_v.rearrange("(k p) n -> p k n", p=P), ld["wv"])
            load(wkv_sb[:], w_kv.rearrange("(k p) n -> p k n", p=P), ld["wc"])
            load(wz_sb[:], w_z.rearrange("(k p) n -> p k n", p=P), ld["wc"])
            load(gw_sb[:], gw.rearrange("p (a h o) -> p a h o", a=2, h=HALF), ld["gw"])
            load(fw_sb[:], fw.rearrange("(k p) n -> p k n", p=P), ld["fw"])
            load(x_sb[:], x.rearrange("(t p) n -> p t n", p=P), ld["x"])
            load(late_sb[:], late, ld["late"])
            load(gates_sb[:], gates.rearrange("(k p) n -> p k n", p=P), ld["gates"])
            load(sel_sb[:], sel, ld["route"])
            load(iota_sb[:], iota, ld["route"])
            for t in range(TILES):
                sp.wait_ge(s_vg_tok, t + 1)
                if t >= 2:
                    sp.wait_ge(s_pv, 2 * (t - 1))
                for b in range(2):
                    for par in range(2):
                        sp.dma_start(vg[par * 64:par * 64 + 64, t % 2, :, b], vg_tok[b * 64:b * 64 + 64, t % 2, par]) \
                          .then_inc(s_vg[t % 2], 16)
            sp.wait_ge(s_wqup_hi, 1)
            sp.wait_ge(s_wqup_lo, 1)
            for j in range(NIT):
                if j >= WB:
                    sp.wait_ge(s_whi, j - WB + 1)
                    sp.wait_ge(s_wlo, j - WB + 1)
                load(w_raw[:, j % WB], wffn[j % FT], ld_w[j % WB])
                if FT + 6 <= j < FT + 6 + TPC:
                    store(j - FT - 6)
            for t in range(TPC, TILES):
                store(t)
            sp.wait_ge(s_st, 16 * TILES)

        @block.scalar
        def _(act):
            def load(dst, src, s):
                act.dma_start(dst, src).then_inc(s, 16)

            load(id_sb[:], ident, ld["id"])
            load(cos_sb[:], cosT, ld["rope"])
            load(sin_sb[:], sinT, ld["rope"])
            load(knw_sb[:], knw, ld["norm"])
            load(qnw_sb[:], qnw, ld["norm"])
            load(decay_sb[:], decay, ld["decay"])
            load(first_sb[:], first, ld["decay"])
            load(mask_sb[:], mask, ld["mask"])
            load(sink_sb[:], sink, ld["mask"])
            load(bias_sb[:], biasT, ld["bias"])

            act.wait_ge(ld["id"], 16)
            nc.scalar.copy(idb_sb[:], id_sb[:]).then_inc(s_const, 1)
            act.wait_ge(ld["wqup"], 16)
            nc.scalar.copy(wqup_hi, wqup_sb).then_inc(s_wqup_hi, 1)
            act.wait_ge(s_qc_mm, 1)
            nc.scalar.copy(qc_hi[:], ps_q[:]).then_inc(s_qc_hi, 1)
            act.wait_ge(s_k_mm, 1)
            nc.scalar.activation(k_sq[:], ps_s[:].rearrange("p (t d) -> p t d", d=D), ACT.Square).then_inc(s_k_sq, 1)
            act.wait_ge(ld["ctx"], 16)
            nc.scalar.activation(kvx[:], ctx_sb[:], ACT.Square).then_inc(s_kvx, 1)
            act.wait_ge(s_v_mm, 1)
            nc.scalar.copy(v_hi[:], ps_t[:]).then_inc(s_v_hi, 1)
            act.wait_ge(ld["gw"], 16)
            nc.scalar.copy(gw_hi[:], gw_sb[:]).then_inc(s_gw_hi, 1)
            act.wait_ge(s_z, 3)
            nc.scalar.activation(z_sb[:], z_sb[:], ACT.Exp).then_inc(s_z_exp, 1)
            act.wait_ge(s_k_t, 1)
            nc.scalar.copy(kT[:], ps_q[:]).then_inc(s_kT, 1)
            for k in range(KH):
                act.wait_ge(s_r_t, k + 1)
                nc.scalar.activation(r1[:, :, k * P:(k + 1) * P],
                                     (ps_t, ps_s)[k][:].rearrange("p (t d) -> p t d", d=P), ACT.Identity,
                                     bias=1.0).then_inc(s_r1, 1)

            def evac_q(u):
                act.wait_ge(s_q_mm, u + 1)
                if u >= 2:
                    act.wait_ge(s_qT_t, u - 1)
                nc.scalar.copy(qs[:, u % 2], ps_q[:].rearrange("p (h d) -> p h d", d=D)).then_inc(s_qs, 1)
                act.wait_ge(s_qs, u + 1)
                if u >= 2:
                    act.wait_ge(s_q_ss, u - 1)
                nc.scalar.activation(q_sq[:, u % 2], qs[:, u % 2], ACT.Square).then_inc(s_q_sq, 1)

            def evac_qT(u):
                act.wait_ge(s_qT_t, u + 1)
                if u >= 2:
                    act.wait_ge(s_s_mm, u - 1)
                nc.scalar.copy(qT[:, u % 2], ps_t[:]).then_inc(s_qT, 1)

            def exp(u):
                act.wait_ge(s_sub, 2 * (u + 1))
                nc.scalar.activation(sk_sb[:, u % 2], sk_sb[:, u % 2], ACT.Exp).then_inc(s_exp, 1)
                nc.scalar.activation(s_sb[:, u % 2], s_sb[:, u % 2], ACT.Exp).then_inc(s_exp, 1)

            def evac_pT(u):
                act.wait_ge(s_pT_t, u + 1)
                if u >= 2:
                    act.wait_ge(s_pv, u - 1)
                nc.scalar.copy(pT[:, u % 2], ps_p[:]).then_inc(s_pT, 1)

            def evac_vg(t):
                act.wait_ge(s_vg_mm, t + 1)
                if t >= 2:
                    act.wait_ge(s_vg[t % 2], 64 * (t // 2))
                nc.scalar.copy(vg_tok[:, t % 2], ps_t[:].rearrange("p (a h o) -> p a h o", a=2, o=GDIM)) \
                    .then_inc(s_vg_tok, 1)

            def evac_x2(t, ps):
                act.wait_ge(s_x2_t, t + 1)
                src = ps[:, 0:HID].rearrange("p (k n) -> p k n", k=KH)
                nc.scalar.copy(x2T[:, :, tok(t)], src).then_inc(s_x2T, 1)
                nc.scalar.copy(x2T_hi[:, :, tok(t)], src).then_inc(s_x2hi, 1)

            def route_copy(c, ps):
                act.wait_ge(s_lg_mm, c + 1)
                if c:
                    act.wait_ge(s_lg_t, c)
                nc.scalar.copy(lgT[:], ps[0:GATES, :]).then_inc(s_lgT, 1)

            def route_exp(c):
                act.wait_ge(s_lsub, c + 1)
                nc.scalar.activation(ex[:], lg[:], ACT.Exp).then_inc(s_lexp, 1)

            def route_cT(c, ps):
                act.wait_ge(s_c_t, c + 1)
                nc.scalar.copy(cT[:, c], ps[:].bitcast(BF16)[0:3 * GATES, 0:CHUNK]).then_inc(s_cT, 1)

            evac_q(0)
            for n in range(UNITS + 1):
                if n >= 6 and n % 2 == 0:
                    evac_x2((n - 6) // 2, ps_p)
                if n == 13:
                    route_copy(0, ps_p)
                if n < UNITS:
                    evac_qT(n)
                if n >= 1:
                    exp(n - 1)
                if n == 15:
                    route_exp(0)
                if n + 1 < UNITS:
                    evac_q(n + 1)
                if n >= 1:
                    evac_pT(n - 1)
                if n < UNITS and n % 2 == 0:
                    evac_vg(n // 2)
            route_cT(0, ps_q)

            def split_w(j):
                act.wait_ge(ld_w[j % WB], 16 * (j // WB + 1))
                if j >= WB:
                    act.wait_ge(s_dn, j - WB + 1)
                nc.scalar.copy(w_hi[:, j % WB], w_raw[:, j % WB]).then_inc(s_whi, 1)

            split_w(0)
            split_w(1)
            for j in range(NIT):
                if j >= 2:
                    act.wait_ge(s_gc, j - 1)
                act.wait_ge(s_g_mm, j + 1)
                nc.scalar.activation(act_g[:, j % 2], ps_q[:, (j % 2) * CHUNK:(j % 2 + 1) * CHUNK], ACT.Silu) \
                    .then_inc(s_silu, 1)
                if j >= 1 and j + 1 < NIT:
                    split_w(j + 1)
                act.wait_ge(s_h, j + 1)
                if j >= 2:
                    act.wait_ge(s_dn, j - 1)
                nc.scalar.copy(h_hi[:, j % 2], h_sb[:, j % 2]).then_inc(s_hhi, 1)
                if j == 4:
                    evac_x2(6, ps_o)
                if j == 7:
                    evac_x2(7, ps_o)
                if j == 8:
                    route_copy(1, ps_o)
                if j == 9:
                    route_exp(1)
                if j == 12:
                    route_cT(1, ps_o)

        @block.tensor
        def _(pe):
            mm = nc.tensor.matmul

            def three(dst, w, a, first_, last_):
                (wh, wl), (ah, al) = w, a
                mm(dst, wh, ah, start=first_, stop=False)
                mm(dst, wl, ah, start=False, stop=False)
                return mm(dst, wh, al, start=False, stop=last_)

            pe.wait_ge(ld["xT"], 16)
            pe.wait_ge(ld["wqc"], 16)
            for c in range(2):
                for k in range(KH):
                    i = mm(ps_q[:, c * 512:(c + 1) * 512], wqc_sb[:, k], xT_sb[:, k, c * 512:(c + 1) * 512],
                           start=k == 0, stop=k == KH - 1)
            i.then_inc(s_qc_mm, 1)
            pe.wait_ge(ld["wk"], 16)
            for t in range(TILES):
                for k in range(KH):
                    i = mm(ps_s[:, tok(t)], xT_sb[:, k, tok(t)], wk_sb[:, k], start=k == 0, stop=k == KH - 1)
            i.then_inc(s_k_mm, 1)
            pe.wait_ge(ld["wv"], 16)
            for c in range(2):
                for k in range(KH):
                    i = mm(ps_t[:, c * 512:(c + 1) * 512], wv_sb[:, k], xT_sb[:, k, c * 512:(c + 1) * 512],
                           start=k == 0, stop=k == KH - 1)
            i.then_inc(s_v_mm, 1)
            pe.wait_ge(ld["wc"], 32)
            for w, ps in ((wz_sb, ps_o), (wkv_sb, ps_p)):
                for k in range(KH):
                    blk = xT_sb[:, k].rearrange("p (b s) -> p b s", s=SEQ)[:, :, 0:BLK]
                    i = mm(ps[:], w[:, k], blk, start=k == 0, stop=k == KH - 1)
                i.then_inc(s_c_mm, 1)
            pe.wait_ge(ld["id"], 16)
            pe.wait_ge(s_k_dve, 7)
            pe.wait_ge(s_qc_hi, 1)
            pe.wait_ge(s_qc_lo, 1)
            for t in range(TILES):
                i = nc.tensor.transpose(ps_q[:, tok(t)], k_n[:, t], id_sb[:])
            i.then_inc(s_k_t, 1)
            pe.wait_ge(s_v_hi, 1)
            pe.wait_ge(s_v_lo, 1)
            for k in range(KH):
                pe.wait_ge(s_scan, k + 1)
                if k == 1:
                    pe.wait_ge(s_k_sq, 1)
                    pe.wait_ge(s_k_dve, 1)
                for t in range(TILES):
                    i = nc.tensor.transpose((ps_t, ps_s)[k][:, tok(t)], rT[:, k, tok(t)], id_sb[:])
                i.then_inc(s_r_t, 1)
            pe.wait_ge(s_skv, 1)
            nc.tensor.transpose(ps_o[0:BATCH, 0:P], c_sb[:], id_sb[:]).then_inc(s_skv_mm, 1)
            pe.wait_ge(s_skv, 2)
            nc.tensor.transpose(ps_o[:, 0:BATCH], skv_t[:], id_sb[0:BATCH, 0:BATCH]).then_inc(s_skv_mm, 1)
            pe.wait_ge(s_skv, 3)
            pe.wait_ge(ld["gw"], 16)
            for h in range(4):
                gwh = gw_sb[:, h % 2].rearrange("p (g c) o -> p g c o", c=2)[:, :, h // 2]
                i = mm(ps_o[0:BATCH, 0:HID], skvT[:], gwh, start=h == 0, stop=h == 3)
            i.then_inc(s_skv_mm, 1)
            pe.wait_ge(s_skv, 4)
            for k in range(KH):
                i = nc.tensor.transpose(ps_o[:, k * BATCH:(k + 1) * BATCH], sg_sb[:, k * P:(k + 1) * P],
                                        id_sb[0:BATCH, 0:BATCH])
            i.then_inc(s_skv_mm, 1)
            pe.wait_ge(s_skv, 5)
            pe.wait_ge(ld["fw"], 16)
            for k in range(KH):
                i = mm(ps_o[0:BATCH, 0:HID], sgT[:, k], fw_sb[:, k], start=k == 0, stop=k == KH - 1)
            i.then_inc(s_skv_mm, 1)

            def q_mm(u):
                t, hf = u // 2, u % 2
                if u >= 1:
                    pe.wait_ge(s_qs, u)
                for c in range(2):
                    cols = slice(hf * 1024 + c * 512, hf * 1024 + (c + 1) * 512)
                    i = three(ps_q[:, c * 512:(c + 1) * 512], (qc_hi[:, tok(t)], qc_lo[:, tok(t)]),
                              (wqup_hi[:, cols], wqup_lo[:, cols]), True, True)
                i.then_inc(s_q_mm, 1)

            def q_turn(u):
                pe.wait_ge(s_rot, u + 1)
                if u % 2 == 1:
                    pe.wait_ge(s_vg_tok, u // 2 + 1)
                if u >= 1:
                    pe.wait_ge(s_qT, u)
                for h in range(HALF):
                    i = nc.tensor.transpose(ps_t[:, h * P:(h + 1) * P], qs[:, u % 2, h], id_sb[:])
                i.then_inc(s_qT_t, 1)

            def scores(u):
                pe.wait_ge(s_qT, u + 1)
                if u >= 1:
                    pe.wait_ge(s_s1, 2 * u)
                for h in range(HALF):
                    i = mm(ps_s[:, h * P:(h + 1) * P], qT[:, u % 2, h * P:(h + 1) * P], kT[:, tok(u // 2)],
                           start=True, stop=True)
                i.then_inc(s_s_mm, 1)

            def p_turn(u):
                pe.wait_ge(s_norm, u + 1)
                for p in range(4):
                    i = nc.tensor.transpose(ps_p[:, p * P:(p + 1) * P],
                                            s_sb[:, u % 2, 2 * p:2 * p + 2].rearrange("p a j -> p (a j)"), id_sb[:])
                i.then_inc(s_pT_t, 1)

            def pv(u):
                t, hf = u // 2, u % 2
                pe.wait_ge(s_pT, u + 1)
                if hf == 0:
                    pe.wait_ge(s_vg[t % 2], 64 * (t // 2 + 1))
                    if t:
                        pe.wait_ge(s_x1p, t)
                for g in range(2):
                    for p in range(2):
                        i = mm(ps_o[:, (2 * hf + g) * P:(2 * hf + g + 1) * P], vg[:, t % 2, 4 * hf + 2 * g + p].rearrange("p b o -> p (b o)"),
                               pT[:, u % 2, (2 * g + p) * P:(2 * g + p + 1) * P], start=p == 0, stop=p == 1)
                i.then_inc(s_pv, 1)

            def vg_mm(t):
                pe.wait_ge(s_qT, 2 * t + 1)
                for a in range(2):
                    cols = (gw_hi[:, a], gw_lo[:, a])
                    i = three(ps_t[:, a * 512:(a + 1) * 512], (v_hi[:, tok(t)], v_lo[:, tok(t)]), cols, True, True)
                i.then_inc(s_vg_mm, 1)

            def final(t):
                pe.wait_ge(s_oT, 4 * (t + 1))
                for k in range(KH):
                    mm(ps_o[:, 0:HID], oT[:, t % 2, k], fw_sb[:, k], start=k == 0, stop=False)
                mm(ps_o[:, 0:HID], late_sb[:, tok(t)], sgf[:], start=False, stop=True).then_inc(s_fin, 1)

            def x2_turn(t, ps):
                pe.wait_ge(s_x2, t + 1)
                for k in range(KH):
                    i = nc.tensor.transpose(ps[:, k * P:(k + 1) * P], x2[:, t % 2, k * P:(k + 1) * P], id_sb[:])
                i.then_inc(s_x2_t, 1)

            def logits(c, ps):
                pe.wait_ge(s_x2T, TPC * (c + 1))
                for k in range(KH):
                    i = mm(ps[0:GATES, :], gates_sb[:, k], x2T[:, k, c * CHUNK:(c + 1) * CHUNK],
                           start=k == 0, stop=k == KH - 1)
                i.then_inc(s_lg_mm, 1)

            def logits_turn(c, ps):
                pe.wait_ge(s_lgT, c + 1)
                for t in range(TPC):
                    i = nc.tensor.transpose(ps[:, t * GATES:(t + 1) * GATES], lgT[:, tok(t)],
                                            id_sb[0:GATES, 0:GATES])
                i.then_inc(s_lg_t, 1)

            def weights_turn(c, ps):
                pe.wait_ge(s_cw, c + 1)
                for t in range(TPC):
                    i = nc.tensor.transpose(ps[:].bitcast(BF16)[0:3 * GATES, tok(t)],
                                            cparts[:, t].rearrange("p a g -> p (a g)"), idb_sb[:])
                i.then_inc(s_c_t, 1)

            pe.wait_ge(s_wqup_hi, 1)
            pe.wait_ge(s_wqup_lo, 1)
            pe.wait_ge(s_kT, 1)
            q_mm(0)
            pe.wait_ge(s_r1, 2)
            pe.wait_ge(s_gw_hi, 1)
            pe.wait_ge(s_gw_lo, 1)
            pe.wait_ge(s_const, 2)
            pe.wait_ge(ld["late"], 16)
            for n in range(UNITS + 1):
                if n >= 6 and n % 2 == 0:
                    pe.wait_ge(s_pT, n - 1)
                    x2_turn((n - 6) // 2, ps_p)
                if n == 13:
                    pe.wait_ge(s_pT, n - 1)
                    pe.wait_ge(ld["gates"], 16)
                    logits(0, ps_p)
                if n == 14:
                    pe.wait_ge(s_qs, n + 1)
                    logits_turn(0, ps_q)
                if n < UNITS:
                    q_turn(n)
                if n + 1 < UNITS:
                    if n == 14:
                        pe.wait_ge(s_lg, 1)
                    q_mm(n + 1)
                if n < UNITS:
                    scores(n)
                if n >= 1:
                    if n >= 6 and n % 2 == 0:
                        pe.wait_ge(s_x2hi, (n - 6) // 2 + 1)
                    if n == 13:
                        pe.wait_ge(s_lgT, 1)
                    p_turn(n - 1)
                if n >= 3 and n % 2 == 1:
                    final((n - 3) // 2)
                if n >= 1:
                    pv(n - 1)
                if n < UNITS and n % 2 == 0:
                    vg_mm(n // 2)
            pe.wait_ge(s_qs, UNITS)
            weights_turn(0, ps_q)

            def up(j):
                c, f = j // FT, j % FT
                toks = slice(c * CHUNK, (c + 1) * CHUNK)
                pe.wait_ge(s_cT, c + 1)
                if j >= 1:
                    pe.wait_ge(s_gc, j)
                if j == 0:
                    pe.wait_ge(s_pT, UNITS)
                mm(ps_p[:], sel_sb[:, tok(f)], cT[:, c], start=True, stop=True).then_inc(s_cb, 1)
                pe.wait_ge(s_whi, j + 1)
                pe.wait_ge(s_wlo, j + 1)
                if j == 0:
                    pe.wait_ge(s_x2lo, TPC)
                if j == FT:
                    pe.wait_ge(s_x2lo, TILES)
                if j >= 2:
                    pe.wait_ge(s_silu, j - 1)
                for s, ps, done in ((0, ps_q, s_g_mm), (1, ps_t, s_u_mm)):
                    dst = ps[:, (j % 2) * CHUNK:(j % 2 + 1) * CHUNK]
                    if s and j >= 2:
                        pe.wait_ge(s_h, j - 1)
                    for k in range(KH):
                        cols = slice(k * HID + s * P, k * HID + (s + 1) * P)
                        i = three(dst, (w_hi[:, j % WB, cols], w_lo[:, j % WB, cols]),
                                  (x2T_hi[:, k, toks], x2T_lo[:, k, toks]), k == 0, k == KH - 1)
                    i.then_inc(done, 1)

            def down(j):
                c, f = j // FT, j % FT
                pe.wait_ge(s_hhi, j + 1)
                pe.wait_ge(s_hlo, j + 1)
                if j == 0:
                    pe.wait_ge(s_s1, 2 * UNITS)
                if j == FT:
                    pe.wait_ge(s_yT, KH)
                for k in range(KH):
                    cols = slice(2 * HID + k * P, 2 * HID + (k + 1) * P)
                    i = three(ps_s[:, k * CHUNK:(k + 1) * CHUNK], (w_hi[:, j % WB, cols], w_lo[:, j % WB, cols]),
                              (h_hi[:, j % 2], h_lo[:, j % 2]), f == 0, f == FT - 1)
                i.then_inc(s_dn, 1)

            def y_turn(c, t):
                n = c * TPC + t
                pe.wait_ge(s_yT, KH * (c + 1))
                if n >= 1:
                    pe.wait_ge(s_y, n)
                for k in range(KH):
                    i = nc.tensor.transpose(ps_o[:, k * P:(k + 1) * P], yT[:, k, tok(t)], id_sb[:])
                i.then_inc(s_y_t, 1)

            pe.wait_ge(ld["route"], 32)
            for j in range(NIT):
                up(j)
                if j >= 1:
                    down(j - 1)
                if j == 0:
                    final(7)
                if j == 4:
                    pe.wait_ge(s_x1p, TILES)
                    x2_turn(6, ps_o)
                if j == 7:
                    pe.wait_ge(s_x2hi, 7)
                    x2_turn(7, ps_o)
                if j == 8:
                    pe.wait_ge(s_x2hi, 8)
                    logits(1, ps_o)
                if j == 9:
                    logits_turn(1, ps_o)
                if j == 12:
                    pe.wait_ge(s_lg, 2)
                    weights_turn(1, ps_o)
                if FT + 2 <= j < FT + 2 + TPC:
                    y_turn(0, j - FT - 2)
            down(NIT - 1)
            for t in range(TPC):
                y_turn(1, t)

        @block.gpsimd
        def _(pool):
            cnt = [0]

            def link(i):
                cnt[0] += 1
                i.then_inc(s_pool, 1)
                pool.wait_ge(s_pool, cnt[0])

            def power(dst, src, scale, eps, rows=P):
                link(nc.gpsimd.tensor_scalar(dst, src, scale, eps, ALU.mult, ALU.add))
                return nc.gpsimd.tensor_tensor(dst, dst, nhalf[0:rows, 0:dst.shape[-1]], ALU.pow)

            link(nc.gpsimd.memset(nhalf[:], -0.5))
            pool.wait_ge(s_k_ss, 1)
            power(k_r[:], k_ss[:], 1.0 / D, RMS_EPS).then_inc(s_k_r, 1)
            pool.wait_ge(s_gw_hi, 1)
            nc.gpsimd.tensor_tensor(gw_lo[:], gw_sb[:], gw_hi[:].bitcast(F32), ALU.subtract).then_inc(s_gw_lo, 1)
            pool.wait_ge(s_skv_ss, 1)
            power(skv_r[:], skv_ss[:], 1.0 / D, RMS_EPS, BATCH).then_inc(s_skv_r, 1)

            def rot(u):
                pool.wait_ge(s_rope, u + 1)
                nc.gpsimd.tensor_tensor(qs[:, u % 2, :, 0:ROT], q_a[:, u % 2], q_b[:, u % 2], ALU.add) \
                    .then_inc(s_rot, 1)
                pool.wait_ge(s_q_ss, u + 1)
                if u >= 2:
                    pool.wait_ge(s_s1, 2 * (u - 1))
                power(q_r[:, u % 2], q_ss[:, u % 2], 1.0, D * RMS_EPS).then_inc(s_q_r, 1)

            def add_mask(u):
                pool.wait_ge(s_s1, 2 * (u + 1))
                nc.gpsimd.tensor_tensor(s_sb[:, u % 2], s_sb[:, u % 2],
                                        bc(mask_sb[:].unsqueeze(1), [P, HALF, SEQ]), ALU.add).then_inc(s_mask, 1)

            def sub_max(u):
                hs = slice((u % 2) * HALF, (u % 2 + 1) * HALF)
                pool.wait_ge(s_max, u + 1)
                nc.gpsimd.tensor_tensor(sk_sb[:, u % 2], sink_sb[:, hs], m_sb[:, u % 2], ALU.subtract) \
                    .then_inc(s_sub, 1)
                nc.gpsimd.tensor_tensor(s_sb[:, u % 2], s_sb[:, u % 2],
                                        bc(m_sb[:, u % 2].unsqueeze(2), [P, HALF, SEQ]), ALU.subtract) \
                    .then_inc(s_sub, 1)

            def norm(u):
                pool.wait_ge(s_l, u + 1)
                nc.gpsimd.tensor_tensor(s_sb[:, u % 2], s_sb[:, u % 2],
                                        bc(l_sb[:, u % 2].unsqueeze(2), [P, HALF, SEQ]), ALU.mult) \
                    .then_inc(s_norm, 1)

            def ln_power(rs, mv, t, wait, done):
                pool.wait_ge(wait, t + 1)
                link(nc.gpsimd.tensor_scalar(rs[:, t % 2:t % 2 + 1], mv[:, t % 2, 1:2], 1.0, LN_EPS,
                                             ALU.mult, ALU.add))
                nc.gpsimd.tensor_tensor(rs[:, t % 2:t % 2 + 1], rs[:, t % 2:t % 2 + 1], nhalf[:, 0:1], ALU.pow) \
                    .then_inc(done, 1)

            pool.wait_ge(ld["mask"], 32)
            rot(0)
            for n in range(UNITS + 1):
                if n >= 1:
                    norm(n - 1)
                if n + 1 < UNITS:
                    rot(n + 1)
                if n >= 4 and n % 2 == 0:
                    ln_power(rs1, mv1, (n - 4) // 2, s_ln1, s_rs1)
                if n < UNITS:
                    add_mask(n)
                    sub_max(n)
                if n >= 4 and n % 2 == 0:
                    ln_power(rs2, mv2, (n - 4) // 2, s_ln2, s_rs2)

            for j in range(NIT):
                pool.wait_ge(s_whi, j + 1)
                nc.gpsimd.tensor_tensor(w_lo[:, j % WB], w_raw[:, j % WB], w_hi[:, j % WB].bitcast(F32),
                                        ALU.subtract).then_inc(s_wlo, 1)
                if j == 2:
                    ln_power(rs1, mv1, 7, s_ln1, s_rs1)
                    ln_power(rs2, mv2, 7, s_ln2, s_rs2)
                if FT + 2 <= j < FT + 2 + TPC:
                    ln_power(rs3, mv3, j - FT - 2, s_ln3, s_rs3)
            for t in range(TPC):
                ln_power(rs3, mv3, TPC + t, s_ln3, s_rs3)

        @block.vector
        def _(dve):
            tt = nc.vector.tensor_tensor

            dve.wait_ge(ld["decay"], 32)
            for k in range(KH):
                i = nc.vector.tensor_scalar(dk[:, k], first_sb[:], decay_sb[:, k:k + 1], None, ALU.mult)
            i.then_inc(s_scan_in, 1)
            dve.wait_ge(s_wqup_hi, 1)
            tt(wqup_lo, wqup_sb, wqup_hi.bitcast(F32), ALU.subtract).then_inc(s_wqup_lo, 1)
            dve.wait_ge(s_qc_hi, 1)
            tt(qc_lo[:], ps_q[:], qc_hi[:].bitcast(F32), ALU.subtract).then_inc(s_qc_lo, 1)
            dve.wait_ge(s_k_sq, 1)
            nc.vector.tensor_reduce(k_ss[:], k_sq[:], AX_X, ALU.add).then_inc(s_k_ss, 1)
            dve.wait_ge(s_k_r, 1)
            dve.wait_ge(ld["norm"], 32)
            dve.wait_ge(ld["rope"], 32)
            kp = ps_s[:].rearrange("p (t d) -> p t d", d=D)
            tt(k_n[:], kp, bc(k_r[:].unsqueeze(2), [P, TILES, D]), ALU.mult).then_inc(s_k_dve, 1)
            dve.wait_ge(s_k_dve, 1)
            tt(k_n[:], k_n[:], bc(knw_sb[:].unsqueeze(1), [P, TILES, D]), ALU.mult).then_inc(s_k_dve, 1)
            dve.wait_ge(s_k_dve, 2)
            h = ROT // 2
            tt(k_a[:], k_n[:, :, 0:ROT], bc(cos_sb[:].unsqueeze(1), [P, TILES, ROT]), ALU.mult).then_inc(s_k_dve, 1)
            tt(k_b[:, :, 0:h], k_n[:, :, h:ROT], bc(sin_sb[:, 0:h].unsqueeze(1), [P, TILES, h]), ALU.mult) \
                .then_inc(s_k_dve, 1)
            tt(k_b[:, :, h:ROT], k_n[:, :, 0:h], bc(sin_sb[:, h:ROT].unsqueeze(1), [P, TILES, h]), ALU.mult) \
                .then_inc(s_k_dve, 1)
            dve.wait_ge(s_k_dve, 5)
            tt(k_n[:, :, 0:ROT], k_a[:], k_b[:], ALU.add).then_inc(s_k_dve, 1)
            dve.wait_ge(s_k_dve, 6)
            tt(k_n[:], k_n[:], bc(qnw_sb[:].unsqueeze(1), [P, TILES, D]), ALU.mult).then_inc(s_k_dve, 1)
            dve.wait_ge(s_v_hi, 1)
            tt(v_lo[:], ps_t[:], v_hi[:].bitcast(F32), ALU.subtract).then_inc(s_v_lo, 1)
            dve.wait_ge(s_kvx, 1)
            dve.wait_ge(s_scan_in, 1)
            for k in range(KH):
                nc.vector.tensor_tensor_scan(rT[:, k], dk[:, k], kvx[:, k], 0.0, ALU.mult, ALU.add) \
                    .then_inc(s_scan, 1)
            dve.wait_ge(s_c_mm, 2)
            dve.wait_ge(ld["bias"], 16)
            zp = ps_o[:].rearrange("p (b m) -> p b m", m=BLK)
            cp = ps_p[:].rearrange("p (b m) -> p b m", m=BLK)
            tt(z_sb[:], zp, bc(bias_sb[:].unsqueeze(1), [P, BATCH, BLK]), ALU.add).then_inc(s_z, 1)
            dve.wait_ge(s_z, 1)
            nc.vector.tensor_reduce(z_max[:], z_sb[:], AX_X, ALU.max).then_inc(s_z, 1)
            dve.wait_ge(s_z, 2)
            tt(z_sb[:], z_sb[:], bc(z_max[:].unsqueeze(2), [P, BATCH, BLK]), ALU.subtract).then_inc(s_z, 1)
            dve.wait_ge(s_z_exp, 1)
            nc.vector.tensor_reduce(z_sum[:], z_sb[:], AX_X, ALU.add).then_inc(s_z, 1)
            dve.wait_ge(s_z, 4)
            tt(z_sb[:], z_sb[:], cp, ALU.mult).then_inc(s_z, 1)
            nc.vector.reciprocal(z_sum[:], z_sum[:]).then_inc(s_z, 1)
            dve.wait_ge(s_z, 6)
            nc.vector.tensor_reduce(c_num[:], z_sb[:], AX_X, ALU.add).then_inc(s_z, 1)
            dve.wait_ge(s_z, 7)
            tt(c_sb[:], c_num[:], z_sum[:], ALU.mult).then_inc(s_skv, 1)
            dve.wait_ge(s_skv_mm, 1)
            nc.vector.tensor_copy(skv_t[:], ps_o[0:BATCH, 0:P]).then_inc(s_z, 1)
            dve.wait_ge(s_z, 8)
            tt(skv_sq[:], skv_t[:], skv_t[:], ALU.mult).then_inc(s_z, 1)
            dve.wait_ge(s_z, 9)
            nc.vector.tensor_reduce(skv_ss[:], skv_sq[:], AX_X, ALU.add).then_inc(s_skv_ss, 1)
            dve.wait_ge(s_skv_r, 1)
            nc.vector.scalar_tensor_tensor(skv_t[:], skv_t[:], skv_r[:, 0:1], knw_sb[0:BATCH, :],
                                           ALU.mult, ALU.mult).then_inc(s_skv, 1)
            dve.wait_ge(s_skv_mm, 2)
            nc.vector.tensor_copy(skvT[:], ps_o[:, 0:BATCH]).then_inc(s_skv, 1)
            dve.wait_ge(s_skv_mm, 3)
            nc.vector.tensor_copy(sg_sb[:], ps_o[0:BATCH, 0:HID]).then_inc(s_skv, 1)
            dve.wait_ge(s_skv_mm, 4)
            nc.vector.tensor_copy(sgT[:], ps_o[:, 0:KH * BATCH].rearrange("p (k b) -> p k b", k=KH)) \
                .then_inc(s_skv, 1)
            dve.wait_ge(s_skv_mm, 5)
            nc.vector.tensor_copy(sgf[:], ps_o[0:BATCH, 0:HID]).then_inc(s_const, 1)

            def rope(u):
                dve.wait_ge(s_qs, u + 1)
                if u >= 2:
                    dve.wait_ge(s_rot, u - 1)
                q = qs[:, u % 2]
                tt(q_a[:, u % 2], q[:, :, 0:ROT], bc(cos_sb[:].unsqueeze(1), [P, HALF, ROT]), ALU.mult)
                tt(q_b[:, u % 2, :, 0:h], q[:, :, h:ROT], bc(sin_sb[:, 0:h].unsqueeze(1), [P, HALF, h]), ALU.mult)
                dve.wait_ge(s_q_sq, u + 1)
                tt(q_b[:, u % 2, :, h:ROT], q[:, :, 0:h], bc(sin_sb[:, h:ROT].unsqueeze(1), [P, HALF, h]),
                   ALU.mult).then_inc(s_rope, 1)
                if u >= 2:
                    dve.wait_ge(s_q_r, u - 1)
                nc.vector.tensor_reduce(q_ss[:, u % 2], q_sq[:, u % 2], AX_X, ALU.add).then_inc(s_q_ss, 1)

            def scale(u):
                dve.wait_ge(s_s_mm, u + 1)
                dve.wait_ge(s_q_r, u + 1)
                if u >= 2:
                    dve.wait_ge(s_pT_t, u - 1)
                sp_ = ps_s[:].rearrange("p (h b j) -> p h b j", b=2, j=SEQ)
                for b in range(2):
                    rows = slice(b * 64, b * 64 + 64)
                    tt(s_sb[rows, u % 2], sp_[rows, :, b], bc(q_r[rows, u % 2].unsqueeze(2), [64, HALF, SEQ]),
                       ALU.mult).then_inc(s_s1, 1)
                dve.wait_ge(s_mask, u + 1)
                if u >= 2:
                    dve.wait_ge(s_sub, 2 * (u - 1))
                nc.vector.tensor_reduce(m_sb[:, u % 2], s_sb[:, u % 2], AX_X, ALU.max).then_inc(s_mx, 1)
                dve.wait_ge(s_mx, u + 1)
                tt(m_sb[:, u % 2], m_sb[:, u % 2], sink_sb[:, (u % 2) * HALF:(u % 2 + 1) * HALF], ALU.max) \
                    .then_inc(s_max, 1)

            def sums(u):
                dve.wait_ge(s_exp, 2 * (u + 1))
                if u >= 2:
                    dve.wait_ge(s_norm, u - 1)
                nc.vector.tensor_reduce(l_sb[:, u % 2], s_sb[:, u % 2], AX_X, ALU.add).then_inc(s_l0, 1)
                dve.wait_ge(s_l0, 2 * u + 1)
                tt(l_sb[:, u % 2], l_sb[:, u % 2], sk_sb[:, u % 2], ALU.add).then_inc(s_l0, 1)
                dve.wait_ge(s_l0, 2 * u + 2)
                nc.vector.reciprocal(l_sb[:, u % 2], l_sb[:, u % 2]).then_inc(s_l, 1)

            def turn_o(t):
                dve.wait_ge(s_pv, 2 * (t + 1))
                if t >= 2:
                    dve.wait_ge(s_fin, t - 1)
                src = ps_o[:].rearrange("p (k a n) -> p k a n", k=KH, a=2)
                for b in range(2):
                    for a in range(2):
                        nc.vector.tensor_copy(oT[a * 64:a * 64 + 64, t % 2, :, b * 64:b * 64 + 64],
                                              src[b * 64:b * 64 + 64, :, a, b * 64:b * 64 + 64]).then_inc(s_oT, 1)

            def ln_a(t):
                p = t % 2
                dve.wait_ge(s_fin, t + 1)
                tt(x1p[:, p], ps_o[:, 0:HID], x_sb[:, t], ALU.add).then_inc(s_x1p, 1)
                dve.wait_ge(s_x1p, t + 1)
                nc.vector.bn_stats(st1[:, p], x1p[:, p]).then_inc(s_lnc, 1)
                dve.wait_ge(s_lnc, 4 * t + 1)
                nc.vector.bn_aggr(mv1[:, p], st1[:, p]).then_inc(s_ln1, 1)

            def ln_b(t):
                p = t % 2
                dve.wait_ge(s_rs1, t + 1)
                dve.wait_ge(s_ln1, t + 1)
                nc.vector.tensor_scalar(x1[:, p], x1p[:, p], mv1[:, p, 0:1], rs1[:, p:p + 1],
                                        ALU.subtract, ALU.mult).then_inc(s_lnc, 1)
                dve.wait_ge(s_lnc, 4 * t + 2)
                tt(x2p[:, p], x1[:, p], r1[:, t], ALU.mult).then_inc(s_lnc, 1)
                dve.wait_ge(s_lnc, 4 * t + 3)
                nc.vector.bn_stats(st2[:, p], x2p[:, p]).then_inc(s_lnc, 1)
                dve.wait_ge(s_lnc, 4 * t + 4)
                nc.vector.bn_aggr(mv2[:, p], st2[:, p]).then_inc(s_ln2, 1)

            def ln_c(t):
                p = t % 2
                dve.wait_ge(s_rs2, t + 1)
                dve.wait_ge(s_ln2, t + 1)
                if t >= 2:
                    dve.wait_ge(s_x2_t, t - 1)
                nc.vector.tensor_scalar(x2[:, p], x2p[:, p], mv2[:, p, 0:1], rs2[:, p:p + 1],
                                        ALU.subtract, ALU.mult).then_inc(s_x2, 1)

            def x2_lo(t):
                dve.wait_ge(s_x2hi, t + 1)
                dve.wait_ge(s_x2T, t + 1)
                tt(x2T_lo[:, :, tok(t)], x2T[:, :, tok(t)], x2T_hi[:, :, tok(t)].bitcast(F32), ALU.subtract) \
                    .then_inc(s_x2lo, 1)

            chain = [0]

            def link(i):
                chain[0] += 1
                i.then_inc(s_rt, 1)
                dve.wait_ge(s_rt, chain[0])

            def route_a(c, ps):
                dve.wait_ge(s_lg_t, c + 1)
                nc.vector.tensor_copy(lg[:], ps[:, 0:TPC * GATES].rearrange("p (t g) -> p t g", g=GATES)) \
                    .then_inc(s_lg, 1)
                dve.wait_ge(s_lg, c + 1)
                link(nc.vector.tensor_reduce(lmax[:], lg[:, :, 0:EXPERTS], AX_X, ALU.max))
                tt(lg[:, :, 0:EXPERTS], lg[:, :, 0:EXPERTS], bc(lmax[:].unsqueeze(2), [P, TPC, EXPERTS]),
                   ALU.subtract)
                nc.vector.tensor_scalar(lg[:, :, EXPERTS:], lg[:, :, EXPERTS:], -1.0, None, ALU.mult) \
                    .then_inc(s_lsub, 1)

            def route_b(c):
                dve.wait_ge(s_lexp, c + 1)
                for t in range(TPC):
                    i = nc.vector.max(top[:, t], ex[:, t, 0:EXPERTS])
                link(i)
                for t in range(TPC):
                    i = nc.vector.max_index(topi[:, t], top[:, t], ex[:, t, 0:EXPERTS])
                link(i)
                link(nc.vector.tensor_copy(topf[:], topi[:, :, 0:2]))
                for r in range(2):
                    i = tt(pick[:, r], bc(iota_sb[:].unsqueeze(1), [P, TPC, EXPERTS]),
                           bc(topf[:, :, r:r + 1], [P, TPC, EXPERTS]), ALU.is_equal)
                link(i)
                link(tt(pick[:, 0], pick[:, 0], pick[:, 1], ALU.add))
                link(tt(pick[:, 0], pick[:, 0], ex[:, :, 0:EXPERTS], ALU.mult))
                link(nc.vector.tensor_reduce(den[:], pick[:, 0], AX_X, ALU.add))
                link(nc.vector.reciprocal(den[:], den[:]))
                tt(cw[:, :, 0:EXPERTS], pick[:, 0], bc(den[:].unsqueeze(2), [P, TPC, EXPERTS]), ALU.mult)
                link(nc.vector.tensor_scalar(ex[:, :, EXPERTS:], ex[:, :, EXPERTS:], 1.0, None, ALU.add))
                link(nc.vector.reciprocal(cw[:, :, EXPERTS:], ex[:, :, EXPERTS:]))
                if c:
                    dve.wait_ge(s_c_t, c)
                link(nc.vector.tensor_copy(cparts[:, :, 0], cw[:]))
                link(tt(cres[:, 0], cw[:], cparts[:, :, 0], ALU.subtract))
                link(nc.vector.tensor_copy(cparts[:, :, 1], cres[:, 0]))
                link(tt(cres[:, 1], cres[:, 0], cparts[:, :, 1], ALU.subtract))
                nc.vector.tensor_copy(cparts[:, :, 2], cres[:, 1]).then_inc(s_cw, 1)

            dve.wait_ge(ld["mask"], 32)
            dve.wait_ge(ld["x"], 16)
            dve.wait_ge(s_r1, 2)
            rope(0)
            for n in range(UNITS + 1):
                if n >= 1:
                    sums(n - 1)
                if n >= 3 and n % 2 == 1:
                    turn_o((n - 3) // 2)
                if n >= 5 and n % 2 == 1:
                    ln_c((n - 5) // 2)
                if n == 14:
                    route_a(0, ps_q)
                if n + 1 < UNITS:
                    rope(n + 1)
                if n >= 4 and n % 2 == 0:
                    ln_b((n - 4) // 2)
                if n < UNITS:
                    scale(n)
                if n >= 3 and n % 2 == 1:
                    ln_a((n - 3) // 2)
                if n >= 6 and n % 2 == 0:
                    x2_lo((n - 6) // 2)
                if n == 15:
                    dve.wait_ge(ld["route"], 32)
                    route_b(0)
            turn_o(7)

            def y_evac(c):
                dve.wait_ge(s_dn, FT * (c + 1))
                if c:
                    dve.wait_ge(s_y_t, TPC)
                for k in range(KH):
                    tt(yT[:, k], ps_s[:, k * CHUNK:(k + 1) * CHUNK], x2T[:, k, c * CHUNK:(c + 1) * CHUNK],
                       ALU.add).then_inc(s_yT, 1)

            def ln_y_a(n):
                p = n % 2
                dve.wait_ge(s_y_t, n + 1)
                if n >= 2:
                    dve.wait_ge(s_yo, n - 1)
                nc.vector.tensor_copy(y_sb[:, p], ps_o[:, 0:HID]).then_inc(s_y, 1)
                dve.wait_ge(s_y, n + 1)
                nc.vector.bn_stats(st3[:, p], y_sb[:, p]).then_inc(s_y3, 1)
                dve.wait_ge(s_y3, n + 1)
                nc.vector.bn_aggr(mv3[:, p], st3[:, p]).then_inc(s_ln3, 1)

            def ln_y_b(n):
                p = n % 2
                dve.wait_ge(s_rs3, n + 1)
                dve.wait_ge(s_ln3, n + 1)
                nc.vector.tensor_scalar(y_out[:, n], y_sb[:, p], mv3[:, p, 0:1], rs3[:, p:p + 1],
                                        ALU.subtract, ALU.mult).then_inc(s_yo, 1)

            for j in range(NIT):
                dve.wait_ge(s_silu, j + 1)
                dve.wait_ge(s_cb, j + 1)
                tt(act_c[:, j % 2], act_g[:, j % 2], ps_p[:], ALU.mult).then_inc(s_gc, 1)
                dve.wait_ge(s_gc, j + 1)
                dve.wait_ge(s_u_mm, j + 1)
                if j >= 2:
                    dve.wait_ge(s_hhi, j - 1)
                tt(h_sb[:, j % 2], act_c[:, j % 2], ps_t[:, (j % 2) * CHUNK:(j % 2 + 1) * CHUNK], ALU.mult) \
                    .then_inc(s_h, 1)
                dve.wait_ge(s_hhi, j + 1)
                if j >= 2:
                    dve.wait_ge(s_dn, j - 1)
                tt(h_lo[:, j % 2], h_sb[:, j % 2], h_hi[:, j % 2].bitcast(F32), ALU.subtract).then_inc(s_hlo, 1)
                if j == 0:
                    ln_c(6)
                if j == 1:
                    ln_a(7)
                if j == 2:
                    ln_b(7)
                if j == 3:
                    ln_c(7)
                if j == 5:
                    x2_lo(6)
                if j == 7:
                    x2_lo(7)
                if j == 9:
                    route_a(1, ps_o)
                if j == 10:
                    route_b(1)
                if j == FT:
                    y_evac(0)
                if FT + 2 <= j < FT + 2 + TPC:
                    ln_y_a(j - FT - 2)
                if FT + 3 <= j < FT + 3 + TPC:
                    ln_y_b(j - FT - 3)
            y_evac(1)
            for t in range(TPC):
                ln_y_a(TPC + t)
                if t:
                    ln_y_b(TPC + t - 1)
            ln_y_b(TILES - 1)


def _constants(np):
    f = np.float32
    inv = (f(1.0) / f(10000.0) ** (np.arange(0, ROT, 2, dtype=f) / f(ROT))).astype(f)
    ang = (np.arange(SEQ, dtype=f)[:, None] * inv).astype(f)
    cos, sin = np.cos(ang).astype(f), np.sin(ang).astype(f)
    t = np.arange(TOK)
    rows = np.arange(FT * P)
    gate = np.where(rows < MOE_ROWS, rows // I_MOE, np.where(rows < MOE_ROWS + I_SH, EXPERTS, GATES))
    key, query = np.arange(SEQ)[None, :], (np.arange(P) % SEQ)[:, None]
    from concourse import mybir as _mybir
    return {
        "cosT": np.tile(np.concatenate([cos, cos], 1), (2, 1)),
        "sinT": np.tile(np.concatenate([-sin, sin], 1), (2, 1)),
        "mask": np.where(key <= query, 0.0, -1e30).astype(f),
        "ident": np.eye(P, dtype=f),
        "first": np.tile((t % SEQ != 0).astype(f), (P, 1)),
        "late": ((t[None, :] // SEQ == np.arange(BATCH)[:, None]) & (t[None, :] % SEQ >= BLK)).astype(f),
        "sel": np.tile(gate[None, :] == np.arange(GATES)[:, None], (3, 1)).astype(_mybir.dt.np(BF16)),
        "iota": np.tile(np.arange(EXPERTS, dtype=f), (P, 1)),
    }


def kernel(**inputs):
    import numpy as np
    import concourse.bacc as _bacc
    from concourse.bass_utils import run_bass_kernel_spmd as _run

    a = {k.replace("L0_", ""): np.asarray(v) for k, v in inputs.items()}
    x = a["x"].reshape(TOK, HID)

    def rep(v):
        return np.tile(v.reshape(1, -1), (P, 1))

    gw = a["attn_group_w"].reshape(GROUPS * 4, D, GDIM).transpose(1, 0, 2).reshape(D, HALF, 2, GDIM)
    gw = gw.transpose(0, 2, 1, 3).reshape(D, 2 * HALF * GDIM)
    fill = np.zeros((FT * P - MOE_ROWS - I_SH, HID), np.float32)
    w1, gu = a["ffn_w1"], a["ffn_shared_gate_up_w"]
    wg = np.concatenate([w1[:, :I_MOE].reshape(MOE_ROWS, HID), gu[:I_SH], fill])
    wu = np.concatenate([w1[:, I_MOE:].reshape(MOE_ROWS, HID), gu[I_SH:], fill])
    wd = np.concatenate([a["ffn_w2"].transpose(0, 2, 1).reshape(MOE_ROWS, HID), a["ffn_shared_down_w"].T, fill])
    up = np.stack([w.reshape(FT, P, KH, P).transpose(0, 3, 2, 1) for w in (wg, wu)], 3)
    wffn = np.concatenate([up.reshape(FT, P, KH * 2 * P), wd.reshape(FT, P, HID)], 2)
    data = {
        "x": x, "xT": x.T, "ctxT": a["ctx_2048"].reshape(TOK, HID).T,
        "w_qc": a["attn_w_qc"], "w_qup": a["attn_w_qup"], "w_kv": a["attn_w_kv_b"], "w_z": a["attn_w_z_b"],
        "biasT": a["attn_bias_b"].T, "w_k": a["attn_w_k"], "w_v": a["attn_w_v"],
        "knw": rep(a["attn_k_norm_w"]), "qnw": rep(a["attn_q_norm_w"]), "sink": rep(a["attn_sink_logit"]),
        "gw": gw, "fw": a["attn_final_w"], "decay": np.repeat(a["xattn_decay"].reshape(-1), HID // HEADS).reshape(KH, P).T,
        "gates": np.concatenate([a["ffn_gate_w"], a["ffn_shared_gate_w"]]).T, "wffn": wffn,
        **_constants(np),
    }
    nc = _bacc.Bacc("TRN2", target_bir_lowering=False, num_devices=1)
    arrays, args = {}, {}
    for name, v in data.items():
        v = np.ascontiguousarray(v)
        arrays[name + "_in"] = v
        args[name] = nc.dram_tensor(name + "_in", v.shape, mybir.dt.from_np(v.dtype), kind="ExternalInput").ap()
    out = nc.dram_tensor("out_dram", (TOK, HID), F32, kind="ExternalOutput").ap()
    build(nc, out=out, **args)
    r = _run(nc, [arrays], core_ids=[0])
    return r.results[0]["out_dram"].reshape(BATCH, SEQ, HID)
```

```python
from contextlib import ExitStack

import concourse.bass as bass
from concourse import mybir

F32 = mybir.dt.float32
F32R = mybir.dt.float32r
BF16 = mybir.dt.bfloat16
U32 = mybir.dt.uint32
ALU = mybir.AluOpType
ACT = mybir.ActivationFunctionType
AX_X = mybir.AxisListType.X

P = 128
BATCH, SEQ, HID = 16, 64, 256
TOK = BATCH * SEQ
TILES = TOK // P
KH = HID // P
HEADS, D, ROT = 16, 128, 64
HALF = HEADS // 2
UNITS = 2 * TILES
GROUPS, GDIM = 4, 64
BLK = 32
EXPERTS, I_MOE, I_SH = 8, 176, 704
MOE_ROWS = EXPERTS * I_MOE
FT = -(-(MOE_ROWS + I_SH) // P)
GATES = EXPERTS + 1
CHUNK = 512
TPC = CHUNK // P
LAG = 2
WB = 4
RMS_EPS = 1e-6
LN_EPS = 1e-5
SCALE = float(D) ** -0.5


def build(nc, x, xT, ctxT, w_qc, w_qup, w_kv, w_z, biasT, w_k, w_v, knw, qnw, sink, gw, fw, decay,
          gates, wffn, cosT, sinT, mask, ident, late, sel, iota, out):
    with ExitStack() as ctx:
        def sb(name, shape, dt=F32):
            return ctx.enter_context(nc.sbuf_tensor(name, shape, dt))

        def psum(name, shape, dt=F32):
            return ctx.enter_context(nc.psum_tensor(name, shape, dt))

        def sem(name):
            return ctx.enter_context(nc.semaphore(name))

        ps_q = psum("ps_q", [P, 1024])
        ps_t = psum("ps_t", [P, 1024])
        ps_s = psum("ps_s", [P, 1024])
        ps_p = psum("ps_p", [P, 512])
        ps_o = psum("ps_o", [P, 512])

        x_sb = sb("x_sb", [P, TILES, HID])
        xT_sb = sb("xT_sb", [P, KH, TOK])
        ctx_sb = sb("ctx_sb", [P, KH, TOK])
        wqc_sb = sb("wqc_sb", [P, KH, P])
        wk_sb = sb("wk_sb", [P, KH, D])
        wv_sb = sb("wv_sb", [P, KH, D])
        wkv_sb = sb("wkv_sb", [P, KH, D])
        wz_sb = sb("wz_sb", [P, KH, D])
        w_raws = sb("w_raws", [P, WB * 3 * HID])
        wqup_sb = w_raws[:, 0:HEADS * D]
        vg_tok = sb("vg_tok", [P, 2, 2, HALF, GDIM])
        gw_sb = vg_tok[:, 1]
        fw_sb = sb("fw_sb", [P, KH, HID])
        bias_sb = sb("bias_sb", [P, BLK])
        knw_sb = sb("knw_sb", [P, D])
        qnw_sb = sb("qnw_sb", [P, D])
        sink_sb = sb("sink_sb", [P, HEADS])
        decay_sb = sb("decay_sb", [P, KH])
        gates_sb = sb("gates_sb", [P, KH, GATES])
        cos_sb = sb("cos_sb", [P, ROT])
        sin_sb = sb("sin_sb", [P, ROT])
        mask_sb = sb("mask_sb", [P, 4 * P], BF16)
        id_sb = sb("id_sb", [P, P])
        idb_sb = sb("idb_sb", [P, P], BF16)
        first_sb = sb("first_sb", [P, TOK])
        late_sb = sb("late_sb", [BATCH, TOK])
        sel_sb = sb("sel_sb", [3 * GATES, FT * P], BF16)
        iota_sb = sb("iota_sb", [P, EXPERTS])
        nhalf = sb("nhalf", [P, 16])

        whi_buf = sb("whi_buf", [P, WB * 3 * HID], F32R)
        wlo_buf = sb("wlo_buf", [P, WB * 3 * HID], F32R)
        wqup_hi, wqup_lo = whi_buf[:, 0:HEADS * D], wlo_buf[:, 0:HEADS * D]
        gw_hi = sb("gw_hi", [P, 2, HALF, GDIM], F32R)
        gw_lo = sb("gw_lo", [P, 2, HALF, GDIM], F32R)
        qc_hi = sb("qc_hi", [P, TOK], F32R)
        qc_lo = sb("qc_lo", [P, TOK], F32R)
        v_hi = sb("v_hi", [P, TOK], F32R)
        v_lo = sb("v_lo", [P, TOK], F32R)

        q_sq = sb("q_sq", [P, 2, HALF, D])
        qs = sb("qs", [P, 2, HALF, D])
        s_sb = sb("s_sb", [P, 2, HALF, SEQ])
        junk = sb("junk", [P, 2, D])
        k_ss = sb("k_ss", [P, TILES])
        k_r = sb("k_r", [P, TILES])
        k_n = s_sb[:].rearrange("p u h j -> p (u h j)").rearrange("p (t d) -> p t d", d=D)
        k_a = q_sq[:, 1].rearrange("p h d -> p (h d)")[:, 0:TILES * ROT].rearrange("p (t d) -> p t d", d=ROT)
        k_b = q_sq[:, 1].rearrange("p h d -> p (h d)")[:, TILES * ROT:].rearrange("p (t d) -> p t d", d=ROT)
        kT = sb("kT", [P, TOK])

        z_sb = sb("z_sb", [P, BATCH, BLK])
        z_max = sb("z_max", [P, BATCH])
        z_sum = sb("z_sum", [P, BATCH])
        c_num = sb("c_num", [P, BATCH])
        c_sb = sb("c_sb", [P, BATCH])
        skv_t = sb("skv_t", [BATCH, D])
        skv_sq = sb("skv_sq", [BATCH, D])
        skv_ss = sb("skv_ss", [BATCH, 1])
        skv_r = sb("skv_r", [BATCH, 1])
        skvT = sb("skvT", [P, BATCH])
        sg_sb = sb("sg_sb", [BATCH, HID])
        sgT = sb("sgT", [P, KH, BATCH])
        sgf = sb("sgf", [BATCH, HID])

        kvx = ctx_sb
        dk = sb("dk", [P, KH, TOK])
        rT = q_sq[:].rearrange("p u h d -> p u (h d)")
        r1 = sb("r1", [P, TILES, HID])

        q_a = sb("q_a", [P, 2, HALF, ROT])
        q_b = sb("q_b", [P, 2, HALF, ROT])
        q_ss = sb("q_ss", [P, 2, HALF])
        q_r = sb("q_r", [P, 2, HALF])
        qT = xT_sb
        m_sb = sb("m_sb", [P, 2, HALF])
        sk_sb = sb("sk_sb", [P, 2, HALF])
        l_sb = sb("l_sb", [P, 2, HALF])
        pT = first_sb[:].rearrange("p (u n) -> p u n", u=2)
        vg = sb("vg", [P, 2, HALF, 2, GDIM])
        oT = sb("oT", [P, 2, KH, P])

        x1p = sb("x1p", [P, 2, HID])
        x1 = sb("x1", [P, 2, HID])
        x2p = sb("x2p", [P, 2, HID])
        x2 = sb("x2", [P, 2, HID])
        st1 = sb("st1", [P, 2, 6])
        mv1 = sb("mv1", [P, 2, 2])
        st2 = sb("st2", [P, 2, 6])
        mv2 = sb("mv2", [P, 2, 2])
        rs1 = sb("rs1", [P, 2])
        rs2 = sb("rs2", [P, 2])
        x2T = ctx_sb
        x2T_hi = sb("x2T_hi", [P, KH, TOK], F32R)
        x2T_lo = sb("x2T_lo", [P, KH, TOK], F32R)

        lgT = sb("lgT", [GATES, CHUNK])
        lg = sb("lg", [P, TPC, GATES])
        lmax = sb("lmax", [P, TPC])
        ex = sb("ex", [P, TPC, GATES])
        top = sb("top", [P, TPC, 8])
        topi = sb("topi", [P, TPC, 8], U32)
        topf = sb("topf", [P, TPC, 2])
        pick = sb("pick", [P, 2, TPC, EXPERTS])
        den = sb("den", [P, TPC])
        cw = sb("cw", [P, TPC, GATES])
        cres = sb("cres", [P, 2, TPC, GATES])
        cparts = sb("cparts", [P, TPC, 3, GATES], BF16)
        cT = z_sb[0:3 * GATES].rearrange("p b m -> p (b m)").bitcast(BF16).rearrange("p (c n) -> p c n", c=2)

        w_raw = w_raws[:].rearrange("p (b n) -> p b n", b=WB)
        w_hi = whi_buf[:].rearrange("p (b n) -> p b n", b=WB)
        w_lo = wlo_buf[:].rearrange("p (b n) -> p b n", b=WB)
        act_g = q_a[:].rearrange("p u h d -> p u (h d)")
        act_c = q_b[:].rearrange("p u h d -> p u (h d)")
        h_sb = s_sb[:].rearrange("p u h j -> p u (h j)")
        h_hi = qc_hi[:].rearrange("p (u n) -> p u n", u=2)
        h_lo = qc_lo[:].rearrange("p (u n) -> p u n", u=2)
        yT = xT_sb[:, :, 0:CHUNK]
        y_sb = x1p
        st3 = sb("st3", [P, 2, 6])
        mv3 = sb("mv3", [P, 2, 2])
        rs3 = sb("rs3", [P, 2])
        y_out = qs[:].rearrange("p u h d -> p (u h d)").rearrange("p (t n) -> p t n", n=HID)

        ld = {n: sem("ld_" + n) for n in ("xT", "wqc", "wk", "wv", "wc", "gw", "fw", "x", "norm", "rope",
                                           "mask", "id", "ctx", "decay", "late", "gates", "route", "bias")}
        ld_wqup = [sem("ld_wqup0"), sem("ld_wqup1")]
        ld_w = [sem(f"ld_w{i}") for i in range(WB)]
        s_const = sem("s_const")
        s_qc_mm, s_v_mm, s_k_mm, s_c_mm = sem("s_qc_mm"), sem("s_v_mm"), sem("s_k_mm"), sem("s_c_mm")
        s_qc_hi, s_qc_lo, s_v_hi, s_v_lo = sem("s_qc_hi"), sem("s_qc_lo"), sem("s_v_hi"), sem("s_v_lo")
        s_wqup_hi, s_gw_hi, s_gw_lo = sem("s_wqup_hi"), sem("s_gw_hi"), sem("s_gw_lo")
        s_k_sq, s_k_ss, s_k_r, s_k_dve, s_k_t, s_kT = (sem("s_k_sq"), sem("s_k_ss"), sem("s_k_r"), sem("s_k_dve"),
                                                      sem("s_k_t"), sem("s_kT"))
        s_z, s_z_exp, s_c_act, s_skv_r, s_skv_mm = (sem("s_z"), sem("s_z_exp"), sem("s_c_act"),
                                                   sem("s_skv_r"), sem("s_skv_mm"))
        s_skv = sem("s_skv")
        s_kvx, s_scan, s_r_t, s_r1 = sem("s_kvx"), sem("s_scan"), sem("s_r_t"), sem("s_r1")
        s_q_mm, s_qs, s_q_sq, s_rope, s_q_ss, s_q_r = (sem("s_q_mm"), sem("s_qs"), sem("s_q_sq"), sem("s_rope"),
                                                      sem("s_q_ss"), sem("s_q_r"))
        s_rot, s_qT_t, s_qT, s_s_mm, s_s1, s_mask, s_max, s_sub = (sem("s_rot"), sem("s_qT_t"), sem("s_qT"),
                                                                  sem("s_s_mm"), sem("s_s1"), sem("s_mask"),
                                                                  sem("s_max"), sem("s_sub"))
        s_exp, s_l, s_norm, s_pT_t, s_pT, s_pv = (sem("s_exp"), sem("s_l"), sem("s_norm"), sem("s_pT_t"),
                                                 sem("s_pT"), sem("s_pv"))
        s_vg_mm, s_vg_tok = sem("s_vg_mm"), sem("s_vg_tok")
        s_vg = [sem("s_vg0"), sem("s_vg1")]
        s_oT, s_fin = sem("s_oT"), sem("s_fin")
        s_x1p, s_ln1, s_rs1, s_ln2, s_rs2, s_x2, s_x2_t, s_x2T, s_x2hi, s_x2lo = (
            sem("s_x1p"), sem("s_ln1"), sem("s_rs1"), sem("s_ln2"), sem("s_rs2"), sem("s_x2"), sem("s_x2_t"),
            sem("s_x2T"), sem("s_x2hi"), sem("s_x2lo"))
        s_lnc = sem("s_lnc")
        s_wqup_lo0, s_wqup_lo1 = sem("s_wqup_lo0"), sem("s_wqup_lo1")
        s_first, s_idb = sem("s_first"), sem("s_idb")
        s_pool, s_scan_in, s_skv_ss, s_mx, s_l0 = (sem("s_pool"), sem("s_scan_in"), sem("s_skv_ss"), sem("s_mx"),
                                                  sem("s_l0"))
        s_lg_mm, s_lgT, s_lg_t, s_lg, s_lsub, s_lexp, s_rt, s_cw, s_c_t, s_cT = (
            sem("s_lg_mm"), sem("s_lgT"), sem("s_lg_t"), sem("s_lg"), sem("s_lsub"), sem("s_lexp"), sem("s_rt"),
            sem("s_cw"), sem("s_c_t"), sem("s_cT"))
        s_whi, s_wlo, s_g_mm, s_u_mm, s_cb, s_silu, s_gc, s_h, s_hhi, s_hlo, s_dn = (
            sem("s_whi"), sem("s_wlo"), sem("s_g_mm"), sem("s_u_mm"), sem("s_cb"), sem("s_silu"), sem("s_gc"),
            sem("s_h"), sem("s_hhi"), sem("s_hlo"), sem("s_dn"))
        s_y3 = sem("s_y3")
        s_yT, s_y_t, s_y, s_ln3, s_rs3, s_yo, s_st = (sem("s_yT"), sem("s_y_t"), sem("s_y"), sem("s_ln3"),
                                                     sem("s_rs3"), sem("s_yo"), sem("s_st"))

        NIT = 2 * FT
        X2_LATE = {2: 5, 3: 6, 6: 7}

        def bc(ap, shape):
            return ap.to_broadcast(shape)

        def tok(t):
            return slice(t * P, (t + 1) * P)

        block = ctx.enter_context(nc.Block())

        @block.sync
        def _(sp):
            def load(dst, src, s):
                sp.dma_start(dst, src).then_inc(s, 16)

            def store(t):
                sp.wait_ge(s_yo, t + 1)
                sp.dma_start(out[tok(t)], y_out[:, t]).then_inc(s_st, 16)

            load(wqc_sb[:], w_qc.rearrange("(k p) n -> p k n", p=P), ld["wqc"])
            load(xT_sb[:], xT.rearrange("(k p) n -> p k n", p=P), ld["xT"])
            load(wk_sb[:], w_k.rearrange("(k p) n -> p k n", p=P), ld["wk"])
            for i in range(2):
                load(wqup_sb[:, i * 1024:(i + 1) * 1024], w_qup[:, i * 1024:(i + 1) * 1024], ld_wqup[i])
            load(wkv_sb[:], w_kv.rearrange("(k p) n -> p k n", p=P), ld["wc"])
            load(wz_sb[:], w_z.rearrange("(k p) n -> p k n", p=P), ld["wc"])
            load(wv_sb[:], w_v.rearrange("(k p) n -> p k n", p=P), ld["wv"])
            load(ctx_sb[:], ctxT.rearrange("(k p) n -> p k n", p=P), ld["ctx"])
            load(gw_sb[:], gw.rearrange("p (a h o) -> p a h o", a=2, h=HALF), ld["gw"])
            load(fw_sb[:], fw.rearrange("(k p) n -> p k n", p=P), ld["fw"])
            load(x_sb[:], x.rearrange("(t p) n -> p t n", p=P), ld["x"])
            load(late_sb[:], late, ld["late"])
            load(gates_sb[:], gates.rearrange("(k p) n -> p k n", p=P), ld["gates"])
            load(sel_sb[:], sel, ld["route"])
            load(iota_sb[:], iota, ld["route"])
            for t in range(TILES):
                sp.wait_ge(s_vg_tok, t + 1)
                if t >= 2:
                    sp.wait_ge(s_pv, 2 * (t - 1))
                for b in range(2):
                    for par in range(2):
                        sp.dma_start(vg[par * 64:par * 64 + 64, t % 2, :, b], vg_tok[b * 64:b * 64 + 64, t % 2, par]) \
                          .then_inc(s_vg[t % 2], 16)
            sp.wait_ge(s_wqup_hi, 2)
            sp.wait_ge(s_wqup_lo0, 1)
            sp.wait_ge(s_wqup_lo1, 1)
            for j in range(NIT):
                if j >= WB:
                    sp.wait_ge(s_whi, j - WB + 1)
                    sp.wait_ge(s_wlo, j - WB + 1)
                load(w_raw[:, j % WB], wffn[j % FT], ld_w[j % WB])
                if FT + 10 <= j < FT + 10 + TPC:
                    store(j - FT - 10)
            for t in range(TPC, TILES):
                store(t)
            sp.wait_ge(s_st, 16 * TILES)

        @block.scalar
        def _(act):
            def load(dst, src, s):
                act.dma_start(dst, src).then_inc(s, 16)

            load(id_sb[:], ident, ld["id"])
            load(cos_sb[:], cosT, ld["rope"])
            load(sin_sb[:], sinT, ld["rope"])
            load(knw_sb[:], knw, ld["norm"])
            load(qnw_sb[:], qnw, ld["norm"])
            load(decay_sb[:], decay, ld["decay"])
            load(mask_sb[:], mask, ld["mask"])
            load(sink_sb[:], sink, ld["mask"])
            load(bias_sb[:], biasT, ld["bias"])

            def wqup_half(i):
                cols = slice(i * 1024, (i + 1) * 1024)
                act.wait_ge(ld_wqup[i], 16)
                nc.scalar.copy(wqup_hi[:, cols], wqup_sb[:, cols]).then_inc(s_wqup_hi, 1)

            wqup_half(0)
            act.wait_ge(s_qc_mm, 1)
            nc.scalar.copy(qc_hi[:], ps_q[:]).then_inc(s_qc_hi, 1)
            act.wait_ge(ld["id"], 16)
            nc.scalar.copy(idb_sb[:], id_sb[:]).then_inc(s_idb, 1)
            act.wait_ge(s_k_mm, 1)
            for t in range(TILES):
                if t >= 2:
                    act.wait_ge(s_k_ss, t - 1)
                nc.scalar.activation(junk[:, t % 2], ps_s[:, t * D:(t + 1) * D], ACT.Square,
                                     accum_out=k_ss[:, t:t + 1]).then_inc(s_k_ss, 1)
            act.wait_ge(s_z, 3)
            nc.scalar.activation(z_sb[:], z_sb[:], ACT.Exp).then_inc(s_z_exp, 1)
            wqup_half(1)
            act.wait_ge(s_v_mm, 1)
            nc.scalar.copy(v_hi[:], ps_t[:]).then_inc(s_v_hi, 1)

            def evac_q(u):
                act.wait_ge(s_q_mm, u + 1)
                if u >= 2:
                    act.wait_ge(s_qT_t, u - 1)
                nc.scalar.copy(qs[:, u % 2], ps_q[:].rearrange("p (h d) -> p h d", d=D)).then_inc(s_qs, 1)

            def square_q(u):
                act.wait_ge(s_qs, u + 1)
                if u >= 2:
                    act.wait_ge(s_q_r, u - 1)
                for h in range(HALF):
                    c = TILES + HALF * u + h
                    act.wait_ge(s_k_ss if c < TILES + 2 else s_q_ss, c - 1 if c < TILES + 2 else c - 1 - TILES)
                    nc.scalar.activation(junk[:, c % 2], qs[:, u % 2, h], ACT.Square,
                                         accum_out=q_ss[:, u % 2, h:h + 1]).then_inc(s_q_ss, 1)

            def evac_qT(u):
                act.wait_ge(s_qT_t, u + 1)
                if u >= 2:
                    act.wait_ge(s_s_mm, u - 1)
                nc.scalar.copy(qT[:, u % 2], ps_t[:]).then_inc(s_qT, 1)

            def evac_r(i):
                k, half = i // 2, i % 2
                act.wait_ge(s_r_t, i + 1)
                nc.scalar.activation(r1[:, half * 4:half * 4 + 4, k * P:(k + 1) * P],
                                     ps_p[:].rearrange("p (t d) -> p t d", d=P), ACT.Identity,
                                     bias=1.0).then_inc(s_r1, 1)

            def exp(u):
                act.wait_ge(s_sub, 2 * (u + 1))
                nc.scalar.activation(sk_sb[:, u % 2], sk_sb[:, u % 2], ACT.Exp).then_inc(s_exp, 1)
                nc.scalar.activation(s_sb[:, u % 2], s_sb[:, u % 2], ACT.Exp).then_inc(s_exp, 1)

            def evac_pT(u):
                act.wait_ge(s_pT_t, u + 1)
                if u >= 2:
                    act.wait_ge(s_pv, u - 1)
                nc.scalar.copy(pT[:, u % 2], ps_p[:]).then_inc(s_pT, 1)

            def evac_vg(t):
                act.wait_ge(s_vg_mm, t + 1)
                if t >= 2:
                    act.wait_ge(s_vg[t % 2], 64 * (t // 2))
                nc.scalar.copy(vg_tok[:, t % 2], ps_t[:].rearrange("p (a h o) -> p a h o", a=2, o=GDIM)) \
                    .then_inc(s_vg_tok, 1)

            def evac_x2(t, ps):
                act.wait_ge(s_x2_t, t + 1)
                src = ps[:, 0:HID].rearrange("p (k n) -> p k n", k=KH)
                nc.scalar.copy(x2T[:, :, tok(t)], src).then_inc(s_x2T, 1)
                nc.scalar.copy(x2T_hi[:, :, tok(t)], src).then_inc(s_x2hi, 1)

            def route_copy(c, ps):
                act.wait_ge(s_lg_mm, c + 1)
                if c:
                    act.wait_ge(s_lg_t, c)
                nc.scalar.copy(lgT[:], ps[0:GATES, :]).then_inc(s_lgT, 1)

            def route_exp(c):
                act.wait_ge(s_lsub, c + 1)
                nc.scalar.activation(ex[:], lg[:], ACT.Exp).then_inc(s_lexp, 1)

            def route_cT(c, ps):
                act.wait_ge(s_c_t, c + 1)
                nc.scalar.copy(cT[:, c], ps[:].bitcast(BF16)[0:3 * GATES, 0:CHUNK]).then_inc(s_cT, 1)

            evac_q(0)
            square_q(0)
            act.wait_ge(ld["gw"], 16)
            nc.scalar.copy(gw_hi[:], gw_sb[:]).then_inc(s_gw_hi, 1)
            act.wait_ge(s_k_t, 1)
            nc.scalar.copy(kT[:], ps_s[:]).then_inc(s_kT, 1)
            act.wait_ge(ld["ctx"], 16)
            nc.scalar.activation(kvx[:], ctx_sb[:], ACT.Square).then_inc(s_kvx, 1)
            for n in range(UNITS):
                if n >= LAG:
                    evac_pT(n - LAG)
                evac_qT(n)
                if n >= 1:
                    exp(n - 1)
                if n == 15:
                    route_exp(0)
                if n + 1 < UNITS:
                    evac_q(n + 1)
                    square_q(n + 1)
                if n % 2 == 0:
                    evac_vg(n // 2)
                if n < 2:
                    evac_r(2 * n)
                    evac_r(2 * n + 1)
                if n >= 6 and n % 2 == 0:
                    evac_x2((n - 6) // 2, ps_p)
                if n == 13:
                    route_copy(0, ps_p)

            def split_w(j):
                act.wait_ge(ld_w[j % WB], 16 * (j // WB + 1))
                if j >= WB:
                    act.wait_ge(s_dn, j - WB + 1)
                nc.scalar.copy(w_hi[:, j % WB], w_raw[:, j % WB]).then_inc(s_whi, 1)

            for j in range(WB - 1):
                split_w(j)
            exp(UNITS - 1)
            route_cT(0, ps_q)
            for j in range(NIT):
                if j >= 2:
                    act.wait_ge(s_gc, j - 1)
                act.wait_ge(s_g_mm, j + 1)
                nc.scalar.activation(act_g[:, j % 2], ps_q[:, (j % 2) * CHUNK:(j % 2 + 1) * CHUNK], ACT.Silu) \
                    .then_inc(s_silu, 1)
                if j >= 1 and j + WB - 2 < NIT:
                    split_w(j + WB - 2)
                act.wait_ge(s_h, j + 1)
                if j >= 2:
                    act.wait_ge(s_dn, j - 1)
                nc.scalar.copy(h_hi[:, j % 2], h_sb[:, j % 2]).then_inc(s_hhi, 1)
                if j < LAG:
                    evac_pT(UNITS - LAG + j)
                if j in X2_LATE:
                    evac_x2(X2_LATE[j], ps_o)
                if j == 8:
                    route_copy(1, ps_o)
                if j == 9:
                    route_exp(1)
                if j == 12:
                    route_cT(1, ps_o)

        @block.tensor
        def _(pe):
            mm = nc.tensor.matmul

            def three(dst, w, a, first_, last_):
                (wh, wl), (ah, al) = w, a
                mm(dst, wh, ah, start=first_, stop=False)
                mm(dst, wl, ah, start=False, stop=False)
                return mm(dst, wh, al, start=False, stop=last_)

            pe.wait_ge(ld["xT"], 16)
            pe.wait_ge(ld["wqc"], 16)
            for c in range(2):
                for k in range(KH):
                    i = mm(ps_q[:, c * 512:(c + 1) * 512], wqc_sb[:, k], xT_sb[:, k, c * 512:(c + 1) * 512],
                           start=k == 0, stop=k == KH - 1)
            i.then_inc(s_qc_mm, 1)
            pe.wait_ge(ld["wk"], 16)
            for t in range(TILES):
                for k in range(KH):
                    i = mm(ps_s[:, tok(t)], xT_sb[:, k, tok(t)], wk_sb[:, k], start=k == 0, stop=k == KH - 1)
            i.then_inc(s_k_mm, 1)
            pe.wait_ge(ld["wc"], 32)
            for w, ps in ((wz_sb, ps_o), (wkv_sb, ps_p)):
                for k in range(KH):
                    blk = xT_sb[:, k].rearrange("p (b s) -> p b s", s=SEQ)[:, :, 0:BLK]
                    i = mm(ps[:], w[:, k], blk, start=k == 0, stop=k == KH - 1)
                i.then_inc(s_c_mm, 1)
            pe.wait_ge(ld["wv"], 16)
            for c in range(2):
                for k in range(KH):
                    i = mm(ps_t[:, c * 512:(c + 1) * 512], wv_sb[:, k], xT_sb[:, k, c * 512:(c + 1) * 512],
                           start=k == 0, stop=k == KH - 1)
            i.then_inc(s_v_mm, 1)

            def keys_turn():
                pe.wait_ge(ld["id"], 16)
                pe.wait_ge(s_k_dve, 7)
                for t in range(TILES):
                    i = nc.tensor.transpose(ps_s[:, tok(t)], k_n[:, t], id_sb[:])
                i.then_inc(s_k_t, 1)

            def scan_turn(i):
                k, half = i // 2, i % 2
                pe.wait_ge(s_scan, k + 1)
                if i:
                    pe.wait_ge(s_r1, i)
                else:
                    pe.wait_ge(s_z, 5)
                for t in range(4):
                    j = nc.tensor.transpose(ps_p[:, tok(t)], rT[:, k, tok(half * 4 + t)], id_sb[:])
                j.then_inc(s_r_t, 1)

            def block_step(i):
                pe.wait_ge(s_skv, i + 1)
                if i == 0:
                    j = nc.tensor.transpose(ps_o[0:BATCH, 0:P], c_sb[:], id_sb[:])
                if i == 1:
                    j = nc.tensor.transpose(ps_o[:, 0:BATCH], skv_t[:], id_sb[0:BATCH, 0:BATCH])
                if i == 2:
                    pe.wait_ge(ld["gw"], 16)
                    for h in range(4):
                        gwh = gw_sb[:, h % 2].rearrange("p (g c) o -> p g c o", c=2)[:, :, h // 2]
                        j = mm(ps_o[0:BATCH, 0:HID], skvT[:], gwh, start=h == 0, stop=h == 3)
                if i == 3:
                    for k in range(KH):
                        j = nc.tensor.transpose(ps_o[:, k * BATCH:(k + 1) * BATCH], sg_sb[:, k * P:(k + 1) * P],
                                                id_sb[0:BATCH, 0:BATCH])
                if i == 4:
                    pe.wait_ge(ld["fw"], 16)
                    for k in range(KH):
                        j = mm(ps_o[0:BATCH, 0:HID], sgT[:, k], fw_sb[:, k], start=k == 0, stop=k == KH - 1)
                j.then_inc(s_skv_mm, 1)

            def q_mm(u):
                t, hf = u // 2, u % 2
                pe.wait_ge(s_wqup_hi, hf + 1)
                pe.wait_ge((s_wqup_lo0, s_wqup_lo1)[hf], 1)
                if u >= 1:
                    pe.wait_ge(s_qs, u)
                else:
                    pe.wait_ge(s_qc_hi, 1)
                    pe.wait_ge(s_qc_lo, 1)
                for c in range(2):
                    cols = slice(hf * 1024 + c * 512, hf * 1024 + (c + 1) * 512)
                    i = three(ps_q[:, c * 512:(c + 1) * 512], (qc_hi[:, tok(t)], qc_lo[:, tok(t)]),
                              (wqup_hi[:, cols], wqup_lo[:, cols]), True, True)
                i.then_inc(s_q_mm, 1)

            def q_turn(u):
                pe.wait_ge(s_rot, u + 1)
                if u % 2 == 1:
                    pe.wait_ge(s_vg_tok, u // 2 + 1)
                if u >= 1:
                    pe.wait_ge(s_qT, u)
                else:
                    pe.wait_ge(s_v_hi, 1)
                    pe.wait_ge(s_v_lo, 1)
                for h in range(HALF):
                    i = nc.tensor.transpose(ps_t[:, h * P:(h + 1) * P], qs[:, u % 2, h], id_sb[:])
                i.then_inc(s_qT_t, 1)

            def scores(u):
                pe.wait_ge(s_qT, u + 1)
                if u >= 1:
                    pe.wait_ge(s_s1, 2 * u)
                else:
                    pe.wait_ge(s_kT, 1)
                    pe.wait_ge(s_idb, 1)
                    pe.wait_ge(ld["mask"], 32)
                for b in range(2):
                    mm(ps_s[:, b * 512:(b + 1) * 512], idb_sb[:], mask_sb[:], start=True, stop=False,
                       skip_group_check=True)
                    for h in range(4 * b, 4 * b + 4):
                        i = mm(ps_s[:, h * P:(h + 1) * P], qT[:, u % 2, h * P:(h + 1) * P], kT[:, tok(u // 2)],
                               start=False, stop=h == 4 * b + 3, skip_group_check=True)
                i.then_inc(s_s_mm, 1)

            def p_turn(u):
                if u == 0:
                    pe.wait_ge(s_r1, 4)
                pe.wait_ge(s_norm, u + 1)
                for p in range(4):
                    i = nc.tensor.transpose(ps_p[:, p * P:(p + 1) * P],
                                            s_sb[:, u % 2, 2 * p:2 * p + 2].rearrange("p a j -> p (a j)"), id_sb[:])
                i.then_inc(s_pT_t, 1)

            def pv(u):
                t, hf = u // 2, u % 2
                pe.wait_ge(s_pT, u + 1)
                if u == 0:
                    pe.wait_ge(s_r1, 4)
                    pe.wait_ge(s_const, 1)
                if hf == 0:
                    pe.wait_ge(s_vg[t % 2], 64 * (t // 2 + 1))
                    if t:
                        pe.wait_ge(s_x1p, t)
                for g in range(2):
                    for p in range(2):
                        i = mm(ps_o[:, (2 * hf + g) * P:(2 * hf + g + 1) * P], vg[:, t % 2, 4 * hf + 2 * g + p].rearrange("p b o -> p (b o)"),
                               pT[:, u % 2, (2 * g + p) * P:(2 * g + p + 1) * P], start=p == 0, stop=p == 1)
                i.then_inc(s_pv, 1)

            def vg_mm(t):
                pe.wait_ge(s_qT, 2 * t + 1)
                if t == 0:
                    pe.wait_ge(s_gw_hi, 1)
                    pe.wait_ge(s_gw_lo, 1)
                for a in range(2):
                    cols = (gw_hi[:, a], gw_lo[:, a])
                    i = three(ps_t[:, a * 512:(a + 1) * 512], (v_hi[:, tok(t)], v_lo[:, tok(t)]), cols, True, True)
                i.then_inc(s_vg_mm, 1)

            def final(t):
                pe.wait_ge(s_oT, 4 * (t + 1))
                for k in range(KH):
                    mm(ps_o[:, 0:HID], oT[:, t % 2, k], fw_sb[:, k], start=k == 0, stop=False)
                if t == 0:
                    pe.wait_ge(ld["late"], 16)
                mm(ps_o[:, 0:HID], late_sb[:, tok(t)], sgf[:], start=False, stop=True).then_inc(s_fin, 1)

            def x2_turn(t, ps):
                pe.wait_ge(s_x2, t + 1)
                for k in range(KH):
                    i = nc.tensor.transpose(ps[:, k * P:(k + 1) * P], x2[:, t % 2, k * P:(k + 1) * P], id_sb[:])
                i.then_inc(s_x2_t, 1)

            def logits(c, ps):
                pe.wait_ge(s_x2T, TPC * (c + 1))
                for k in range(KH):
                    i = mm(ps[0:GATES, :], gates_sb[:, k], x2T[:, k, c * CHUNK:(c + 1) * CHUNK],
                           start=k == 0, stop=k == KH - 1)
                i.then_inc(s_lg_mm, 1)

            def logits_turn(c, ps):
                pe.wait_ge(s_lgT, c + 1)
                for t in range(TPC):
                    i = nc.tensor.transpose(ps[:, t * GATES:(t + 1) * GATES], lgT[:, tok(t)],
                                            id_sb[0:GATES, 0:GATES])
                i.then_inc(s_lg_t, 1)

            def weights_turn(c, ps):
                pe.wait_ge(s_cw, c + 1)
                for t in range(TPC):
                    i = nc.tensor.transpose(ps[:].bitcast(BF16)[0:3 * GATES, tok(t)],
                                            cparts[:, t].rearrange("p a g -> p (a g)"), idb_sb[:])
                i.then_inc(s_c_t, 1)

            q_mm(0)
            keys_turn()
            for n in range(UNITS):
                if n == 2:
                    block_step(4)
                if n >= LAG:
                    if n >= 7 and n % 2 == 1:
                        pe.wait_ge(s_x2hi, (n - 7) // 2 + 1)
                    if n == 14:
                        pe.wait_ge(s_lgT, 1)
                    p_turn(n - LAG)
                q_turn(n)
                if n == 14:
                    pe.wait_ge(s_qs, n + 1)
                    logits_turn(0, ps_q)
                    pe.wait_ge(s_lg, 1)
                if n + 1 < UNITS:
                    q_mm(n + 1)
                if n >= LAG:
                    pv(n - LAG)
                if n % 2 == 0:
                    vg_mm(n // 2)
                scores(n)
                if n < 2:
                    scan_turn(2 * n)
                    block_step(2 * n)
                    scan_turn(2 * n + 1)
                    block_step(2 * n + 1)
                if n >= 3 and n % 2 == 1:
                    final((n - 3) // 2)
                if n >= 6 and n % 2 == 0:
                    pe.wait_ge(s_pT, n - 1)
                    x2_turn((n - 6) // 2, ps_p)
                if n == 13:
                    pe.wait_ge(s_pT, n - 1)
                    pe.wait_ge(ld["gates"], 16)
                    logits(0, ps_p)
            pe.wait_ge(s_qs, UNITS)
            weights_turn(0, ps_q)

            def up(j):
                c, f = j // FT, j % FT
                toks = slice(c * CHUNK, (c + 1) * CHUNK)
                pe.wait_ge(s_cT, c + 1)
                if j >= 1:
                    pe.wait_ge(s_gc, j)
                if j <= LAG:
                    pe.wait_ge(s_pT, UNITS - LAG + j)
                if j == 0:
                    pe.wait_ge(s_x2hi, 5)
                mm(ps_p[:], sel_sb[:, tok(f)], cT[:, c], start=True, stop=True).then_inc(s_cb, 1)
                pe.wait_ge(s_whi, j + 1)
                pe.wait_ge(s_wlo, j + 1)
                if j == 0:
                    pe.wait_ge(s_x2lo, TPC)
                if j == FT:
                    pe.wait_ge(s_x2lo, TILES)
                if j >= 2:
                    pe.wait_ge(s_silu, j - 1)
                for s, ps, done in ((0, ps_q, s_g_mm), (1, ps_t, s_u_mm)):
                    dst = ps[:, (j % 2) * CHUNK:(j % 2 + 1) * CHUNK]
                    if s and j >= 2:
                        pe.wait_ge(s_h, j - 1)
                    for k in range(KH):
                        cols = slice(k * HID + s * P, k * HID + (s + 1) * P)
                        i = three(dst, (w_hi[:, j % WB, cols], w_lo[:, j % WB, cols]),
                                  (x2T_hi[:, k, toks], x2T_lo[:, k, toks]), k == 0, k == KH - 1)
                    i.then_inc(done, 1)

            def down(j):
                c, f = j // FT, j % FT
                pe.wait_ge(s_hhi, j + 1)
                pe.wait_ge(s_hlo, j + 1)
                if j == 0:
                    pe.wait_ge(s_s1, 2 * UNITS)
                if j == FT:
                    pe.wait_ge(s_yT, KH)
                for k in range(KH):
                    cols = slice(2 * HID + k * P, 2 * HID + (k + 1) * P)
                    i = three(ps_s[:, k * CHUNK:(k + 1) * CHUNK], (w_hi[:, j % WB, cols], w_lo[:, j % WB, cols]),
                              (h_hi[:, j % 2], h_lo[:, j % 2]), f == 0, f == FT - 1)
                i.then_inc(s_dn, 1)

            def y_turn(c, t):
                n = c * TPC + t
                pe.wait_ge(s_yT, KH * (c + 1))
                if n >= 1:
                    pe.wait_ge(s_y, n)
                for k in range(KH):
                    i = nc.tensor.transpose(ps_o[:, k * P:(k + 1) * P], yT[:, k, tok(t)], id_sb[:])
                i.then_inc(s_y_t, 1)

            pe.wait_ge(ld["route"], 32)
            for j in range(NIT):
                up(j)
                if j >= 1:
                    down(j - 1)
                if j < LAG:
                    pe.wait_ge(s_gc, j + 1)
                    p_turn(UNITS - LAG + j)
                    pv(UNITS - LAG + j)
                if j == LAG - 1:
                    final(TILES - 1)
                if j in X2_LATE:
                    pe.wait_ge(s_x1p, TILES)
                    pe.wait_ge(s_x2hi, X2_LATE[j])
                    x2_turn(X2_LATE[j], ps_o)
                if j == 8:
                    pe.wait_ge(s_x2hi, 8)
                    logits(1, ps_o)
                if j == 9:
                    logits_turn(1, ps_o)
                if j == 12:
                    pe.wait_ge(s_lg, 2)
                    weights_turn(1, ps_o)
                if FT + 2 <= j < FT + 2 + TPC:
                    y_turn(0, j - FT - 2)
            down(NIT - 1)
            for t in range(TPC):
                y_turn(1, t)

        @block.gpsimd
        def _(pool):
            cnt = [0]

            def link(i):
                cnt[0] += 1
                i.then_inc(s_pool, 1)
                pool.wait_ge(s_pool, cnt[0])

            def power(dst, src, scale, eps, rows=P):
                link(nc.gpsimd.tensor_scalar(dst, src, scale, eps, ALU.mult, ALU.add))
                return nc.gpsimd.tensor_tensor(dst, dst, nhalf[0:rows, 0:dst.shape[-1]], ALU.pow)

            link(nc.gpsimd.memset(nhalf[:], -0.5))
            link(nc.gpsimd.memset(first_sb[:], 1.0))
            nc.gpsimd.memset(first_sb[:].rearrange("p (b s) -> p b s", s=SEQ)[:, :, 0:1], 0.0).then_inc(s_first, 1)
            pool.wait_ge(s_wqup_hi, 1)
            pool.wait_ge(s_k_ss, TILES)
            power(k_r[:], k_ss[:], 1.0 / D, RMS_EPS).then_inc(s_k_r, 1)
            pool.wait_ge(s_wqup_hi, 2)
            nc.gpsimd.tensor_tensor(wqup_lo[:, 1024:2048], wqup_sb[:, 1024:2048],
                                    wqup_hi[:, 1024:2048].bitcast(F32), ALU.subtract).then_inc(s_wqup_lo1, 1)

            def r_q(u):
                pool.wait_ge(s_q_ss, HALF * (u + 1))
                if u >= 2:
                    pool.wait_ge(s_s1, 2 * (u - 1))
                power(q_r[:, u % 2], q_ss[:, u % 2], 1.0, D * RMS_EPS).then_inc(s_q_r, 1)

            def rot(u):
                pool.wait_ge(s_rope, u + 1)
                pool.wait_ge(s_q_ss, HALF * (u + 1))
                nc.gpsimd.tensor_tensor(qs[:, u % 2, :, 0:ROT], q_a[:, u % 2], q_b[:, u % 2], ALU.add) \
                    .then_inc(s_rot, 1)

            def sub_max(u):
                hs = slice((u % 2) * HALF, (u % 2 + 1) * HALF)
                pool.wait_ge(s_max, u + 1)
                nc.gpsimd.tensor_tensor(sk_sb[:, u % 2], sink_sb[:, hs], m_sb[:, u % 2], ALU.subtract) \
                    .then_inc(s_sub, 1)
                nc.gpsimd.tensor_tensor(s_sb[:, u % 2], s_sb[:, u % 2],
                                        bc(m_sb[:, u % 2].unsqueeze(2), [P, HALF, SEQ]), ALU.subtract) \
                    .then_inc(s_sub, 1)

            def norm(u):
                pool.wait_ge(s_l, u + 1)
                nc.gpsimd.tensor_tensor(s_sb[:, u % 2], s_sb[:, u % 2],
                                        bc(l_sb[:, u % 2].unsqueeze(2), [P, HALF, SEQ]), ALU.mult) \
                    .then_inc(s_norm, 1)

            def ln_power(rs, mv, t, wait, done):
                pool.wait_ge(wait, t + 1)
                link(nc.gpsimd.tensor_scalar(rs[:, t % 2:t % 2 + 1], mv[:, t % 2, 1:2], 1.0, LN_EPS,
                                             ALU.mult, ALU.add))
                nc.gpsimd.tensor_tensor(rs[:, t % 2:t % 2 + 1], rs[:, t % 2:t % 2 + 1], nhalf[:, 0:1], ALU.pow) \
                    .then_inc(done, 1)

            def low_w(j):
                pool.wait_ge(s_whi, j + 1)
                nc.gpsimd.tensor_tensor(w_lo[:, j % WB], w_raw[:, j % WB], w_hi[:, j % WB].bitcast(F32),
                                        ALU.subtract).then_inc(s_wlo, 1)

            rot(0)
            pool.wait_ge(s_gw_hi, 1)
            nc.gpsimd.tensor_tensor(gw_lo[:], gw_sb[:], gw_hi[:].bitcast(F32), ALU.subtract).then_inc(s_gw_lo, 1)
            for n in range(UNITS):
                if n >= 1:
                    sub_max(n - 1)
                r_q(n)
                if n >= 5 and n % 2 == 1:
                    ln_power(rs2, mv2, (n - 5) // 2, s_ln2, s_rs2)
                if n >= 1:
                    norm(n - 1)
                if n >= 4 and n % 2 == 0:
                    ln_power(rs1, mv1, (n - 4) // 2, s_ln1, s_rs1)
                if n + 1 < UNITS:
                    rot(n + 1)
                if n == 0:
                    pool.wait_ge(s_skv_ss, 1)
                    power(skv_r[:], skv_ss[:], 1.0 / D, RMS_EPS, BATCH).then_inc(s_skv_r, 1)
            low_w(0)
            sub_max(UNITS - 1)
            norm(UNITS - 1)
            for j in range(1, WB - 1):
                low_w(j)
            for j in range(NIT):
                if j >= 1 and j + WB - 2 < NIT:
                    low_w(j + WB - 2)
                for k, power_, rs, mv, a, b in ((0, 6, rs1, mv1, s_ln1, s_rs1), (1, 6, rs2, mv2, s_ln2, s_rs2),
                                                (2, 7, rs1, mv1, s_ln1, s_rs1), (3, 7, rs2, mv2, s_ln2, s_rs2)):
                    if j == k:
                        ln_power(rs, mv, power_, a, b)
                if FT + 2 <= j < FT + 2 + TPC:
                    ln_power(rs3, mv3, j - FT - 2, s_ln3, s_rs3)
            for t in range(TPC):
                ln_power(rs3, mv3, TPC + t, s_ln3, s_rs3)

        @block.vector
        def _(dve):
            tt = nc.vector.tensor_tensor

            dve.wait_ge(s_wqup_hi, 1)
            tt(wqup_lo[:, 0:1024], wqup_sb[:, 0:1024], wqup_hi[:, 0:1024].bitcast(F32), ALU.subtract) \
                .then_inc(s_wqup_lo0, 1)
            dve.wait_ge(s_qc_hi, 1)
            tt(qc_lo[:], ps_q[:], qc_hi[:].bitcast(F32), ALU.subtract).then_inc(s_qc_lo, 1)
            dve.wait_ge(s_c_mm, 2)
            dve.wait_ge(ld["bias"], 16)
            zp = ps_o[:].rearrange("p (b m) -> p b m", m=BLK)
            cp = ps_p[:].rearrange("p (b m) -> p b m", m=BLK)
            tt(z_sb[:], zp, bc(bias_sb[:].unsqueeze(1), [P, BATCH, BLK]), ALU.add).then_inc(s_z, 1)
            dve.wait_ge(s_z, 1)
            nc.vector.tensor_reduce(z_max[:], z_sb[:], AX_X, ALU.max).then_inc(s_z, 1)
            dve.wait_ge(s_z, 2)
            tt(z_sb[:], z_sb[:], bc(z_max[:].unsqueeze(2), [P, BATCH, BLK]), ALU.subtract).then_inc(s_z, 1)
            dve.wait_ge(s_k_r, 1)
            dve.wait_ge(ld["norm"], 32)
            dve.wait_ge(ld["rope"], 32)
            kp = ps_s[:].rearrange("p (t d) -> p t d", d=D)
            tt(k_n[:], kp, bc(k_r[:].unsqueeze(2), [P, TILES, D]), ALU.mult).then_inc(s_k_dve, 1)
            dve.wait_ge(s_k_dve, 1)
            tt(k_n[:], k_n[:], bc(knw_sb[:].unsqueeze(1), [P, TILES, D]), ALU.mult).then_inc(s_k_dve, 1)
            dve.wait_ge(s_k_dve, 2)
            h = ROT // 2
            tt(k_a[:], k_n[:, :, 0:ROT], bc(cos_sb[:].unsqueeze(1), [P, TILES, ROT]), ALU.mult).then_inc(s_k_dve, 1)
            tt(k_b[:, :, 0:h], k_n[:, :, h:ROT], bc(sin_sb[:, 0:h].unsqueeze(1), [P, TILES, h]), ALU.mult) \
                .then_inc(s_k_dve, 1)
            tt(k_b[:, :, h:ROT], k_n[:, :, 0:h], bc(sin_sb[:, h:ROT].unsqueeze(1), [P, TILES, h]), ALU.mult) \
                .then_inc(s_k_dve, 1)
            dve.wait_ge(s_k_dve, 5)
            tt(k_n[:, :, 0:ROT], k_a[:], k_b[:], ALU.add).then_inc(s_k_dve, 1)
            dve.wait_ge(s_k_dve, 6)
            tt(k_n[:], k_n[:], bc(qnw_sb[:].unsqueeze(1), [P, TILES, D]), ALU.mult).then_inc(s_k_dve, 1)
            dve.wait_ge(s_z_exp, 1)
            nc.vector.tensor_reduce(z_sum[:], z_sb[:], AX_X, ALU.add).then_inc(s_z, 1)
            dve.wait_ge(s_z, 4)
            tt(z_sb[:], z_sb[:], cp, ALU.mult).then_inc(s_z, 1)
            nc.vector.reciprocal(z_sum[:], z_sum[:]).then_inc(s_z, 1)
            dve.wait_ge(s_z, 6)
            nc.vector.tensor_reduce(c_num[:], z_sb[:], AX_X, ALU.add).then_inc(s_z, 1)
            dve.wait_ge(s_z, 7)
            tt(c_sb[:], c_num[:], z_sum[:], ALU.mult).then_inc(s_skv, 1)
            dve.wait_ge(s_v_hi, 1)
            tt(v_lo[:], ps_t[:], v_hi[:].bitcast(F32), ALU.subtract).then_inc(s_v_lo, 1)

            def scan(k):
                if k == 0:
                    dve.wait_ge(s_kvx, 1)
                    dve.wait_ge(ld["decay"], 16)
                    dve.wait_ge(s_first, 1)
                    for i in range(KH):
                        nc.vector.tensor_scalar(dk[:, i], first_sb[:], decay_sb[:, i:i + 1], None, ALU.mult) \
                            .then_inc(s_scan_in, 1)
                dve.wait_ge(s_scan_in, KH)
                nc.vector.tensor_tensor_scan(rT[:, k], dk[:, k], kvx[:, k], 0.0, ALU.mult, ALU.add) \
                    .then_inc(s_scan, 1)

            def block_norm():
                dve.wait_ge(s_skv_mm, 1)
                nc.vector.tensor_copy(skv_t[:], ps_o[0:BATCH, 0:P]).then_inc(s_z, 1)
                dve.wait_ge(s_z, 8)
                tt(skv_sq[:], skv_t[:], skv_t[:], ALU.mult).then_inc(s_z, 1)
                dve.wait_ge(s_z, 9)
                nc.vector.tensor_reduce(skv_ss[:], skv_sq[:], AX_X, ALU.add).then_inc(s_skv_ss, 1)
                dve.wait_ge(s_skv_r, 1)
                nc.vector.scalar_tensor_tensor(skv_t[:], skv_t[:], skv_r[:, 0:1], knw_sb[0:BATCH, :],
                                               ALU.mult, ALU.mult).then_inc(s_skv, 1)

            def block_copy(i, dst, src, done):
                dve.wait_ge(s_skv_mm, i)
                nc.vector.tensor_copy(dst, src).then_inc(done, 1)

            def rope(u):
                dve.wait_ge(s_qs, u + 1)
                if u >= 2:
                    dve.wait_ge(s_rot, u - 1)
                q = qs[:, u % 2]
                tt(q_a[:, u % 2], q[:, :, 0:ROT], bc(cos_sb[:].unsqueeze(1), [P, HALF, ROT]), ALU.mult)
                tt(q_b[:, u % 2, :, 0:h], q[:, :, h:ROT], bc(sin_sb[:, 0:h].unsqueeze(1), [P, HALF, h]), ALU.mult)
                tt(q_b[:, u % 2, :, h:ROT], q[:, :, 0:h], bc(sin_sb[:, h:ROT].unsqueeze(1), [P, HALF, h]),
                   ALU.mult).then_inc(s_rope, 1)

            def scale(u):
                dve.wait_ge(s_s_mm, u + 1)
                dve.wait_ge(s_q_r, u + 1)
                if u >= 2:
                    dve.wait_ge(s_pT_t, u - 1)
                sp_ = ps_s[:].rearrange("p (h b j) -> p h b j", b=2, j=SEQ)
                for b in range(2):
                    rows = slice(b * 64, b * 64 + 64)
                    tt(s_sb[rows, u % 2], sp_[rows, :, b], bc(q_r[rows, u % 2].unsqueeze(2), [64, HALF, SEQ]),
                       ALU.mult).then_inc(s_s1, 1)
                dve.wait_ge(s_s1, 2 * (u + 1))
                if u >= 2:
                    dve.wait_ge(s_sub, 2 * (u - 1))
                nc.vector.tensor_reduce(m_sb[:, u % 2], s_sb[:, u % 2], AX_X, ALU.max).then_inc(s_mx, 1)
                dve.wait_ge(s_mx, u + 1)
                tt(m_sb[:, u % 2], m_sb[:, u % 2], sink_sb[:, (u % 2) * HALF:(u % 2 + 1) * HALF], ALU.max) \
                    .then_inc(s_max, 1)

            def sums(u):
                dve.wait_ge(s_exp, 2 * (u + 1))
                if u >= 2:
                    dve.wait_ge(s_norm, u - 1)
                nc.vector.tensor_reduce(l_sb[:, u % 2], s_sb[:, u % 2], AX_X, ALU.add).then_inc(s_l0, 1)
                dve.wait_ge(s_l0, 2 * u + 1)
                tt(l_sb[:, u % 2], l_sb[:, u % 2], sk_sb[:, u % 2], ALU.add).then_inc(s_l0, 1)
                dve.wait_ge(s_l0, 2 * u + 2)
                nc.vector.reciprocal(l_sb[:, u % 2], l_sb[:, u % 2]).then_inc(s_l, 1)

            def turn_o(t):
                dve.wait_ge(s_pv, 2 * (t + 1))
                if t >= 2:
                    dve.wait_ge(s_fin, t - 1)
                src = ps_o[:].rearrange("p (k a n) -> p k a n", k=KH, a=2)
                for b in range(2):
                    for a in range(2):
                        nc.vector.tensor_copy(oT[a * 64:a * 64 + 64, t % 2, :, b * 64:b * 64 + 64],
                                              src[b * 64:b * 64 + 64, :, a, b * 64:b * 64 + 64]).then_inc(s_oT, 1)

            def ln_a(t):
                p = t % 2
                dve.wait_ge(s_fin, t + 1)
                tt(x1p[:, p], ps_o[:, 0:HID], x_sb[:, t], ALU.add).then_inc(s_x1p, 1)
                dve.wait_ge(s_x1p, t + 1)
                nc.vector.bn_stats(st1[:, p], x1p[:, p]).then_inc(s_lnc, 1)
                dve.wait_ge(s_lnc, 4 * t + 1)
                nc.vector.bn_aggr(mv1[:, p], st1[:, p]).then_inc(s_ln1, 1)

            def ln_b(t):
                p = t % 2
                dve.wait_ge(s_rs1, t + 1)
                dve.wait_ge(s_ln1, t + 1)
                nc.vector.tensor_scalar(x1[:, p], x1p[:, p], mv1[:, p, 0:1], rs1[:, p:p + 1],
                                        ALU.subtract, ALU.mult).then_inc(s_lnc, 1)
                dve.wait_ge(s_lnc, 4 * t + 2)
                tt(x2p[:, p], x1[:, p], r1[:, t], ALU.mult).then_inc(s_lnc, 1)
                dve.wait_ge(s_lnc, 4 * t + 3)
                nc.vector.bn_stats(st2[:, p], x2p[:, p]).then_inc(s_lnc, 1)
                dve.wait_ge(s_lnc, 4 * t + 4)
                nc.vector.bn_aggr(mv2[:, p], st2[:, p]).then_inc(s_ln2, 1)

            def ln_c(t):
                p = t % 2
                dve.wait_ge(s_rs2, t + 1)
                dve.wait_ge(s_ln2, t + 1)
                if t >= 2:
                    dve.wait_ge(s_x2_t, t - 1)
                nc.vector.tensor_scalar(x2[:, p], x2p[:, p], mv2[:, p, 0:1], rs2[:, p:p + 1],
                                        ALU.subtract, ALU.mult).then_inc(s_x2, 1)

            def x2_lo(t):
                dve.wait_ge(s_x2hi, t + 1)
                dve.wait_ge(s_x2T, t + 1)
                tt(x2T_lo[:, :, tok(t)], x2T[:, :, tok(t)], x2T_hi[:, :, tok(t)].bitcast(F32), ALU.subtract) \
                    .then_inc(s_x2lo, 1)

            chain = [0]

            def link(i):
                chain[0] += 1
                i.then_inc(s_rt, 1)
                dve.wait_ge(s_rt, chain[0])

            def route_a(c, ps):
                dve.wait_ge(s_lg_t, c + 1)
                nc.vector.tensor_copy(lg[:], ps[:, 0:TPC * GATES].rearrange("p (t g) -> p t g", g=GATES)) \
                    .then_inc(s_lg, 1)
                dve.wait_ge(s_lg, c + 1)
                link(nc.vector.tensor_reduce(lmax[:], lg[:, :, 0:EXPERTS], AX_X, ALU.max))
                tt(lg[:, :, 0:EXPERTS], lg[:, :, 0:EXPERTS], bc(lmax[:].unsqueeze(2), [P, TPC, EXPERTS]),
                   ALU.subtract)
                nc.vector.tensor_scalar(lg[:, :, EXPERTS:], lg[:, :, EXPERTS:], -1.0, None, ALU.mult) \
                    .then_inc(s_lsub, 1)

            def route_b(c):
                dve.wait_ge(s_lexp, c + 1)
                for t in range(TPC):
                    i = nc.vector.max(top[:, t], ex[:, t, 0:EXPERTS])
                link(i)
                for t in range(TPC):
                    i = nc.vector.max_index(topi[:, t], top[:, t], ex[:, t, 0:EXPERTS])
                link(i)
                link(nc.vector.tensor_copy(topf[:], topi[:, :, 0:2]))
                for r in range(2):
                    i = tt(pick[:, r], bc(iota_sb[:].unsqueeze(1), [P, TPC, EXPERTS]),
                           bc(topf[:, :, r:r + 1], [P, TPC, EXPERTS]), ALU.is_equal)
                link(i)
                link(tt(pick[:, 0], pick[:, 0], pick[:, 1], ALU.add))
                link(tt(pick[:, 0], pick[:, 0], ex[:, :, 0:EXPERTS], ALU.mult))
                link(nc.vector.tensor_reduce(den[:], pick[:, 0], AX_X, ALU.add))
                link(nc.vector.reciprocal(den[:], den[:]))
                tt(cw[:, :, 0:EXPERTS], pick[:, 0], bc(den[:].unsqueeze(2), [P, TPC, EXPERTS]), ALU.mult)
                link(nc.vector.tensor_scalar(ex[:, :, EXPERTS:], ex[:, :, EXPERTS:], 1.0, None, ALU.add))
                link(nc.vector.reciprocal(cw[:, :, EXPERTS:], ex[:, :, EXPERTS:]))
                if c:
                    dve.wait_ge(s_c_t, c)
                link(nc.vector.tensor_copy(cparts[:, :, 0], cw[:]))
                link(tt(cres[:, 0], cw[:], cparts[:, :, 0], ALU.subtract))
                link(nc.vector.tensor_copy(cparts[:, :, 1], cres[:, 0]))
                link(tt(cres[:, 1], cres[:, 0], cparts[:, :, 1], ALU.subtract))
                nc.vector.tensor_copy(cparts[:, :, 2], cres[:, 1]).then_inc(s_cw, 1)

            dve.wait_ge(ld["mask"], 32)
            rope(0)
            for n in range(UNITS):
                if n < 2:
                    scan(n)
                if n == 2:
                    block_copy(5, sgf[:], ps_o[0:BATCH, 0:HID], s_const)
                if n >= 1:
                    sums(n - 1)
                if n >= 5 and n % 2 == 1:
                    ln_c((n - 5) // 2)
                if n >= 3 and n % 2 == 1:
                    turn_o((n - 3) // 2)
                if n >= 7 and n % 2 == 1:
                    x2_lo((n - 7) // 2)
                if n == 14:
                    route_a(0, ps_q)
                if n + 1 < UNITS:
                    rope(n + 1)
                if n >= 4 and n % 2 == 0:
                    ln_b((n - 4) // 2)
                scale(n)
                if n == 0:
                    block_norm()
                    block_copy(2, skvT[:], ps_o[:, 0:BATCH], s_skv)
                if n == 1:
                    block_copy(3, sg_sb[:], ps_o[0:BATCH, 0:HID], s_skv)
                    block_copy(4, sgT[:], ps_o[:, 0:KH * BATCH].rearrange("p (k b) -> p k b", k=KH), s_skv)
                if n >= 3 and n % 2 == 1:
                    if n == 3:
                        dve.wait_ge(ld["x"], 16)
                        dve.wait_ge(s_r1, 4)
                    ln_a((n - 3) // 2)
                if n == 15:
                    dve.wait_ge(ld["route"], 32)
                    route_b(0)
            sums(UNITS - 1)

            def y_evac(c):
                dve.wait_ge(s_dn, FT * (c + 1))
                if c:
                    dve.wait_ge(s_y_t, TPC)
                for k in range(KH):
                    tt(yT[:, k], ps_s[:, k * CHUNK:(k + 1) * CHUNK], x2T[:, k, c * CHUNK:(c + 1) * CHUNK],
                       ALU.add).then_inc(s_yT, 1)

            def ln_y_a(n):
                p = n % 2
                dve.wait_ge(s_y_t, n + 1)
                if n >= 2:
                    dve.wait_ge(s_yo, n - 1)
                nc.vector.tensor_copy(y_sb[:, p], ps_o[:, 0:HID]).then_inc(s_y, 1)
                dve.wait_ge(s_y, n + 1)
                nc.vector.bn_stats(st3[:, p], y_sb[:, p]).then_inc(s_y3, 1)
                dve.wait_ge(s_y3, n + 1)
                nc.vector.bn_aggr(mv3[:, p], st3[:, p]).then_inc(s_ln3, 1)

            def ln_y_b(n):
                p = n % 2
                dve.wait_ge(s_rs3, n + 1)
                dve.wait_ge(s_ln3, n + 1)
                nc.vector.tensor_scalar(y_out[:, n], y_sb[:, p], mv3[:, p, 0:1], rs3[:, p:p + 1],
                                        ALU.subtract, ALU.mult).then_inc(s_yo, 1)

            for j in range(NIT):
                dve.wait_ge(s_silu, j + 1)
                dve.wait_ge(s_cb, j + 1)
                tt(act_c[:, j % 2], act_g[:, j % 2], ps_p[:], ALU.mult).then_inc(s_gc, 1)
                dve.wait_ge(s_gc, j + 1)
                dve.wait_ge(s_u_mm, j + 1)
                if j >= 2:
                    dve.wait_ge(s_hhi, j - 1)
                else:
                    dve.wait_ge(s_pT_t, UNITS - LAG + j + 1)
                tt(h_sb[:, j % 2], act_c[:, j % 2], ps_t[:, (j % 2) * CHUNK:(j % 2 + 1) * CHUNK], ALU.mult) \
                    .then_inc(s_h, 1)
                dve.wait_ge(s_hhi, j + 1)
                if j >= 2:
                    dve.wait_ge(s_dn, j - 1)
                tt(h_lo[:, j % 2], h_sb[:, j % 2], h_hi[:, j % 2].bitcast(F32), ALU.subtract).then_inc(s_hlo, 1)
                if j == 0:
                    ln_b(6)
                if j == 1:
                    ln_c(6)
                    turn_o(7)
                    ln_a(7)
                if j == 2:
                    ln_b(7)
                if j == 3:
                    ln_c(7)
                if j - 1 in X2_LATE:
                    x2_lo(X2_LATE[j - 1])
                if j == 9:
                    route_a(1, ps_o)
                if j == 10:
                    route_b(1)
                if j == FT:
                    y_evac(0)
                if FT + 2 <= j < FT + 2 + TPC:
                    ln_y_a(j - FT - 2)
                if FT + 3 <= j < FT + 3 + TPC:
                    ln_y_b(j - FT - 3)
            y_evac(1)
            for t in range(TPC):
                ln_y_a(TPC + t)
                if t:
                    ln_y_b(TPC + t - 1)
            ln_y_b(TILES - 1)


def _constants(np):
    f = np.float32
    inv = (f(1.0) / f(10000.0) ** (np.arange(0, ROT, 2, dtype=f) / f(ROT))).astype(f)
    ang = (np.arange(SEQ, dtype=f)[:, None] * inv).astype(f)
    cos, sin = np.cos(ang).astype(f), np.sin(ang).astype(f)
    t = np.arange(TOK)
    rows = np.arange(FT * P)
    gate = np.where(rows < MOE_ROWS, rows // I_MOE, np.where(rows < MOE_ROWS + I_SH, EXPERTS, GATES))
    key, query = np.arange(SEQ)[None, :], (np.arange(P) % SEQ)[:, None]
    from concourse import mybir as _mybir
    return {
        "cosT": np.tile(np.concatenate([cos, cos], 1), (2, 1)),
        "sinT": np.tile(np.concatenate([-sin, sin], 1), (2, 1)),
        "mask": np.tile(np.where(key <= query, 0.0, -1e30), (1, 8)).astype(_mybir.dt.np(BF16)),
        "ident": np.eye(P, dtype=f),
        "late": ((t[None, :] // SEQ == np.arange(BATCH)[:, None]) & (t[None, :] % SEQ >= BLK)).astype(f),
        "sel": np.tile(gate[None, :] == np.arange(GATES)[:, None], (3, 1)).astype(_mybir.dt.np(BF16)),
        "iota": np.tile(np.arange(EXPERTS, dtype=f), (P, 1)),
    }


def kernel(**inputs):
    import numpy as np
    import concourse.bacc as _bacc
    from concourse.bass_utils import run_bass_kernel_spmd as _run

    a = {k.replace("L0_", ""): np.asarray(v) for k, v in inputs.items()}
    x = a["x"].reshape(TOK, HID)

    def rep(v):
        return np.tile(v.reshape(1, -1), (P, 1))

    gw = a["attn_group_w"].reshape(GROUPS * 4, D, GDIM).transpose(1, 0, 2).reshape(D, HALF, 2, GDIM)
    gw = gw.transpose(0, 2, 1, 3).reshape(D, 2 * HALF * GDIM)
    fill = np.zeros((FT * P - MOE_ROWS - I_SH, HID), np.float32)
    w1, gu = a["ffn_w1"], a["ffn_shared_gate_up_w"]
    wg = np.concatenate([w1[:, :I_MOE].reshape(MOE_ROWS, HID), gu[:I_SH], fill])
    wu = np.concatenate([w1[:, I_MOE:].reshape(MOE_ROWS, HID), gu[I_SH:], fill])
    wd = np.concatenate([a["ffn_w2"].transpose(0, 2, 1).reshape(MOE_ROWS, HID), a["ffn_shared_down_w"].T, fill])
    up = np.stack([w.reshape(FT, P, KH, P).transpose(0, 3, 2, 1) for w in (wg, wu)], 3)
    wffn = np.concatenate([up.reshape(FT, P, KH * 2 * P), wd.reshape(FT, P, HID)], 2)
    data = {
        "x": x, "xT": x.T, "ctxT": a["ctx_2048"].reshape(TOK, HID).T,
        "w_qc": a["attn_w_qc"], "w_qup": a["attn_w_qup"], "w_kv": a["attn_w_kv_b"], "w_z": a["attn_w_z_b"],
        "biasT": a["attn_bias_b"].T, "w_k": a["attn_w_k"], "w_v": a["attn_w_v"],
        "knw": rep(a["attn_k_norm_w"]), "qnw": rep(a["attn_q_norm_w"]), "sink": rep(a["attn_sink_logit"]),
        "gw": gw, "fw": a["attn_final_w"], "decay": np.repeat(a["xattn_decay"].reshape(-1), HID // HEADS).reshape(KH, P).T,
        "gates": np.concatenate([a["ffn_gate_w"], a["ffn_shared_gate_w"]]).T, "wffn": wffn,
        **_constants(np),
    }
    nc = _bacc.Bacc("TRN2", target_bir_lowering=False, num_devices=1)
    arrays, args = {}, {}
    for name, v in data.items():
        v = np.ascontiguousarray(v)
        arrays[name + "_in"] = v
        args[name] = nc.dram_tensor(name + "_in", v.shape, mybir.dt.from_np(v.dtype), kind="ExternalInput").ap()
    out = nc.dram_tensor("out_dram", (TOK, HID), F32, kind="ExternalOutput").ap()
    build(nc, out=out, **args)
    r = _run(nc, [arrays], core_ids=[0])
    return r.results[0]["out_dram"].reshape(BATCH, SEQ, HID)
```

```python
from contextlib import ExitStack

import concourse.bass as bass
from concourse import mybir

F32 = mybir.dt.float32
F32R = mybir.dt.float32r
BF16 = mybir.dt.bfloat16
U32 = mybir.dt.uint32
ALU = mybir.AluOpType
ACT = mybir.ActivationFunctionType
AX_X = mybir.AxisListType.X

P = 128
BATCH, SEQ, HID = 16, 64, 256
TOK = BATCH * SEQ
TILES = TOK // P
KT = TILES // 2
KH = HID // P
HEADS, D, ROT = 16, 128, 64
HALF = HEADS // 2
UNITS = 2 * TILES
GROUPS, GDIM = 4, 64
BLK = 32
EXPERTS, I_MOE, I_SH = 8, 176, 704
MOE_ROWS = EXPERTS * I_MOE
FT = -(-(MOE_ROWS + I_SH) // P)
SHARED_FT = MOE_ROWS // P
GATES = EXPERTS + 1
CHUNK = 512
TPC = CHUNK // P
LAG = 2
WB = 4
HB = 4
LAST_DOWN = 4
TABLES = (("ident", P), ("cos", ROT), ("sin", ROT), ("knw", D), ("qnw", D), ("sink", HEADS), ("bias", BLK),
          ("iota", EXPERTS))
LAST_ROWS = MOE_ROWS + I_SH - (FT - 1) * P
RMS_EPS = 1e-6
LN_EPS = 1e-5


def build(nc, x, xT, ctxT, w_x, w_qup, gw, fw, gates, wffn, decay, tables, mask, late, sel, out):
    with ExitStack() as ctx:
        def sb(name, shape, dt=F32):
            return ctx.enter_context(nc.sbuf_tensor(name, shape, dt))

        def psum(name, shape, dt=F32):
            return ctx.enter_context(nc.psum_tensor(name, shape, dt))

        def sem(name):
            return ctx.enter_context(nc.semaphore(name))

        ps_q = psum("ps_q", [P, 1024])
        ps_t = psum("ps_t", [P, 1024])
        ps_s = psum("ps_s", [P, 1024])
        ps_p = psum("ps_p", [P, 512])
        ps_o = psum("ps_o", [P, 512])

        x_sb = sb("x_sb", [P, TILES, HID])
        xT_sb = sb("xT_sb", [P, KH, TOK])
        ctx_sb = sb("ctx_sb", [P, KH, TOK])
        wx_sb = sb("wx_sb", [P, KH, 5 * D])
        wqc_sb, wk_sb, wv_sb, wkv_sb, wz_sb = (wx_sb[:, :, i * D:(i + 1) * D] for i in range(5))
        w_raws = sb("w_raws", [P, WB * 3 * HID])
        wqup_sb = w_raws[:, 0:HEADS * D]
        vg_tok = sb("vg_tok", [P, 2, 2, HALF, GDIM])
        gw_sb = vg_tok[:, 1]
        fw_sb = sb("fw_sb", [P, KH, HID])
        tab_sb = sb("tab_sb", [P, sum(n for _, n in TABLES)])
        at = {}
        for name, n in TABLES:
            at[name] = tab_sb[:, sum(at_.shape[-1] for at_ in at.values()):][:, 0:n]
        id_sb, cos_sb, sin_sb, knw_sb, qnw_sb = at["ident"], at["cos"], at["sin"], at["knw"], at["qnw"]
        sink_sb, bias_sb, iota_sb = at["sink"], at["bias"], at["iota"]
        decay_sb = sb("decay_sb", [P, KH])
        gates_sb = sb("gates_sb", [P, KH, GATES])
        mask_sb = sb("mask_sb", [P, 4 * P], BF16)
        idb_sb = sb("idb_sb", [P, P], BF16)
        first_sb = sb("first_sb", [P, TOK])
        late_sb = sb("late_sb", [BATCH, TOK])
        sel_sb = sb("sel_sb", [3 * GATES, FT * P], BF16)
        nhalf = sb("nhalf", [P, 16])

        whi_buf = sb("whi_buf", [P, WB * 3 * HID], F32R)
        wlo_buf = sb("wlo_buf", [P, WB * 3 * HID], F32R)
        wqup_hi, wqup_lo = whi_buf[:, 0:HEADS * D], wlo_buf[:, 0:HEADS * D]
        gw_hi = sb("gw_hi", [P, 2, HALF, GDIM], F32R)
        gw_lo = sb("gw_lo", [P, 2, HALF, GDIM], F32R)
        qc_hi = sb("qc_hi", [P, TOK], F32R)
        qc_lo = sb("qc_lo", [P, TOK], F32R)
        v_hi = sb("v_hi", [P, TOK], F32R)
        v_lo = sb("v_lo", [P, TOK], F32R)

        q_sq = sb("q_sq", [P, 2, HALF, D])
        qs = sb("qs", [P, 2, HALF, D])
        s_sb = sb("s_sb", [P, 2, HALF, SEQ])
        junk = sb("junk", [P, 2, D])
        k_ss = sb("k_ss", [P, TILES])
        k_r = sb("k_r", [P, TILES])
        kT = sb("kT", [P, TOK])

        z_sb = sb("z_sb", [P, BATCH, BLK])
        z_max = sb("z_max", [P, BATCH])
        z_sum = sb("z_sum", [P, BATCH])
        c_num = sb("c_num", [P, BATCH])
        c_sb = sb("c_sb", [P, BATCH])
        skv_t = sb("skv_t", [BATCH, D])
        skv_sq = sb("skv_sq", [BATCH, D])
        skv_ss = sb("skv_ss", [BATCH, 1])
        skv_r = sb("skv_r", [BATCH, 1])
        skvT = sb("skvT", [P, BATCH])
        sg_sb = sb("sg_sb", [BATCH, HID])
        sgT = sb("sgT", [P, KH, BATCH])
        sgf = sb("sgf", [BATCH, HID])

        kvx = ctx_sb
        dk = sb("dk", [P, KH, TOK])
        rT = q_sq[:].rearrange("p u h d -> p u (h d)")
        r1 = sb("r1", [P, TILES, HID])

        q_a = sb("q_a", [P, 2, HALF, ROT])
        q_b = sb("q_b", [P, 2, HALF, ROT])
        q_ss = sb("q_ss", [P, 2, HALF])
        q_r = sb("q_r", [P, 2, HALF])
        qT = xT_sb
        m_sb = sb("m_sb", [P, 2, HALF])
        sk_sb = sb("sk_sb", [P, 2, HALF])
        l_sb = sb("l_sb", [P, 2, HALF])
        pT = first_sb[:].rearrange("p (u n) -> p u n", u=2)
        vg = sb("vg", [P, 2, HALF, 2, GDIM])
        oT = sb("oT", [P, 2, KH, P])

        x1p = sb("x1p", [P, 2, HID])
        x1 = sb("x1", [P, 2, HID])
        x2p = sb("x2p", [P, 2, HID])
        x2 = sb("x2", [P, 2, HID])
        st1 = sb("st1", [P, 2, 6])
        mv1 = sb("mv1", [P, 2, 2])
        st2 = sb("st2", [P, 2, 6])
        mv2 = sb("mv2", [P, 2, 2])
        rs1 = sb("rs1", [P, 2])
        rs2 = sb("rs2", [P, 2])
        x2T = ctx_sb
        x2T_hi = sb("x2T_hi", [P, KH, TOK], F32R)
        x2T_lo = sb("x2T_lo", [P, KH, TOK], F32R)

        def key_rows(ap, n):
            return ap.rearrange("p (t d) -> p t d", d=n)

        KC, KR = KT * D, KT * ROT
        k_raw, k_junk = key_rows(w_raws[:, 3 * KC:4 * KC], D), key_rows(w_raws[:, 2 * KC:3 * KC], D)
        q_sq1 = q_sq[:, 1].rearrange("p h d -> p (h d)")
        k_n = (key_rows(s_sb[:, 0].rearrange("p h j -> p (h j)"), D), key_rows(w_raws[:, 0:KC], D))
        k_a = (key_rows(q_sq1[:, 0:KR], ROT), key_rows(w_raws[:, KC:KC + KR], ROT))
        k_b = (key_rows(q_sq1[:, KR:2 * KR], ROT), key_rows(w_raws[:, KC + KR:KC + 2 * KR], ROT))

        lgT = sb("lgT", [GATES, CHUNK])
        lg = sb("lg", [P, TPC, GATES])
        lmax = sb("lmax", [P, TPC])
        ex = sb("ex", [P, TPC, GATES])
        top = sb("top", [P, TPC, 8])
        topi = sb("topi", [P, TPC, 8], U32)
        topf = sb("topf", [P, TPC, 2])
        pick = sb("pick", [P, 2, TPC, EXPERTS])
        den = sb("den", [P, TPC])
        cw = sb("cw", [P, TPC, GATES])
        cres = sb("cres", [P, 2, TPC, GATES])
        cparts = sb("cparts", [P, TPC, 3, GATES], BF16)
        cT = z_sb[0:3 * GATES].rearrange("p b m -> p (b m)").bitcast(BF16).rearrange("p (c n) -> p c n", c=2)

        w_raw = w_raws[:].rearrange("p (b n) -> p b n", b=WB)
        w_hi = whi_buf[:].rearrange("p (b n) -> p b n", b=WB)
        w_lo = wlo_buf[:].rearrange("p (b n) -> p b n", b=WB)
        act_g = q_a[:].rearrange("p u h d -> p u (h d)")
        act_c = q_b[:].rearrange("p u h d -> p u (h d)")
        h_sb = s_sb[:].rearrange("p u h j -> p u (h j)")
        h_hi = [a[:, i * CHUNK:(i + 1) * CHUNK] for a in (qc_hi, v_hi) for i in range(2)]
        h_lo = [a[:, i * CHUNK:(i + 1) * CHUNK] for a in (qc_lo, v_lo) for i in range(2)]
        yT = xT_sb[:, :, 0:CHUNK]
        st3 = sb("st3", [P, TPC, 6])
        mv3 = sb("mv3", [P, TPC, 2])
        rs3 = sb("rs3", [P, TPC])
        y_out = qs[:].rearrange("p u h d -> p (u h d)").rearrange("p (t n) -> p t n", n=HID)

        ld = {n: sem("ld_" + n) for n in ("wqk", "wvc", "decay", "tab", "mask", "ctx", "gw", "fw", "x", "late",
                                          "gates", "sel")}
        ld_xT = [sem("ld_xT0"), sem("ld_xT1")]
        ld_wqup = [sem("ld_wqup0"), sem("ld_wqup1")]
        ld_w = [sem(f"ld_w{i}") for i in range(WB)]
        s_table, s_sgf = sem("s_table"), sem("s_sgf")
        s_qc_mm, s_v_mm, s_k_mm, s_c_mm = sem("s_qc_mm"), sem("s_v_mm"), sem("s_k_mm"), sem("s_c_mm")
        s_qc_hi, s_qc_lo, s_v_hi, s_v_lo = sem("s_qc_hi"), sem("s_qc_lo"), sem("s_v_hi"), sem("s_v_lo")
        s_wqup_hi, s_gw_hi, s_gw_lo = sem("s_wqup_hi"), sem("s_gw_hi"), sem("s_gw_lo")
        s_wqup_lo0, s_wqup_lo1 = sem("s_wqup_lo0"), sem("s_wqup_lo1")
        s_first, s_idb = sem("s_first"), sem("s_idb")
        s_k_ss, s_k_r, s_k_dve, s_k_t, s_kT, s_k_raw = (sem("s_k_ss"), sem("s_k_r"), sem("s_k_dve"),
                                                        sem("s_k_t"), sem("s_kT"), sem("s_k_raw"))
        s_z, s_z_exp, s_skv, s_skv_ss, s_skv_r, s_skv_mm = (sem("s_z"), sem("s_z_exp"), sem("s_skv"),
                                                            sem("s_skv_ss"), sem("s_skv_r"), sem("s_skv_mm"))
        s_scan_in = sem("s_scan_in")
        s_kvx, s_scan, s_r_t, s_r1 = sem("s_kvx"), sem("s_scan"), sem("s_r_t"), sem("s_r1")
        s_q_mm, s_qs, s_rope, s_q_ss, s_q_r = (sem("s_q_mm"), sem("s_qs"), sem("s_rope"), sem("s_q_ss"),
                                               sem("s_q_r"))
        s_rot, s_qT_t, s_qT, s_s_mm, s_s1, s_mx, s_max, s_sub = (sem("s_rot"), sem("s_qT_t"), sem("s_qT"),
                                                                 sem("s_s_mm"), sem("s_s1"), sem("s_mx"),
                                                                 sem("s_max"), sem("s_sub"))
        s_exp, s_l0, s_l, s_norm, s_pT_t, s_pT, s_pv = (sem("s_exp"), sem("s_l0"), sem("s_l"), sem("s_norm"),
                                                        sem("s_pT_t"), sem("s_pT"), sem("s_pv"))
        s_vg_mm, s_vg_tok = sem("s_vg_mm"), sem("s_vg_tok")
        s_vg = [sem("s_vg0"), sem("s_vg1")]
        s_oT, s_fin = sem("s_oT"), sem("s_fin")
        s_x1p, s_ln1, s_rs1, s_ln2, s_rs2, s_x2, s_x2_t, s_x2T, s_x2hi, s_x2lo = (
            sem("s_x1p"), sem("s_ln1"), sem("s_rs1"), sem("s_ln2"), sem("s_rs2"), sem("s_x2"), sem("s_x2_t"),
            sem("s_x2T"), sem("s_x2hi"), sem("s_x2lo"))
        s_lnc = sem("s_lnc")
        s_pool = sem("s_pool")
        s_lg_mm, s_lgT, s_lg_t, s_lg, s_lsub, s_lexp, s_rt, s_cw, s_c_t, s_cT = (
            sem("s_lg_mm"), sem("s_lgT"), sem("s_lg_t"), sem("s_lg"), sem("s_lsub"), sem("s_lexp"), sem("s_rt"),
            sem("s_cw"), sem("s_c_t"), sem("s_cT"))
        s_whi, s_wlo, s_g_mm, s_u_mm, s_cb, s_silu, s_gc, s_h, s_hhi, s_hlo, s_dn = (
            sem("s_whi"), sem("s_wlo"), sem("s_g_mm"), sem("s_u_mm"), sem("s_cb"), sem("s_silu"), sem("s_gc"),
            sem("s_h"), sem("s_hhi"), sem("s_hlo"), sem("s_dn"))
        s_dn_end = sem("s_dn_end")
        s_yT, s_y_t, s_y3, s_ln3, s_rs3, s_yo, s_st = (sem("s_yT"), sem("s_y_t"), sem("s_y3"), sem("s_ln3"),
                                                       sem("s_rs3"), sem("s_yo"), sem("s_st"))

        NIT = 2 * FT
        W_EARLY = {12: 0, 14: 1, 15: 2}
        Y_EARLY = {FT + 2 * (t + 1): t for t in range(TPC)}
        X2_LATE = {3: 5, 4: 6, 7: 7}

        def bc(ap, shape):
            return ap.to_broadcast(shape)

        def tok(t):
            return slice(t * P, (t + 1) * P)

        def rows_of(j):
            return P if (j + 1) % FT else LAST_ROWS

        def spreads(j):
            return (SHARED_FT + 1) * (j // FT) + min(j % FT, SHARED_FT) + 1

        def y_ps(n):
            if n < TPC:
                return ps_o[:, 0:HID]
            return (ps_q, ps_t)[(n - TPC) // 2][:, (n % 2) * CHUNK:(n % 2) * CHUNK + HID]

        block = ctx.enter_context(nc.Block())

        @block.sync
        def _(sp):
            def load(dst, src, s):
                sp.dma_start(dst, src).then_inc(s, 16)

            def store(t):
                sp.wait_ge(s_yo, t + 1)
                sp.dma_start(out[tok(t)], y_out[:, t]).then_inc(s_st, 16)

            wx = w_x.rearrange("(k p) n -> p k n", p=P)
            load(wx_sb[:, :, 0:2 * D], wx[:, :, 0:2 * D], ld["wqk"])
            for c in range(2):
                cols = slice(c * 512, (c + 1) * 512)
                load(xT_sb[:, :, cols], xT[:, cols].rearrange("(k p) n -> p k n", p=P), ld_xT[c])
            for i in range(2):
                load(wqup_sb[:, i * 1024:(i + 1) * 1024], w_qup[:, i * 1024:(i + 1) * 1024], ld_wqup[i])
                if i == 0:
                    load(tab_sb[:], tables, ld["tab"])
            load(wx_sb[:, :, 2 * D:], wx[:, :, 2 * D:], ld["wvc"])
            load(ctx_sb[:], ctxT.rearrange("(k p) n -> p k n", p=P), ld["ctx"])
            load(gw_sb[:], gw.rearrange("p (a h o) -> p a h o", a=2, h=HALF), ld["gw"])
            load(mask_sb[:], mask, ld["mask"])
            load(fw_sb[:], fw.rearrange("(k p) n -> p k n", p=P), ld["fw"])
            load(x_sb[:], x.rearrange("(t p) n -> p t n", p=P), ld["x"])
            load(late_sb[:], late, ld["late"])
            load(gates_sb[:], gates.rearrange("(k p) n -> p k n", p=P), ld["gates"])
            load(sel_sb[:], sel, ld["sel"])
            sp.wait_ge(s_wqup_hi, 2)
            sp.wait_ge(s_wqup_lo0, 1)
            sp.wait_ge(s_wqup_lo1, 1)
            load(w_raw[:, WB - 1], wffn[0], ld_w[0])
            for t in range(TILES):
                if t == KT:
                    sp.wait_ge(s_k_t, 2)
                    for j in range(1, WB):
                        load(w_raw[:, (j - 1) % WB], wffn[j], ld_w[j % WB])
                sp.wait_ge(s_vg_tok, t + 1)
                if t >= 2:
                    sp.wait_ge(s_pv, 2 * (t - 1))
                for b in range(2):
                    for par in range(2):
                        sp.dma_start(vg[par * 64:par * 64 + 64, t % 2, :, b], vg_tok[b * 64:b * 64 + 64, t % 2, par]) \
                          .then_inc(s_vg[t % 2], 16)
            for j in range(WB, NIT):
                sp.wait_ge(s_whi, j - WB + 1)
                sp.wait_ge(s_wlo, j - WB + 1)
                load(w_raw[:, (j - 1) % WB], wffn[j % FT], ld_w[j % WB])
                if FT + 12 <= j < FT + 12 + TPC:
                    store(j - FT - 12)
            for t in range(TPC, TILES):
                store(t)
            sp.wait_ge(s_st, 16 * TILES)

        @block.scalar
        def _(act):
            act.dma_start(decay_sb[:], decay).then_inc(ld["decay"], 16)

            def wqup_half(i):
                cols = slice(i * 1024, (i + 1) * 1024)
                act.wait_ge(ld_wqup[i], 16)
                nc.scalar.copy(wqup_hi[:, cols], wqup_sb[:, cols]).then_inc(s_wqup_hi, 1)

            act.wait_ge(s_first, 1)
            nc.scalar.activation(junk[:, 0, 0:1], nhalf[:, 0:1], ACT.Square).then_inc(s_table, 1)
            wqup_half(0)
            act.wait_ge(s_qc_mm, 1)
            nc.scalar.copy(qc_hi[:], ps_q[:]).then_inc(s_qc_hi, 1)
            wqup_half(1)
            act.wait_ge(ld["tab"], 16)
            nc.scalar.copy(idb_sb[:], id_sb[:]).then_inc(s_idb, 1)
            act.wait_ge(s_k_mm, 1)
            act.wait_ge(s_table, 1)
            for t in range(KT):
                if t >= 2:
                    act.wait_ge(s_k_ss, t - 1)
                nc.scalar.activation(junk[:, t % 2], ps_s[:, t * D:(t + 1) * D], ACT.Square,
                                     accum_out=k_ss[:, t:t + 1]).then_inc(s_k_ss, 1)

            def evac_q(u):
                for c in range(2):
                    act.wait_ge(s_q_mm, 2 * u + c + 1)
                    if u >= 2:
                        act.wait_ge(s_qT_t, 2 * (u - 1))
                    nc.scalar.copy(qs[:, u % 2, 4 * c:4 * c + 4],
                                   ps_q[:, c * 512:(c + 1) * 512].rearrange("p (h d) -> p h d", d=D)) \
                        .then_inc(s_qs, 1)

            def square_q(u):
                if u >= 2:
                    act.wait_ge(s_q_r, u - 1)
                for h in range(HALF):
                    c = KT + HALF * u + h
                    act.wait_ge(s_k_ss if c < KT + 2 else s_q_ss, c - 1 if c < KT + 2 else c - 1 - KT)
                    nc.scalar.activation(junk[:, c % 2], ps_q[:, h * D:(h + 1) * D], ACT.Square,
                                         accum_out=q_ss[:, u % 2, h:h + 1]).then_inc(s_q_ss, 1)

            def evac_qT(u):
                for c in range(2):
                    act.wait_ge(s_qT_t, 2 * u + c + 1)
                    if u >= 2:
                        act.wait_ge(s_s_mm, u - 1)
                    cols = slice(c * 512, (c + 1) * 512)
                    nc.scalar.copy(qT[:, u % 2, cols], ps_t[:, cols]).then_inc(s_qT, 1)

            def evac_kT(i, ps):
                act.wait_ge(s_k_t, i + 1)
                nc.scalar.copy(kT[:, i * KT * P:(i + 1) * KT * P], ps[:, 0:KT * P]).then_inc(s_kT, 1)

            def square_k():
                act.wait_ge(s_k_raw, 1)
                for t in range(KT):
                    nc.scalar.activation(k_junk[:, t], k_raw[:, t], ACT.Square,
                                         accum_out=k_ss[:, KT + t:KT + t + 1]).then_inc(s_k_ss, 1)

            def evac_r(i):
                k, half = i // 2, i % 2
                act.wait_ge(s_r_t, i + 1)
                nc.scalar.activation(r1[:, half * 4:half * 4 + 4, k * P:(k + 1) * P],
                                     (ps_o, ps_p)[k][:].rearrange("p (t d) -> p t d", d=P), ACT.Identity,
                                     bias=1.0).then_inc(s_r1, 1)

            def exp(u):
                act.wait_ge(s_sub, 2 * (u + 1))
                nc.scalar.activation(sk_sb[:, u % 2], sk_sb[:, u % 2], ACT.Exp).then_inc(s_exp, 1)
                nc.scalar.activation(s_sb[:, u % 2], s_sb[:, u % 2], ACT.Exp).then_inc(s_exp, 1)

            def evac_pT(u):
                act.wait_ge(s_pT_t, u + 1)
                if u >= 2:
                    act.wait_ge(s_pv, u - 1)
                nc.scalar.copy(pT[:, u % 2], ps_p[:]).then_inc(s_pT, 1)

            def evac_vg(t):
                act.wait_ge(s_vg_mm, t + 1)
                if t >= 2:
                    act.wait_ge(s_vg[t % 2], 64 * (t // 2))
                nc.scalar.copy(vg_tok[:, t % 2], ps_t[:].rearrange("p (a h o) -> p a h o", a=2, o=GDIM)) \
                    .then_inc(s_vg_tok, 1)

            def evac_x2(t, ps):
                act.wait_ge(s_x2_t, t + 1)
                src = ps[:, 0:HID].rearrange("p (k n) -> p k n", k=KH)
                nc.scalar.copy(x2T[:, :, tok(t)], src).then_inc(s_x2T, 1)
                nc.scalar.copy(x2T_hi[:, :, tok(t)], src).then_inc(s_x2hi, 1)

            def route_copy(c, ps):
                act.wait_ge(s_lg_mm, c + 1)
                if c:
                    act.wait_ge(s_lg_t, c)
                nc.scalar.copy(lgT[:], ps[0:GATES, :]).then_inc(s_lgT, 1)

            def route_exp(c):
                act.wait_ge(s_lsub, c + 1)
                nc.scalar.activation(ex[:], lg[:], ACT.Exp).then_inc(s_lexp, 1)

            def route_cT(c, ps):
                act.wait_ge(s_c_t, c + 1)
                nc.scalar.copy(cT[:, c], ps[:].bitcast(BF16)[0:3 * GATES, 0:CHUNK]).then_inc(s_cT, 1)

            def split_w(j):
                act.wait_ge(ld_w[j % WB], 16 * (j // WB + 1))
                if j >= WB:
                    act.wait_ge(s_dn, j - WB + 1)
                nc.scalar.copy(w_hi[:, (j - 1) % WB], w_raw[:, (j - 1) % WB]).then_inc(s_whi, 1)

            evac_q(0)
            square_q(0)
            act.wait_ge(s_wqup_lo1, 1)
            nc.scalar.copy(k_raw[:], key_rows(ps_s[:, KT * D:], D)).then_inc(s_k_raw, 1)
            act.wait_ge(s_v_mm, 1)
            nc.scalar.copy(v_hi[:], ps_t[:]).then_inc(s_v_hi, 1)
            act.wait_ge(ld["gw"], 16)
            nc.scalar.copy(gw_hi[:], gw_sb[:]).then_inc(s_gw_hi, 1)
            act.wait_ge(ld["ctx"], 16)
            nc.scalar.activation(kvx[:], ctx_sb[:], ACT.Square).then_inc(s_kvx, 1)
            evac_kT(0, ps_s)
            evac_qT(0)
            evac_q(1)
            act.wait_ge(s_z, 3)
            nc.scalar.activation(z_sb[:], z_sb[:], ACT.Exp).then_inc(s_z_exp, 1)
            for n in range(UNITS):
                if n == 4:
                    evac_r(3)
                if 0 < n < UNITS - 1:
                    evac_q(n + 1)
                if n == 1:
                    evac_r(1)
                if n >= LAG:
                    evac_pT(n - LAG)
                if n:
                    evac_qT(n)
                if n == 13:
                    route_copy(0, ps_p)
                if n >= 1:
                    exp(n - 1)
                if n == 14:
                    route_exp(0)
                if n + 1 < UNITS:
                    square_q(n + 1)
                if n >= 6 and n % 2 == 0:
                    evac_x2((n - 6) // 2, ps_p)
                if n % 2 == 0:
                    evac_vg(n // 2)
                if n in W_EARLY:
                    split_w(W_EARLY[n])
                if n == 3:
                    square_k()
                if n == 7:
                    evac_kT(1, ps_p)
                if n == 0:
                    evac_r(0)
                if n == 3:
                    evac_r(2)

            route_cT(0, ps_p)
            evac_pT(UNITS - 2)
            exp(UNITS - 1)
            for j in range(NIT):
                if j >= 2:
                    act.wait_ge(s_gc, j - 1)
                if j == 1:
                    evac_pT(UNITS - 1)
                act.wait_ge(s_g_mm, j + 1)
                r = slice(0, rows_of(j))
                nc.scalar.activation(act_g[r, j % 2], ps_q[r, (j % 2) * CHUNK:(j % 2 + 1) * CHUNK], ACT.Silu) \
                    .then_inc(s_silu, 1)
                if j >= 1 and j + WB - 2 < NIT:
                    split_w(j + WB - 2)
                act.wait_ge(s_h, j + 1)
                if j >= HB:
                    act.wait_ge(s_dn, j - HB + 1)
                nc.scalar.copy(h_hi[j % HB][r], h_sb[r, j % 2]).then_inc(s_hhi, 1)
                if j in X2_LATE:
                    evac_x2(X2_LATE[j], ps_o)
                if j == 8:
                    route_copy(1, ps_o)
                if j == 10:
                    route_exp(1)
                if j == 14:
                    route_cT(1, ps_o)

        @block.tensor
        def _(pe):
            mm = nc.tensor.matmul

            def three(dst, w, a, first_, last_):
                (wh, wl), (ah, al) = w, a
                mm(dst, wh, ah, start=first_, stop=False)
                mm(dst, wl, ah, start=False, stop=False)
                return mm(dst, wh, al, start=False, stop=last_)

            pe.wait_ge(s_first, 1)
            for i in range(2):
                mm(ps_o[:], first_sb[:, 0:P], first_sb[:, 0:512], start=True, stop=True)
            pe.wait_ge(ld["wqk"], 16)
            for c in range(2):
                pe.wait_ge(ld_xT[c], 16)
                for k in range(KH):
                    i = mm(ps_q[:, c * 512:(c + 1) * 512], wqc_sb[:, k], xT_sb[:, k, c * 512:(c + 1) * 512],
                           start=k == 0, stop=k == KH - 1)
            i.then_inc(s_qc_mm, 1)
            for t in range(TILES):
                for k in range(KH):
                    i = mm(ps_s[:, tok(t)], xT_sb[:, k, tok(t)], wk_sb[:, k], start=k == 0, stop=k == KH - 1)
            i.then_inc(s_k_mm, 1)

            def values():
                pe.wait_ge(ld["wvc"], 16)
                for c in range(2):
                    for k in range(KH):
                        i = mm(ps_t[:, c * 512:(c + 1) * 512], wv_sb[:, k], xT_sb[:, k, c * 512:(c + 1) * 512],
                               start=k == 0, stop=k == KH - 1)
                i.then_inc(s_v_mm, 1)

            def compress():
                pe.wait_ge(ld["wvc"], 16)
                for w, ps in ((wz_sb, ps_o), (wkv_sb, ps_p)):
                    for k in range(KH):
                        blk = xT_sb[:, k].rearrange("p (b s) -> p b s", s=SEQ)[:, :, 0:BLK]
                        i = mm(ps[:], w[:, k], blk, start=k == 0, stop=k == KH - 1)
                    i.then_inc(s_c_mm, 1)

            def keys_turn(i, ps):
                pe.wait_ge(ld["tab"], 16)
                pe.wait_ge(s_k_dve, 6 * (i + 1))
                for t in range(KT):
                    j = nc.tensor.transpose(ps[:, tok(t)], k_n[i][:, t], id_sb[:])
                j.then_inc(s_k_t, 1)

            def scan_turn(i):
                k, half = i // 2, i % 2
                pe.wait_ge(s_scan, k + 1)
                if i % 2:
                    pe.wait_ge(s_r1, i)
                else:
                    pe.wait_ge(s_z, 5 if k else 1)
                for t in range(4):
                    j = nc.tensor.transpose((ps_o, ps_p)[k][:, tok(t)], rT[:, k, tok(half * 4 + t)], id_sb[:])
                j.then_inc(s_r_t, 1)

            def block_step(i):
                pe.wait_ge(s_skv, i + 1)
                if i == 0:
                    pe.wait_ge(s_r1, 2)
                    j = nc.tensor.transpose(ps_o[0:BATCH, 0:P], c_sb[:], id_sb[:])
                if i == 1:
                    j = nc.tensor.transpose(ps_o[:, 0:BATCH], skv_t[:], id_sb[0:BATCH, 0:BATCH])
                if i == 2:
                    pe.wait_ge(ld["gw"], 16)
                    for h in range(4):
                        gwh = gw_sb[:, h % 2].rearrange("p (g c) o -> p g c o", c=2)[:, :, h // 2]
                        j = mm(ps_o[0:BATCH, 0:HID], skvT[:], gwh, start=h == 0, stop=h == 3)
                if i == 3:
                    for k in range(KH):
                        j = nc.tensor.transpose(ps_o[:, k * BATCH:(k + 1) * BATCH], sg_sb[:, k * P:(k + 1) * P],
                                                id_sb[0:BATCH, 0:BATCH])
                if i == 4:
                    pe.wait_ge(ld["fw"], 16)
                    for k in range(KH):
                        j = mm(ps_o[0:BATCH, 0:HID], sgT[:, k], fw_sb[:, k], start=k == 0, stop=k == KH - 1)
                j.then_inc(s_skv_mm, 1)

            def q_mm(u):
                t, hf = u // 2, u % 2
                pe.wait_ge(s_wqup_hi, hf + 1)
                pe.wait_ge((s_wqup_lo0, s_wqup_lo1)[hf], 1)
                if u >= 1:
                    pe.wait_ge(s_qs, 2 * u)
                    pe.wait_ge(s_q_ss, HALF * u)
                else:
                    pe.wait_ge(s_qc_hi, 1)
                    pe.wait_ge(s_qc_lo, 1)
                for c in range(2):
                    cols = slice(hf * 1024 + c * 512, hf * 1024 + (c + 1) * 512)
                    three(ps_q[:, c * 512:(c + 1) * 512], (qc_hi[:, tok(t)], qc_lo[:, tok(t)]),
                          (wqup_hi[:, cols], wqup_lo[:, cols]), True, True).then_inc(s_q_mm, 1)

            def q_turn(u):
                pe.wait_ge(s_rot, u + 1)
                if u % 2 == 1:
                    pe.wait_ge(s_vg_tok, u // 2 + 1)
                if u >= 1:
                    pe.wait_ge(s_qT, 2 * u)
                else:
                    pe.wait_ge(s_v_hi, 1)
                    pe.wait_ge(s_v_lo, 1)
                for c in range(2):
                    for h in range(4 * c, 4 * c + 4):
                        i = nc.tensor.transpose(ps_t[:, h * P:(h + 1) * P], qs[:, u % 2, h], id_sb[:])
                    i.then_inc(s_qT_t, 1)

            def scores(u):
                if u >= 1:
                    pe.wait_ge(s_s1, 2 * u)
                else:
                    pe.wait_ge(s_kT, 1)
                    pe.wait_ge(s_k_raw, 1)
                    pe.wait_ge(s_idb, 1)
                    pe.wait_ge(ld["mask"], 16)
                for b in range(2):
                    mm(ps_s[:, b * 512:(b + 1) * 512], idb_sb[:], mask_sb[:], start=True, stop=False,
                       skip_group_check=True)
                    pe.wait_ge(s_qT, 2 * u + b + 1)
                    for h in range(4 * b, 4 * b + 4):
                        i = mm(ps_s[:, h * P:(h + 1) * P], qT[:, u % 2, h * P:(h + 1) * P], kT[:, tok(u // 2)],
                               start=False, stop=h == 4 * b + 3, skip_group_check=True)
                i.then_inc(s_s_mm, 1)

            def p_turn(u):
                if u == 0:
                    pe.wait_ge(s_z, 5)
                if u == 2:
                    pe.wait_ge(s_r1, 4)
                pe.wait_ge(s_norm, u + 1)
                for p in range(4):
                    i = nc.tensor.transpose(ps_p[:, p * P:(p + 1) * P],
                                            s_sb[:, u % 2, 2 * p:2 * p + 2].rearrange("p a j -> p (a j)"), id_sb[:])
                i.then_inc(s_pT_t, 1)

            def pv(u):
                t, hf = u // 2, u % 2
                pe.wait_ge(s_pT, u + 1)
                if u == 0:
                    pe.wait_ge(s_sgf, 1)
                if hf == 0:
                    pe.wait_ge(s_vg[t % 2], 64 * (t // 2 + 1))
                    if t:
                        pe.wait_ge(s_x1p, t)
                for g in range(2):
                    for p in range(2):
                        i = mm(ps_o[:, (2 * hf + g) * P:(2 * hf + g + 1) * P],
                               vg[:, t % 2, 4 * hf + 2 * g + p].rearrange("p b o -> p (b o)"),
                               pT[:, u % 2, (2 * g + p) * P:(2 * g + p + 1) * P], start=p == 0, stop=p == 1)
                i.then_inc(s_pv, 1)

            def vg_mm(t):
                pe.wait_ge(s_qT, 2 * (2 * t + 1))
                if t == 0:
                    pe.wait_ge(s_gw_hi, 1)
                    pe.wait_ge(s_gw_lo, 1)
                for a in range(2):
                    cols = (gw_hi[:, a], gw_lo[:, a])
                    i = three(ps_t[:, a * 512:(a + 1) * 512], (v_hi[:, tok(t)], v_lo[:, tok(t)]), cols, True, True)
                i.then_inc(s_vg_mm, 1)

            def final(t):
                pe.wait_ge(s_oT, 4 * (t + 1))
                for k in range(KH):
                    mm(ps_o[:, 0:HID], oT[:, t % 2, k], fw_sb[:, k], start=k == 0, stop=False)
                if t == 0:
                    pe.wait_ge(ld["late"], 16)
                mm(ps_o[:, 0:HID], late_sb[:, tok(t)], sgf[:], start=False, stop=True).then_inc(s_fin, 1)

            def x2_turn(t, ps):
                pe.wait_ge(s_x2, t + 1)
                for k in range(KH):
                    i = nc.tensor.transpose(ps[:, k * P:(k + 1) * P], x2[:, t % 2, k * P:(k + 1) * P], id_sb[:])
                i.then_inc(s_x2_t, 1)

            def logits(c, ps):
                pe.wait_ge(s_x2T, TPC * (c + 1))
                for k in range(KH):
                    i = mm(ps[0:GATES, :], gates_sb[:, k], x2T[:, k, c * CHUNK:(c + 1) * CHUNK],
                           start=k == 0, stop=k == KH - 1)
                i.then_inc(s_lg_mm, 1)

            def logits_turn(c, ps):
                pe.wait_ge(s_lgT, c + 1)
                for t in range(TPC):
                    i = nc.tensor.transpose(ps[:, t * GATES:(t + 1) * GATES], lgT[:, tok(t)],
                                            id_sb[0:GATES, 0:GATES])
                i.then_inc(s_lg_t, 1)

            def weights_turn(c, ps):
                pe.wait_ge(s_cw, c + 1)
                for t in range(TPC):
                    i = nc.tensor.transpose(ps[:].bitcast(BF16)[0:3 * GATES, tok(t)],
                                            cparts[:, t].rearrange("p a g -> p (a g)"), idb_sb[:])
                i.then_inc(s_c_t, 1)

            q_mm(0)
            values()
            compress()
            keys_turn(0, ps_s)
            q_turn(0)
            q_mm(1)
            for n in range(UNITS):
                if n >= 4 and n % 2 == 0:
                    final((n - 4) // 2)
                if n == 4:
                    scan_turn(3)
                if 0 < n < UNITS - 1:
                    q_mm(n + 1)
                if n == 1:
                    scan_turn(1)
                if n >= LAG:
                    if n >= 7 and n % 2 == 1:
                        pe.wait_ge(s_x2hi, (n - 7) // 2 + 1)
                    if n == 14:
                        pe.wait_ge(s_lg, 1)
                    if n == 8:
                        pe.wait_ge(s_kT, 2)
                    p_turn(n - LAG)
                if n:
                    q_turn(n)
                if n == 1:
                    block_step(0)
                if n == 2:
                    block_step(1)
                if n == 13:
                    pe.wait_ge(s_pT, n - 1)
                    pe.wait_ge(ld["gates"], 16)
                    logits(0, ps_p)
                if n >= 3:
                    pv(n - LAG)
                if n == 3:
                    scan_turn(2)
                if n == 7:
                    keys_turn(1, ps_p)
                if n >= 6 and n % 2 == 0:
                    x2_turn((n - 6) // 2, ps_p)
                if n == 2:
                    block_step(2)
                if n and n % 2 == 0:
                    vg_mm(n // 2)
                if n == 2:
                    block_step(3)
                    block_step(4)
                scores(n)
                if n == 2:
                    pv(0)
                if n == 0:
                    vg_mm(0)
                    scan_turn(0)
                if n == 13:
                    logits_turn(0, ps_p)
            weights_turn(0, ps_p)
            pe.wait_ge(s_qs, 2 * UNITS)
            pe.wait_ge(s_q_ss, UNITS * HALF)

            def spread(j):
                c, f = j // FT, j % FT
                if f > SHARED_FT:
                    return
                pe.wait_ge(s_cT, c + 1)
                if j >= 1:
                    pe.wait_ge(s_gc, j)
                if j < LAG:
                    pe.wait_ge(s_pT, UNITS - LAG + j + 1)
                mm(ps_p[:], sel_sb[:, tok(f)], cT[:, c], start=True, stop=True).then_inc(s_cb, 1)

            def up(j):
                c, f = j // FT, j % FT
                toks = slice(c * CHUNK, (c + 1) * CHUNK)
                if j == 0:
                    pe.wait_ge(s_qT, 2 * UNITS)
                pe.wait_ge(s_whi, j + 1)
                pe.wait_ge(s_wlo, j + 1)
                if j == 0:
                    pe.wait_ge(s_x2lo, TPC)
                if j == FT:
                    pe.wait_ge(s_x2lo, TILES)
                if j >= 2:
                    pe.wait_ge(s_silu, j - 1)
                if j == FT + 1:
                    pe.wait_ge(s_h, j - 1)
                for s, ps, done in ((0, ps_q, s_g_mm), (1, ps_t, s_u_mm))[:1 if f == FT - 1 else 2]:
                    if s and j >= 3:
                        spread(j)
                    dst = ps[:, (j % 2) * CHUNK:(j % 2 + 1) * CHUNK]
                    if s and j >= 2:
                        pe.wait_ge(s_h, j - 1)
                    for k in range(KH):
                        cols = slice(k * HID + s * P, k * HID + (s + 1) * P)
                        i = three(dst, (w_hi[:, (j - 1) % WB, cols], w_lo[:, (j - 1) % WB, cols]),
                                  (x2T_hi[:, k, toks], x2T_lo[:, k, toks]), k == 0, k == KH - 1)
                    i.then_inc(done, 1)

            def down(j, ks=range(KH)):
                c, f = j // FT, j % FT
                pe.wait_ge(s_hhi, j + 1)
                pe.wait_ge(s_hlo, j + 1)
                if j == 0:
                    pe.wait_ge(s_s1, 2 * UNITS)
                if j == FT:
                    pe.wait_ge(s_yT, 2)
                rows = slice(0, rows_of(j))
                for k in ks:
                    cols = slice(2 * HID + k * P, 2 * HID + (k + 1) * P)
                    i = three(ps_s[:, k * CHUNK:(k + 1) * CHUNK],
                              (w_hi[rows, (j - 1) % WB, cols], w_lo[rows, (j - 1) % WB, cols]),
                              (h_hi[j % HB][rows], h_lo[j % HB][rows]), f == 0, f == FT - 1)
                if j < NIT - LAST_DOWN:
                    i.then_inc(s_dn, 1)
                elif j == NIT - 1:
                    i.then_inc(s_dn_end, 1)

            def y_turn(t):
                pe.wait_ge(s_yT, t // 2 + 1)
                if t >= 1:
                    pe.wait_ge(s_yo, t)
                for k in range(KH):
                    i = nc.tensor.transpose(y_ps(t)[:, k * P:(k + 1) * P], yT[:, k, tok(t)], id_sb[:])
                i.then_inc(s_y_t, 1)

            pe.wait_ge(ld["sel"], 16)
            for j in range(NIT):
                up(j)
                if j == 0:
                    pe.wait_ge(s_cT, 1)
                    p_turn(UNITS - 2)
                    final(TILES - 2)
                    spread(0)
                    pv(UNITS - 2)
                if j == 1:
                    pe.wait_ge(s_gc, 1)
                    p_turn(UNITS - 1)
                if j == 2:
                    spread(1)
                    down(0)
                    pv(UNITS - 1)
                    spread(2)
                    down(1)
                    final(TILES - 1)
                if j == FT:
                    down(j - 2)
                if 2 < j <= NIT - LAST_DOWN and j != FT - 1:
                    down(j - 1)
                if j in X2_LATE:
                    pe.wait_ge(s_x1p, TILES)
                    pe.wait_ge(s_x2hi, X2_LATE[j])
                    x2_turn(X2_LATE[j], ps_o)
                if j == 8:
                    pe.wait_ge(s_x2hi, 8)
                    logits(1, ps_o)
                if j == 9:
                    logits_turn(1, ps_o)
                if j == 14:
                    weights_turn(1, ps_o)
                if j in Y_EARLY:
                    y_turn(Y_EARLY[j])
            for j in range(NIT - LAST_DOWN, NIT - 1):
                down(j, [0])
            for j in range(NIT - LAST_DOWN, NIT - 2):
                down(j, [1])
            down(NIT - 1, [0])
            down(NIT - 2, [1])
            down(NIT - 1, [1])
            pe.wait_ge(s_yT, 3)
            for n in range(TPC, TILES):
                nc.tensor.transpose(y_ps(n)[:, 0:P], yT[:, 0, tok(n - TPC)], id_sb[:])
            for n in range(TPC, TILES):
                if n % 2 == 0:
                    pe.wait_ge(s_yT, 4 + (n - TPC) // 2)
                nc.tensor.transpose(y_ps(n)[:, P:2 * P], yT[:, 1, tok(n - TPC)], id_sb[:]).then_inc(s_y_t, 1)

        @block.gpsimd
        def _(pool):
            cnt = [0]

            def link(i):
                cnt[0] += 1
                i.then_inc(s_pool, 1)
                pool.wait_ge(s_pool, cnt[0])

            def power(dst, src, scale, eps, rows=P):
                link(nc.gpsimd.tensor_scalar(dst, src, scale, eps, ALU.mult, ALU.add))
                return nc.gpsimd.tensor_tensor(dst, dst, nhalf[0:rows, 0:dst.shape[-1]], ALU.pow)

            link(nc.gpsimd.memset(nhalf[:], -0.5))
            link(nc.gpsimd.memset(first_sb[:], 1.0))
            nc.gpsimd.memset(first_sb[:].rearrange("p (b s) -> p b s", s=SEQ)[:, :, 0:1], 0.0).then_inc(s_first, 1)
            pool.wait_ge(ld["decay"], 16)
            pool.wait_ge(s_first, 1)
            for i in range(KH):
                nc.gpsimd.tensor_scalar(dk[:, i], first_sb[:], decay_sb[:, i:i + 1], None, ALU.mult) \
                    .then_inc(s_scan_in, 1)
            pool.wait_ge(s_wqup_hi, 2)
            nc.gpsimd.tensor_tensor(wqup_lo[:, 1024:2048], wqup_sb[:, 1024:2048],
                                    wqup_hi[:, 1024:2048].bitcast(F32), ALU.subtract).then_inc(s_wqup_lo1, 1)

            def r_k(i):
                pool.wait_ge(s_k_ss, KT * (i + 1))
                tiles = slice(i * KT, (i + 1) * KT)
                power(k_r[:, tiles], k_ss[:, tiles], 1.0 / D, RMS_EPS).then_inc(s_k_r, 1)

            r_k(0)

            def r_q(u):
                pool.wait_ge(s_q_ss, HALF * (u + 1))
                if u >= 2:
                    pool.wait_ge(s_s1, 2 * (u - 1))
                power(q_r[:, u % 2], q_ss[:, u % 2], 1.0, D * RMS_EPS).then_inc(s_q_r, 1)

            def rot(u):
                pool.wait_ge(s_rope, u + 1)
                nc.gpsimd.tensor_tensor(qs[:, u % 2, :, 0:ROT], q_a[:, u % 2], q_b[:, u % 2], ALU.add) \
                    .then_inc(s_rot, 1)

            def sub_max(u):
                hs = slice((u % 2) * HALF, (u % 2 + 1) * HALF)
                pool.wait_ge(s_max, u + 1)
                nc.gpsimd.tensor_tensor(sk_sb[:, u % 2], sink_sb[:, hs], m_sb[:, u % 2], ALU.subtract) \
                    .then_inc(s_sub, 1)
                nc.gpsimd.tensor_tensor(s_sb[:, u % 2], s_sb[:, u % 2],
                                        bc(m_sb[:, u % 2].unsqueeze(2), [P, HALF, SEQ]), ALU.subtract) \
                    .then_inc(s_sub, 1)

            def norm(u):
                pool.wait_ge(s_l, u + 1)
                nc.gpsimd.tensor_tensor(s_sb[:, u % 2], s_sb[:, u % 2],
                                        bc(l_sb[:, u % 2].unsqueeze(2), [P, HALF, SEQ]), ALU.mult) \
                    .then_inc(s_norm, 1)

            def ln_power(rs, mv, t, wait, done):
                p = t % rs.shape[-1]
                pool.wait_ge(wait, t + 1)
                link(nc.gpsimd.tensor_scalar(rs[:, p:p + 1], mv[:, p, 1:2], 1.0, LN_EPS,
                                             ALU.mult, ALU.add))
                nc.gpsimd.tensor_tensor(rs[:, p:p + 1], rs[:, p:p + 1], nhalf[:, 0:1], ALU.pow) \
                    .then_inc(done, 1)

            def low_w(j):
                b = (j - 1) % WB
                pool.wait_ge(s_whi, j + 1)
                nc.gpsimd.tensor_tensor(w_lo[:, b], w_raw[:, b], w_hi[:, b].bitcast(F32), ALU.subtract) \
                    .then_inc(s_wlo, 1)

            rot(0)
            r_q(0)
            pool.wait_ge(s_gw_hi, 1)
            nc.gpsimd.tensor_tensor(gw_lo[:], gw_sb[:], gw_hi[:].bitcast(F32), ALU.subtract).then_inc(s_gw_lo, 1)
            for n in range(UNITS):
                if n >= 1:
                    r_q(n)
                    sub_max(n - 1)
                if n >= 5 and n % 2 == 1:
                    ln_power(rs2, mv2, (n - 5) // 2, s_ln2, s_rs2)
                if n >= 4 and n % 2 == 0:
                    ln_power(rs1, mv1, (n - 4) // 2, s_ln1, s_rs1)
                if n + 1 < UNITS:
                    rot(n + 1)
                if n >= 1:
                    norm(n - 1)
                if n == 3:
                    r_k(1)
                if n == 13:
                    low_w(0)
                if n == 15:
                    low_w(1)
                if n == 1:
                    pool.wait_ge(s_skv_ss, 1)
                    power(skv_r[:], skv_ss[:], 1.0 / D, RMS_EPS, BATCH).then_inc(s_skv_r, 1)
            sub_max(UNITS - 1)
            low_w(2)
            norm(UNITS - 1)
            for j in range(NIT):
                if j >= 1 and j + WB - 2 < NIT:
                    low_w(j + WB - 2)
                if j in (0, 3):
                    ln_power(rs1, mv1, 6 + j // 3, s_ln1, s_rs1)
                if j in (1, 4):
                    ln_power(rs2, mv2, 6 + j // 3, s_ln2, s_rs2)
                if j in Y_EARLY:
                    ln_power(rs3, mv3, Y_EARLY[j], s_ln3, s_rs3)
            for t in range(TPC):
                ln_power(rs3, mv3, TPC + t, s_ln3, s_rs3)

        @block.vector
        def _(dve):
            tt = nc.vector.tensor_tensor

            dve.wait_ge(s_wqup_hi, 1)
            tt(wqup_lo[:, 0:1024], wqup_sb[:, 0:1024], wqup_hi[:, 0:1024].bitcast(F32), ALU.subtract) \
                .then_inc(s_wqup_lo0, 1)
            dve.wait_ge(s_qc_hi, 1)
            tt(qc_lo[:], ps_q[:], qc_hi[:].bitcast(F32), ALU.subtract).then_inc(s_qc_lo, 1)

            def scan(k):
                if k == 0:
                    dve.wait_ge(s_kvx, 1)
                dve.wait_ge(s_scan_in, KH)
                nc.vector.tensor_tensor_scan(rT[:, k], dk[:, k], kvx[:, k], 0.0, ALU.mult, ALU.add) \
                    .then_inc(s_scan, 1)

            def block_sum():
                dve.wait_ge(s_z_exp, 1)
                nc.vector.tensor_reduce(z_sum[:], z_sb[:], AX_X, ALU.add).then_inc(s_z, 1)
                dve.wait_ge(s_z, 4)
                tt(z_sb[:], z_sb[:], cp, ALU.mult).then_inc(s_z, 1)
                nc.vector.reciprocal(z_sum[:], z_sum[:]).then_inc(s_z, 1)
                dve.wait_ge(s_z, 6)
                nc.vector.tensor_reduce(c_num[:], z_sb[:], AX_X, ALU.add).then_inc(s_z, 1)
                dve.wait_ge(s_z, 7)
                tt(c_sb[:], c_num[:], z_sum[:], ALU.mult).then_inc(s_skv, 1)

            def block_norm():
                dve.wait_ge(s_skv_mm, 1)
                nc.vector.tensor_copy(skv_t[:], ps_o[0:BATCH, 0:P]).then_inc(s_z, 1)
                dve.wait_ge(s_z, 8)
                tt(skv_sq[:], skv_t[:], skv_t[:], ALU.mult).then_inc(s_z, 1)
                dve.wait_ge(s_z, 9)
                nc.vector.tensor_reduce(skv_ss[:], skv_sq[:], AX_X, ALU.add).then_inc(s_skv_ss, 1)

            def block_scale():
                dve.wait_ge(s_skv_r, 1)
                nc.vector.scalar_tensor_tensor(skv_t[:], skv_t[:], skv_r[:, 0:1], knw_sb[0:BATCH, :],
                                               ALU.mult, ALU.mult).then_inc(s_skv, 1)

            def block_copy(i, dst, src, done):
                dve.wait_ge(s_skv_mm, i)
                nc.vector.tensor_copy(dst, src).then_inc(done, 1)

            h = ROT // 2

            def rope(u):
                dve.wait_ge(s_qs, 2 * (u + 1))
                if u >= 2:
                    dve.wait_ge(s_rot, u - 1)
                q = qs[:, u % 2]
                tt(q_a[:, u % 2], q[:, :, 0:ROT], bc(cos_sb[:].unsqueeze(1), [P, HALF, ROT]), ALU.mult)
                tt(q_b[:, u % 2, :, 0:h], q[:, :, h:ROT], bc(sin_sb[:, 0:h].unsqueeze(1), [P, HALF, h]), ALU.mult)
                tt(q_b[:, u % 2, :, h:ROT], q[:, :, 0:h], bc(sin_sb[:, h:ROT].unsqueeze(1), [P, HALF, h]),
                   ALU.mult).then_inc(s_rope, 1)

            def k_norm(i):
                dve.wait_ge(s_k_r, i + 1)
                for t in range(KT):
                    src = k_raw[:, t] if i else ps_s[:, tok(t)]
                    j = nc.vector.scalar_tensor_tensor(k_n[i][:, t], src, k_r[:, i * KT + t:i * KT + t + 1], knw_sb[:],
                                                       ALU.mult, ALU.mult)
                j.then_inc(s_k_dve, 1)

            def k_rope(i):
                dve.wait_ge(s_k_dve, 6 * i + 1)
                tt(k_a[i], k_n[i][:, :, 0:ROT], bc(cos_sb[:].unsqueeze(1), [P, KT, ROT]), ALU.mult).then_inc(s_k_dve, 1)
                tt(k_b[i][:, :, 0:h], k_n[i][:, :, h:ROT], bc(sin_sb[:, 0:h].unsqueeze(1), [P, KT, h]), ALU.mult) \
                    .then_inc(s_k_dve, 1)
                tt(k_b[i][:, :, h:ROT], k_n[i][:, :, 0:h], bc(sin_sb[:, h:ROT].unsqueeze(1), [P, KT, h]), ALU.mult) \
                    .then_inc(s_k_dve, 1)

            def k_weight(i):
                dve.wait_ge(s_k_dve, 6 * i + 4)
                tt(k_n[i][:, :, 0:ROT], k_a[i], k_b[i], ALU.add).then_inc(s_k_dve, 1)
                dve.wait_ge(s_k_dve, 6 * i + 5)
                tt(k_n[i][:], k_n[i][:], bc(qnw_sb[:].unsqueeze(1), [P, KT, D]), ALU.mult).then_inc(s_k_dve, 1)

            def scale(u):
                dve.wait_ge(s_s_mm, u + 1)
                dve.wait_ge(s_q_r, u + 1)
                if u >= 2:
                    dve.wait_ge(s_pT_t, u - 1)
                pairs = ps_s[:].rearrange("p (h b j) -> p h b j", b=2, j=SEQ)
                for b in range(2):
                    rows = slice(b * 64, b * 64 + 64)
                    tt(s_sb[rows, u % 2], pairs[rows, :, b], bc(q_r[rows, u % 2].unsqueeze(2), [64, HALF, SEQ]),
                       ALU.mult).then_inc(s_s1, 1)
                dve.wait_ge(s_s1, 2 * (u + 1))
                if u >= 2:
                    dve.wait_ge(s_sub, 2 * (u - 1))
                nc.vector.tensor_reduce(m_sb[:, u % 2], s_sb[:, u % 2], AX_X, ALU.max).then_inc(s_mx, 1)
                dve.wait_ge(s_mx, u + 1)
                tt(m_sb[:, u % 2], m_sb[:, u % 2], sink_sb[:, (u % 2) * HALF:(u % 2 + 1) * HALF], ALU.max) \
                    .then_inc(s_max, 1)

            def sums(u):
                dve.wait_ge(s_exp, 2 * (u + 1))
                if u >= 2:
                    dve.wait_ge(s_norm, u - 1)
                nc.vector.tensor_reduce(l_sb[:, u % 2], s_sb[:, u % 2], AX_X, ALU.add).then_inc(s_l0, 1)
                dve.wait_ge(s_l0, 2 * u + 1)
                tt(l_sb[:, u % 2], l_sb[:, u % 2], sk_sb[:, u % 2], ALU.add).then_inc(s_l0, 1)
                dve.wait_ge(s_l0, 2 * u + 2)
                nc.vector.reciprocal(l_sb[:, u % 2], l_sb[:, u % 2]).then_inc(s_l, 1)

            def turn_o(t):
                dve.wait_ge(s_pv, 2 * (t + 1))
                if t >= 2:
                    dve.wait_ge(s_fin, t - 1)
                src = ps_o[:].rearrange("p (k a n) -> p k a n", k=KH, a=2)
                for b in range(2):
                    for a in range(2):
                        nc.vector.tensor_copy(oT[a * 64:a * 64 + 64, t % 2, :, b * 64:b * 64 + 64],
                                              src[b * 64:b * 64 + 64, :, a, b * 64:b * 64 + 64]).then_inc(s_oT, 1)

            def ln_a(t):
                p = t % 2
                dve.wait_ge(s_fin, t + 1)
                tt(x1p[:, p], ps_o[:, 0:HID], x_sb[:, t], ALU.add).then_inc(s_x1p, 1)
                dve.wait_ge(s_x1p, t + 1)
                nc.vector.bn_stats(st1[:, p], x1p[:, p]).then_inc(s_lnc, 1)
                dve.wait_ge(s_lnc, 4 * t + 1)
                nc.vector.bn_aggr(mv1[:, p], st1[:, p]).then_inc(s_ln1, 1)

            def ln_b(t):
                p = t % 2
                dve.wait_ge(s_rs1, t + 1)
                dve.wait_ge(s_ln1, t + 1)
                nc.vector.tensor_scalar(x1[:, p], x1p[:, p], mv1[:, p, 0:1], rs1[:, p:p + 1],
                                        ALU.subtract, ALU.mult).then_inc(s_lnc, 1)
                dve.wait_ge(s_lnc, 4 * t + 2)
                tt(x2p[:, p], x1[:, p], r1[:, t], ALU.mult).then_inc(s_lnc, 1)
                dve.wait_ge(s_lnc, 4 * t + 3)
                nc.vector.bn_stats(st2[:, p], x2p[:, p]).then_inc(s_lnc, 1)
                dve.wait_ge(s_lnc, 4 * t + 4)
                nc.vector.bn_aggr(mv2[:, p], st2[:, p]).then_inc(s_ln2, 1)

            def ln_c(t):
                p = t % 2
                dve.wait_ge(s_rs2, t + 1)
                dve.wait_ge(s_ln2, t + 1)
                if t >= 2:
                    dve.wait_ge(s_x2_t, t - 1)
                nc.vector.tensor_scalar(x2[:, p], x2p[:, p], mv2[:, p, 0:1], rs2[:, p:p + 1],
                                        ALU.subtract, ALU.mult).then_inc(s_x2, 1)

            def x2_lo(t):
                dve.wait_ge(s_x2hi, t + 1)
                dve.wait_ge(s_x2T, t + 1)
                tt(x2T_lo[:, :, tok(t)], x2T[:, :, tok(t)], x2T_hi[:, :, tok(t)].bitcast(F32), ALU.subtract) \
                    .then_inc(s_x2lo, 1)

            chain = [0]

            def link(i):
                chain[0] += 1
                i.then_inc(s_rt, 1)
                dve.wait_ge(s_rt, chain[0])

            def route_a(c, ps):
                dve.wait_ge(s_lg_t, c + 1)
                nc.vector.tensor_copy(lg[:], ps[:, 0:TPC * GATES].rearrange("p (t g) -> p t g", g=GATES)) \
                    .then_inc(s_lg, 1)
                dve.wait_ge(s_lg, c + 1)
                link(nc.vector.tensor_reduce(lmax[:], lg[:, :, 0:EXPERTS], AX_X, ALU.max))
                tt(lg[:, :, 0:EXPERTS], lg[:, :, 0:EXPERTS], bc(lmax[:].unsqueeze(2), [P, TPC, EXPERTS]),
                   ALU.subtract)
                nc.vector.tensor_scalar(lg[:, :, EXPERTS:], lg[:, :, EXPERTS:], -1.0, None, ALU.mult) \
                    .then_inc(s_lsub, 1)

            def route_b(c):
                dve.wait_ge(s_lexp, c + 1)
                for t in range(TPC):
                    i = nc.vector.max(top[:, t], ex[:, t, 0:EXPERTS])
                link(i)
                for t in range(TPC):
                    i = nc.vector.max_index(topi[:, t], top[:, t], ex[:, t, 0:EXPERTS])
                link(i)
                link(nc.vector.tensor_copy(topf[:], topi[:, :, 0:2]))
                for r in range(2):
                    i = tt(pick[:, r], bc(iota_sb[:].unsqueeze(1), [P, TPC, EXPERTS]),
                           bc(topf[:, :, r:r + 1], [P, TPC, EXPERTS]), ALU.is_equal)
                link(i)

            def route_weights(c):
                link(tt(pick[:, 0], pick[:, 0], pick[:, 1], ALU.add))
                link(tt(pick[:, 0], pick[:, 0], ex[:, :, 0:EXPERTS], ALU.mult))
                link(nc.vector.tensor_reduce(den[:], pick[:, 0], AX_X, ALU.add))
                link(nc.vector.reciprocal(den[:], den[:]))

            def route_c(c):
                tt(cw[:, :, 0:EXPERTS], pick[:, 0], bc(den[:].unsqueeze(2), [P, TPC, EXPERTS]), ALU.mult)
                link(nc.vector.tensor_scalar(ex[:, :, EXPERTS:], ex[:, :, EXPERTS:], 1.0, None, ALU.add))
                link(nc.vector.reciprocal(cw[:, :, EXPERTS:], ex[:, :, EXPERTS:]))
                if c:
                    dve.wait_ge(s_c_t, c)
                link(nc.vector.tensor_copy(cparts[:, :, 0], cw[:]))
                link(tt(cres[:, 0], cw[:], cparts[:, :, 0], ALU.subtract))
                link(nc.vector.tensor_copy(cparts[:, :, 1], cres[:, 0]))
                link(tt(cres[:, 1], cres[:, 0], cparts[:, :, 1], ALU.subtract))
                nc.vector.tensor_copy(cparts[:, :, 2], cres[:, 1]).then_inc(s_cw, 1)

            dve.wait_ge(ld["tab"], 16)
            rope(0)
            k_norm(0)
            k_rope(0)
            k_weight(0)
            dve.wait_ge(s_v_hi, 1)
            tt(v_lo[:], ps_t[:], v_hi[:].bitcast(F32), ALU.subtract).then_inc(s_v_lo, 1)
            dve.wait_ge(s_c_mm, 2)
            zp = ps_o[:].rearrange("p (b m) -> p b m", m=BLK)
            cp = ps_p[:].rearrange("p (b m) -> p b m", m=BLK)
            tt(z_sb[:], zp, bc(bias_sb[:].unsqueeze(1), [P, BATCH, BLK]), ALU.add).then_inc(s_z, 1)
            dve.wait_ge(s_z, 1)
            nc.vector.tensor_reduce(z_max[:], z_sb[:], AX_X, ALU.max).then_inc(s_z, 1)
            dve.wait_ge(s_z, 2)
            tt(z_sb[:], z_sb[:], bc(z_max[:].unsqueeze(2), [P, BATCH, BLK]), ALU.subtract).then_inc(s_z, 1)
            for n in range(UNITS):
                if n == 2:
                    block_scale()
                    block_copy(2, skvT[:], ps_o[:, 0:BATCH], s_skv)
                if n + 1 < UNITS:
                    rope(n + 1)
                else:
                    route_c(0)
                if n == 0:
                    scan(0)
                if n == 2:
                    block_copy(3, sg_sb[:], ps_o[0:BATCH, 0:HID], s_skv)
                    block_copy(4, sgT[:], ps_o[:, 0:KH * BATCH].rearrange("p (k b) -> p k b", k=KH), s_skv)
                if n >= 3 and n % 2 == 1:
                    turn_o((n - 3) // 2)
                if n >= 1:
                    sums(n - 1)
                if n == 1:
                    block_norm()
                if n == 2:
                    block_copy(5, sgf[:], ps_o[0:BATCH, 0:HID], s_sgf)
                if n >= 5 and n % 2 == 1:
                    ln_c((n - 5) // 2)
                if n >= 7 and n % 2 == 1:
                    x2_lo((n - 7) // 2)
                if n == 14:
                    route_b(0)
                if n >= 4 and n % 2 == 0:
                    if n == 4:
                        dve.wait_ge(s_r1, 4)
                    ln_b((n - 4) // 2)
                if n in (4, 5, 6):
                    (k_norm, k_rope, k_weight)[n - 4](1)
                scale(n)
                if n == 0:
                    block_sum()
                if n == 2:
                    scan(1)
                if n == 13:
                    route_a(0, ps_p)
                if n == 14:
                    route_weights(0)
                if n >= 3 and n % 2 == 1:
                    if n == 3:
                        dve.wait_ge(ld["x"], 16)
                    ln_a((n - 3) // 2)
            sums(UNITS - 1)

            def y_sum(c, ks, toks):
                of_all = slice(c * CHUNK + toks.start, c * CHUNK + toks.stop)
                tt(yT[:, ks, toks], ps_s[:].rearrange("p (k n) -> p k n", k=KH)[:, ks, toks],
                   x2T[:, ks, of_all], ALU.add).then_inc(s_yT, 1)

            def ln_y_a(n):
                p = n % TPC
                dve.wait_ge(s_y_t, n + 1)
                if n >= TPC:
                    dve.wait_ge(s_yo, n - TPC + 1)
                nc.vector.bn_stats(st3[:, p], y_ps(n)).then_inc(s_y3, 1)
                dve.wait_ge(s_y3, n + 1)
                nc.vector.bn_aggr(mv3[:, p], st3[:, p]).then_inc(s_ln3, 1)

            def ln_y_b(n):
                p = n % TPC
                dve.wait_ge(s_rs3, n + 1)
                dve.wait_ge(s_ln3, n + 1)
                nc.vector.tensor_scalar(y_out[:, n], y_ps(n), mv3[:, p, 0:1], rs3[:, p:p + 1],
                                        ALU.subtract, ALU.mult).then_inc(s_yo, 1)

            for j in range(NIT):
                dve.wait_ge(s_silu, j + 1)
                dve.wait_ge(s_cb, spreads(j))
                r = slice(0, rows_of(j))
                tt(act_c[r, j % 2], act_g[r, j % 2], ps_p[r], ALU.mult).then_inc(s_gc, 1)
                dve.wait_ge(s_gc, j + 1)
                bank = slice((j % 2) * CHUNK, (j % 2 + 1) * CHUNK)
                up_rows = ps_t[:, bank]
                if (j + 1) % FT == 0:
                    up_rows = ps_q[LAST_ROWS:2 * LAST_ROWS, bank]
                else:
                    dve.wait_ge(s_u_mm, j + 1 - j // FT)
                if j >= 2:
                    dve.wait_ge(s_hhi, j - 1)
                else:
                    dve.wait_ge(s_pT_t, UNITS - LAG + j + 1)
                tt(h_sb[r, j % 2], act_c[r, j % 2], up_rows, ALU.mult).then_inc(s_h, 1)
                dve.wait_ge(s_hhi, j + 1)
                if j >= HB:
                    dve.wait_ge(s_dn, j - HB + 1)
                tt(h_lo[j % HB][r], h_sb[r, j % 2], h_hi[j % HB][r].bitcast(F32), ALU.subtract).then_inc(s_hlo, 1)
                if j in (0, 3):
                    ln_b(6 + j // 3)
                if j in (1, 4):
                    ln_c(6 + j // 3)
                if j == 1:
                    turn_o(7)
                if j == 2:
                    ln_a(7)
                if j - 1 in X2_LATE:
                    x2_lo(X2_LATE[j - 1])
                if j == 9:
                    route_a(1, ps_o)
                if j == 11:
                    route_b(1)
                if j == 12:
                    route_weights(1)
                if j == 13:
                    route_c(1)
                if j == FT:
                    dve.wait_ge(s_dn, FT)
                    for i in range(2):
                        y_sum(0, slice(0, KH), slice(i * 2 * P, (i + 1) * 2 * P))
                if j in Y_EARLY:
                    ln_y_a(Y_EARLY[j])
                if j - 1 in Y_EARLY:
                    ln_y_b(Y_EARLY[j - 1])
            dve.wait_ge(s_y_t, TPC)
            dve.wait_ge(s_dn_end, 1)
            y_sum(1, slice(0, 1), slice(0, CHUNK))
            dve.wait_ge(s_dn_end, 2)
            for i in range(2):
                y_sum(1, slice(1, 2), slice(i * 2 * P, (i + 1) * 2 * P))
            for t in range(TPC, TILES):
                ln_y_a(t)
            for t in range(TPC, TILES):
                ln_y_b(t)


def _constants(np):
    f = np.float32
    inv = (f(1.0) / f(10000.0) ** (np.arange(0, ROT, 2, dtype=f) / f(ROT))).astype(f)
    ang = (np.arange(SEQ, dtype=f)[:, None] * inv).astype(f)
    cos, sin = np.cos(ang).astype(f), np.sin(ang).astype(f)
    t = np.arange(TOK)
    rows = np.arange(FT * P)
    gate = np.where(rows < MOE_ROWS, rows // I_MOE, EXPERTS)
    key, query = np.arange(SEQ)[None, :], (np.arange(P) % SEQ)[:, None]
    return {
        "cos": np.tile(np.concatenate([cos, cos], 1), (2, 1)),
        "sin": np.tile(np.concatenate([-sin, sin], 1), (2, 1)),
        "ident": np.eye(P, dtype=f),
        "iota": np.tile(np.arange(EXPERTS, dtype=f), (P, 1)),
    }, {
        "mask": np.tile(np.where(key <= query, 0.0, -1e30), (1, 8)).astype(mybir.dt.np(BF16)),
        "late": ((t[None, :] // SEQ == np.arange(BATCH)[:, None]) & (t[None, :] % SEQ >= BLK)).astype(f),
        "sel": np.tile(gate[None, :] == np.arange(GATES)[:, None], (3, 1)).astype(mybir.dt.np(BF16)),
    }


def kernel(**inputs):
    import numpy as np
    import concourse.bacc as _bacc
    from concourse.bass_utils import run_bass_kernel_spmd as _run

    a = {k.replace("L0_", ""): np.asarray(v) for k, v in inputs.items()}
    x = a["x"].reshape(TOK, HID)

    def rep(v):
        return np.tile(v.reshape(1, -1), (P, 1))

    gw = a["attn_group_w"].reshape(GROUPS * 4, D, GDIM).transpose(1, 0, 2).reshape(D, HALF, 2, GDIM)
    gw = gw.transpose(0, 2, 1, 3).reshape(D, 2 * HALF * GDIM)
    fill = np.zeros((FT * P - MOE_ROWS - I_SH, HID), np.float32)
    w1, gu = a["ffn_w1"], a["ffn_shared_gate_up_w"]
    wg = np.concatenate([w1[:, :I_MOE].reshape(MOE_ROWS, HID), gu[:I_SH], fill])
    wu = np.concatenate([w1[:, I_MOE:].reshape(MOE_ROWS, HID), gu[I_SH:], fill])
    wd = np.concatenate([a["ffn_w2"].transpose(0, 2, 1).reshape(MOE_ROWS, HID), a["ffn_shared_down_w"].T, fill])
    up = np.stack([w.reshape(FT, P, KH, P).transpose(0, 3, 2, 1) for w in (wg, wu)], 3)
    up[-1, :, :, 0, LAST_ROWS:2 * LAST_ROWS] = up[-1, :, :, 1, :LAST_ROWS]
    wffn = np.concatenate([up.reshape(FT, P, KH * 2 * P), wd.reshape(FT, P, HID)], 2)
    tables, masks = _constants(np)
    tables.update(knw=rep(a["attn_k_norm_w"]), qnw=rep(a["attn_q_norm_w"]), sink=rep(a["attn_sink_logit"]),
                  bias=a["attn_bias_b"].T)
    data = {
        "x": x, "xT": x.T, "ctxT": a["ctx_2048"].reshape(TOK, HID).T,
        "w_x": np.concatenate([a["attn_" + w] for w in ("w_qc", "w_k", "w_v", "w_kv_b", "w_z_b")], 1),
        "w_qup": a["attn_w_qup"], "gw": gw, "fw": a["attn_final_w"],
        "gates": np.concatenate([a["ffn_gate_w"], a["ffn_shared_gate_w"]]).T, "wffn": wffn,
        "decay": np.repeat(a["xattn_decay"].reshape(-1), HID // HEADS).reshape(KH, P).T,
        "tables": np.concatenate([tables[n] for n, _ in TABLES], 1), **masks,
    }
    nc = _bacc.Bacc("TRN2", target_bir_lowering=False, num_devices=1)
    arrays, args = {}, {}
    for name, v in data.items():
        v = np.ascontiguousarray(v)
        arrays[name + "_in"] = v
        args[name] = nc.dram_tensor(name + "_in", v.shape, mybir.dt.from_np(v.dtype), kind="ExternalInput").ap()
    out = nc.dram_tensor("out_dram", (TOK, HID), F32, kind="ExternalOutput").ap()
    build(nc, out=out, **args)
    r = _run(nc, [arrays], core_ids=[0])
    return r.results[0]["out_dram"].reshape(BATCH, SEQ, HID)
```
